# Optimizing a Trainium2 kernel written in Bass

```python
import numpy as np
import jax
import jax.numpy as jnp

def _softmax(x, axis=-1):
    return jax.nn.softmax(x, axis=axis)

def _gelu(x):
    return jax.nn.gelu(x, approximate=True)

def _silu(x):
    return jax.nn.silu(x)

def _sigmoid(x):
    return jax.nn.sigmoid(x)

def _layernorm(x, axis=-1, eps=1e-05):
    m = jnp.mean(x, axis=axis, keepdims=True)
    v = jnp.var(x, axis=axis, keepdims=True)
    return (x - m) / jnp.sqrt(v + eps)

def _scatter_add(tgt, idx, src, axis=0):
    return tgt.at[idx].add(src)

def _segment_sum(src, seg, n):
    return jax.ops.segment_sum(src, seg, n)
kernel_name = 'mk_perceiver_d1_seqx_r8_58e566'

def setup_inputs(seed: int=0):
    np.random.seed(seed)
    _w = jnp.asarray

    def _rec_inputs():
        import jax
        import jax.numpy as jnp
        _rk = jax.random.key(seed)
        x = -0.0003929 + 0.9999 * jax.random.normal(jax.random.fold_in(_rk, 1), (32, 64, 256), jnp.float32)
        _lenS = 64 - jax.random.randint(jax.random.fold_in(_rk, 7), (32,), 0, max(1, 64 // 4) + 1, jnp.int32)
        _lenS2 = 1601 - jax.random.randint(jax.random.fold_in(_rk, 8), (32,), 0, max(1, 1601 // 4) + 1, jnp.int32)
        _ctx_2048P = jax.random.normal(jax.random.fold_in(_rk, 11), (32, 16, 256), jnp.float32)
        _ctx_2048c = jax.random.dirichlet(jax.random.fold_in(_rk, 511), 0.3 * jnp.ones((16,), jnp.float32), (32, 1601))
        _ctx_2048t = jnp.einsum('bsk,bkd->bsd', _ctx_2048c, _ctx_2048P)
        _ctx_2048t = _ctx_2048t * jax.lax.rsqrt(jnp.mean(jnp.square(_ctx_2048t)) + 1e-12) * 0.953939
        ctx_2048 = -0.000514642 + 1.00011 * (_ctx_2048t + 0.3 * jax.random.normal(jax.random.fold_in(_rk, 611), (32, 1601, 256), jnp.float32))
        return (x, ctx_2048)
    x, ctx_2048 = _rec_inputs()

    def _L0_xattn_setup():
        import jax, jax.numpy as jnp
        import numpy as np
        NUM_HEADS = 16

        def _qdq(x):
            s = jnp.maximum(jnp.max(jnp.abs(x), axis=-1, keepdims=True) / 127.0, 1e-08)
            return jnp.clip(jnp.round(x / s), -127.0, 127.0) * s
        key = jax.random.key(seed)
        ks = jax.random.split(key, 8)
        B, N, M, D = (2, 512, 64, 256)
        w_std = 0.02
        return {'x': jax.random.normal(ks[0], (B, N, D), jnp.float32), 'cond': jax.random.normal(ks[1], (B, M, D), jnp.float32), 'wq': jax.random.normal(ks[2], (D, D), jnp.float32) * w_std, 'bq': jax.random.normal(ks[3], (D,), jnp.float32) * w_std, 'wkv': jax.random.normal(ks[4], (2 * D, D), jnp.float32) * w_std, 'bkv': jax.random.normal(ks[5], (2 * D,), jnp.float32) * w_std, 'wp': jax.random.normal(ks[6], (D, D), jnp.float32) * w_std, 'bp': jax.random.normal(ks[7], (D,), jnp.float32) * w_std}
    _L0_xattn_all = _L0_xattn_setup()
    _L0_xattn_in = {k: v for k, v in _L0_xattn_all.items() if k in ('wq', 'bq', 'wkv', 'bkv', 'wp', 'bp')}
    del _L0_xattn_all

    def _L0_attn_setup():
        import jax, jax.numpy as jnp
        import numpy as np

        def _selective_scan(x, dt, a_mat, b_mat, c_mat):
            a_bar = jnp.exp(dt[..., None] * a_mat[None, None])
            b_bar_x = (dt * x)[..., None] * b_mat[:, :, None, :]
            a_t = jnp.moveaxis(a_bar, 1, 0)
            bx_t = jnp.moveaxis(b_bar_x, 1, 0)
            c_t = jnp.moveaxis(c_mat, 1, 0)
            h0 = jnp.zeros(a_t.shape[1:], dtype=x.dtype)

            def step(h, inp):
                a, bx, c = inp
                h = a * h + bx
                y = jnp.einsum('bdn,bn->bd', h, c)
                return (h, y)
            _, ys = jax.lax.scan(step, h0, (a_t, bx_t, c_t))
            return jnp.moveaxis(ys, 0, 1)
        key = jax.random.key(seed)
        ks = jax.random.split(key, 5)
        B, L, D, N, R = (2, 256, 256, 16, 128)
        x = jax.random.normal(ks[0], (B, L, D), dtype=jnp.float32)
        x_proj_w = jax.random.normal(ks[1], (R + 2 * N, D), dtype=jnp.float32) * (1.0 / np.sqrt(D))
        dt_proj_w = jax.random.normal(ks[2], (D, R), dtype=jnp.float32) * (1.0 / np.sqrt(R))
        dt_proj_b = jax.random.normal(ks[3], (D,), dtype=jnp.float32) * 0.1
        A_log = jnp.broadcast_to(jnp.log(jnp.arange(1, N + 1, dtype=jnp.float32)), (D, N))
        D_param = jnp.ones((D,), dtype=jnp.float32)
        return {'x': x, 'x_proj_w': x_proj_w, 'dt_proj_w': dt_proj_w, 'dt_proj_b': dt_proj_b, 'A_log': A_log, 'D_param': D_param}
    _L0_attn_all = _L0_attn_setup()
    _L0_attn_in = {k: v for k, v in _L0_attn_all.items() if k in ('x_proj_w', 'dt_proj_w', 'dt_proj_b', 'A_log', 'D_param')}
    del _L0_attn_all

    def _L0_ffn_setup():
        import jax, jax.numpy as jnp
        import numpy as np
        NUM_EXPERTS = 64
        TOP_K = 8
        HIDDEN = 256
        FFN = 96
        BATCH, SEQ = (1, 256)
        CAP_FACTOR = 2

        def _moe_forward(hidden_states, gate_w, w_gate, w_up, w_down):
            B, S, D = hidden_states.shape
            E = gate_w.shape[0]
            x = hidden_states.reshape(-1, D)
            N = x.shape[0]
            P = N * TOP_K
            C = CAP_FACTOR * P // E
            logits = x @ gate_w.T
            probs = jax.nn.softmax(logits, axis=-1)
            scores, idx = jax.lax.top_k(probs, TOP_K)
            flat_e = idx.reshape(-1)
            order = jnp.argsort(flat_e)
            e_sorted = flat_e[order]
            tok_sorted = order // TOP_K
            s_sorted = scores.reshape(-1)[order]
            counts = jnp.bincount(e_sorted, length=E)
            starts = jnp.cumsum(counts) - counts
            pos = jnp.arange(P) - starts[e_sorted]
            valid = pos < C
            safe_pos = jnp.minimum(pos, C - 1)
            xbuf = jnp.zeros((E, C, D), dtype=x.dtype).at[e_sorted, pos].set(x[tok_sorted], mode='drop')
            g = jnp.einsum('ecd,efd->ecf', xbuf, w_gate)
            u = jnp.einsum('ecd,efd->ecf', xbuf, w_up)
            y = jnp.einsum('ecf,edf->ecd', jax.nn.silu(g) * u, w_down)
            y_pair = y[e_sorted, safe_pos] * (s_sorted * valid)[:, None]
            out = jnp.zeros((N, D), dtype=x.dtype).at[tok_sorted].add(y_pair)
            return out.reshape(B, S, D)
        key = jax.random.key(seed)
        k1, k2, k3, k4, k5 = jax.random.split(key, 5)
        hidden_states = jax.random.normal(k1, (BATCH, SEQ, HIDDEN), dtype=jnp.float32)
        gate_w = jax.random.normal(k2, (NUM_EXPERTS, HIDDEN), dtype=jnp.float32) * 0.02
        w_gate = jax.random.normal(k3, (NUM_EXPERTS, FFN, HIDDEN), dtype=jnp.float32) * 0.02
        w_up = jax.random.normal(k4, (NUM_EXPERTS, FFN, HIDDEN), dtype=jnp.float32) * 0.02
        w_down = jax.random.normal(k5, (NUM_EXPERTS, HIDDEN, FFN), dtype=jnp.float32) * 0.02
        return {'hidden_states': hidden_states, 'gate_w': gate_w, 'w_gate': w_gate, 'w_up': w_up, 'w_down': w_down}
    _L0_ffn_all = _L0_ffn_setup()
    _L0_ffn_in = {k: v for k, v in _L0_ffn_all.items() if k in ('gate_w', 'w_gate', 'w_up', 'w_down')}
    del _L0_ffn_all
    return {'x': x, 'ctx_2048': ctx_2048, 'L0_xattn_wq': _L0_xattn_in['wq'], 'L0_xattn_bq': _L0_xattn_in['bq'], 'L0_xattn_wkv': _L0_xattn_in['wkv'], 'L0_xattn_bkv': _L0_xattn_in['bkv'], 'L0_xattn_wp': _L0_xattn_in['wp'], 'L0_xattn_bp': _L0_xattn_in['bp'], 'L0_attn_x_proj_w': _L0_attn_in['x_proj_w'], 'L0_attn_dt_proj_w': _L0_attn_in['dt_proj_w'], 'L0_attn_dt_proj_b': _L0_attn_in['dt_proj_b'], 'L0_attn_A_log': _L0_attn_in['A_log'], 'L0_attn_D_param': _L0_attn_in['D_param'], 'L0_ffn_gate_w': _L0_ffn_in['gate_w'], 'L0_ffn_w_gate': _L0_ffn_in['w_gate'], 'L0_ffn_w_up': _L0_ffn_in['w_up'], 'L0_ffn_w_down': _L0_ffn_in['w_down']}

def reference(x, ctx_2048, L0_xattn_wq, L0_xattn_bq, L0_xattn_wkv, L0_xattn_bkv, L0_xattn_wp, L0_xattn_bp, L0_attn_x_proj_w, L0_attn_dt_proj_w, L0_attn_dt_proj_b, L0_attn_A_log, L0_attn_D_param, L0_ffn_gate_w, L0_ffn_w_gate, L0_ffn_w_up, L0_ffn_w_down):
    import jax
    import jax.numpy as jnp

    def _L0_xattn_ref(x, cond, wq, bq, wkv, bkv, wp, bp):
        import jax, jax.numpy as jnp
        import numpy as np
        NUM_HEADS = 16

        def _qdq(x):
            s = jnp.maximum(jnp.max(jnp.abs(x), axis=-1, keepdims=True) / 127.0, 1e-08)
            return jnp.clip(jnp.round(x / s), -127.0, 127.0) * s
        B, N, C = x.shape
        M = cond.shape[1]
        H = NUM_HEADS
        Dh = C // H
        q = _qdq(x) @ _qdq(wq).T + bq
        kv = cond @ wkv.T + bkv
        k, v = jnp.split(kv, 2, axis=-1)
        q = q.reshape(B, N, H, Dh)
        k = k.reshape(B, M, H, Dh)
        v = v.reshape(B, M, H, Dh)
        scale = 1.0 / np.sqrt(Dh)
        attn = jax.nn.softmax(jnp.einsum('bnhd,bmhd->bhnm', q, k) * scale, axis=-1)
        o = jnp.einsum('bhnm,bmhd->bnhd', attn, v).reshape(B, N, C)
        out = _qdq(o) @ _qdq(wp).T + bp
        return out

    def _L0_attn_ref(x, x_proj_w, dt_proj_w, dt_proj_b, A_log, D_param):
        import jax, jax.numpy as jnp
        import numpy as np

        def _selective_scan(x, dt, a_mat, b_mat, c_mat):
            a_bar = jnp.exp(dt[..., None] * a_mat[None, None])
            b_bar_x = (dt * x)[..., None] * b_mat[:, :, None, :]
            a_t = jnp.moveaxis(a_bar, 1, 0)
            bx_t = jnp.moveaxis(b_bar_x, 1, 0)
            c_t = jnp.moveaxis(c_mat, 1, 0)
            h0 = jnp.zeros(a_t.shape[1:], dtype=x.dtype)

            def step(h, inp):
                a, bx, c = inp
                h = a * h + bx
                y = jnp.einsum('bdn,bn->bd', h, c)
                return (h, y)
            _, ys = jax.lax.scan(step, h0, (a_t, bx_t, c_t))
            return jnp.moveaxis(ys, 0, 1)
        R = dt_proj_w.shape[1]
        N = A_log.shape[1]
        xp = jnp.einsum('bld,pd->blp', x, x_proj_w)
        dt_low, b_mat, c_mat = jnp.split(xp, [R, R + N], axis=-1)
        dt = jax.nn.softplus(jnp.einsum('blr,dr->bld', dt_low, dt_proj_w) + dt_proj_b)
        a_mat = -jnp.exp(A_log)
        y = _selective_scan(x, dt, a_mat, b_mat, c_mat)
        return y + x * D_param[None, None, :]

    def _L0_ffn_ref(hidden_states, gate_w, w_gate, w_up, w_down):
        import jax, jax.numpy as jnp
        import numpy as np
        NUM_EXPERTS = 64
        TOP_K = 8
        HIDDEN = 256
        FFN = 96
        BATCH, SEQ = (1, 256)
        CAP_FACTOR = 2

        def _moe_forward(hidden_states, gate_w, w_gate, w_up, w_down):
            B, S, D = hidden_states.shape
            E = gate_w.shape[0]
            x = hidden_states.reshape(-1, D)
            N = x.shape[0]
            P = N * TOP_K
            C = CAP_FACTOR * P // E
            logits = x @ gate_w.T
            probs = jax.nn.softmax(logits, axis=-1)
            scores, idx = jax.lax.top_k(probs, TOP_K)
            flat_e = idx.reshape(-1)
            order = jnp.argsort(flat_e)
            e_sorted = flat_e[order]
            tok_sorted = order // TOP_K
            s_sorted = scores.reshape(-1)[order]
            counts = jnp.bincount(e_sorted, length=E)
            starts = jnp.cumsum(counts) - counts
            pos = jnp.arange(P) - starts[e_sorted]
            valid = pos < C
            safe_pos = jnp.minimum(pos, C - 1)
            xbuf = jnp.zeros((E, C, D), dtype=x.dtype).at[e_sorted, pos].set(x[tok_sorted], mode='drop')
            g = jnp.einsum('ecd,efd->ecf', xbuf, w_gate)
            u = jnp.einsum('ecd,efd->ecf', xbuf, w_up)
            y = jnp.einsum('ecf,edf->ecd', jax.nn.silu(g) * u, w_down)
            y_pair = y[e_sorted, safe_pos] * (s_sorted * valid)[:, None]
            out = jnp.zeros((N, D), dtype=x.dtype).at[tok_sorted].add(y_pair)
            return out.reshape(B, S, D)
        return _moe_forward(hidden_states, gate_w, w_gate, w_up, w_down)
    x = x + _L0_xattn_ref(_layernorm(x, axis=-1), ctx_2048, L0_xattn_wq, L0_xattn_bq, L0_xattn_wkv, L0_xattn_bkv, L0_xattn_wp, L0_xattn_bp)
    x = x + _L0_attn_ref(_layernorm(x, axis=-1), L0_attn_x_proj_w, L0_attn_dt_proj_w, L0_attn_dt_proj_b, L0_attn_A_log, L0_attn_D_param)
    x = x + _L0_ffn_ref(_layernorm(x, axis=-1), L0_ffn_gate_w, L0_ffn_w_gate, L0_ffn_w_up, L0_ffn_w_down)
    return x

_drawn_inputs = setup_inputs


def setup_inputs(seed=0):
    import zlib

    import numpy as np

    out = dict(_drawn_inputs(seed))
    spreads = {'L0_attn_D_param': (1.0, 0.2)}
    factors = {'L0_xattn_wq': 8.0,
     'L0_xattn_bq': 64.0,
     'L0_xattn_bkv': 5.972,
     'L0_ffn_gate_w': 8.0,
     'L0_ffn_w_gate': 8.0,
     'L0_ffn_w_up': 8.0,
     'L0_ffn_w_down': 8.0}
    for name, (base, spread) in spreads.items():
        noise = np.random.default_rng([zlib.crc32(name.encode()), seed]).standard_normal(out[name].shape)
        drawn = base * np.exp(spread * noise) if base else spread * noise
        out[name] = jnp.asarray(drawn.astype(out[name].dtype))
    for name, factor in factors.items():
        out[name] = (out[name] * factor).astype(out[name].dtype)
    return out
```

```python
from contextlib import ExitStack

import numpy as np
import concourse.bass as bass
from concourse import mybir

F32 = mybir.dt.float32
F32R = mybir.dt.float32r
BF16 = mybir.dt.bfloat16
U32 = mybir.dt.uint32
ALU = mybir.AluOpType
ACT = mybir.ActivationFunctionType
AX = mybir.AxisListType

P = 128
B, N, D = 32, 64, 256
M = 1601
H, DH = 16, 16
DT = D // P
TOK = B * N
PAIRS = TOK // P
HG = 8
STRIPS = 4
MP = 1602
KT = (M + P - 1) // P
CHUNKS = [(c, min(512, M - c)) for c in range(0, M, 512)]
NS, R = 16, 128
E, TOPK, FF = 64, 8, 96
CAP = 2 * TOK * TOPK // E
CT = CAP // P
MAGIC = 12582912.0
EPS = 1e-5
LN_TINY = 1e-30

STEPS = 4
SLOTS = STEPS * STRIPS
PV_SPLIT = [0, 4, 7, 10, 13]
V_UNITS = [[t for t in (2 * u, 2 * u + 1) if t < KT] for u in range((KT + 1) // 2)]
V_OF_STEP = {0: [4, 5, 6], 1: [0, 1, 2, 3], 2: [4, 5, 6], 3: [0, 1, 2, 3]}



def a_order():
    order = []
    for slot in range(SLOTS):
        j, s = divmod(slot, STRIPS)
        if slot == 8:
            order.append(("O", 0))
        if slot == 12:
            order += [("O", 1), ("XQ",), ("Q",)]
        order.append(("K", (j + 1) % STEPS, s))
        if s < len(V_OF_STEP[j]):
            order.append(("V", 1 if j in (1, 2) else 0, V_OF_STEP[j][s]))
    return order


A_ORDER = a_order()
assert A_ORDER.index(("V", 0, 6)) < A_ORDER.index(("K", 1, 3)) and A_ORDER.index(("V", 1, 6)) < A_ORDER.index(("K", 3, 3))
AHEAD = A_ORDER[A_ORDER.index(("XQ",)):]
B_ORDER = ["O2", "O3", "oqT", "proj", "ln2T", "xp", "dt", "yT", "ln3T", "logits", "pos"]
DVE_ORDER = ["OQ", "X2", "V2", "LN2", "Z", "EZ", "U", "S00", "S01", "Y0", "S10", "S11", "Y1", "V3", "LN3", "LOGITS", "SEL", "ROUTE"]
ACT_ORDER = ["EXPZ", "LNZ", "AB00", "AB01", "AB10", "AB11"]
POOL_ORDER = ["R2", "BX0", "BX1", "R3"]


B_LINKS = 53


def a_at(i, *name):
    return len(AHEAD) + (i - (name in AHEAD)) * len(A_ORDER) + A_ORDER.index(name) + 1


def in_order(order):
    def at(i, name):
        return i * len(order) + order.index(name) + 1
    return at


b_at, dve_at, act_at, pool_at = (in_order(o) for o in (B_ORDER, DVE_ORDER, ACT_ORDER, POOL_ORDER))


def keys_in(t):
    return min(P, M - t * P)


def after(eng, sem, value):
    if isinstance(value, int) and value <= 0:
        return
    eng.wait_ge(sem, value)


class Chain:

    def __init__(self, eng, sem, turn, per, pause=None):
        self.eng, self.sem, self.base, self.per, self.n, self.pause = eng, sem, turn * per, per, 0, pause

    def __call__(self, ins):
        self.n += 1
        ins.then_inc(self.sem, 1)
        self.eng.wait_ge(self.sem, self.base + self.n)

    def carried(self, ins=None):
        if ins is not None:
            self(ins)
        self.n += 1
        self.eng.memset(self.pause, 0.0).then_inc(self.sem, 1)

    def end(self):
        assert self.n == self.per, self.n


def over_pairs(eng, body):
    body(0, True, False, True)
    body(1, True, True, True)
    with eng.Fori(2, PAIRS - 1) as i:
        body(i, True, True, True)
    body(PAIRS - 1, True, True, False)
    body(PAIRS, False, True, False)


def pieces(i, slot, cur, prev, nxt):
    j, s = divmod(slot, STRIPS)
    old = (i - 1, 3) if j == 0 else (i, j - 1)
    tiles = list(range(PV_SPLIT[s], PV_SPLIT[s + 1])) if (prev if j == 0 else cur) else []
    k = v = None
    if cur and (j < 3 or nxt):
        k = (i, j + 1, s) if j < 3 else (i + 1, 0, s)
        if s < len(V_OF_STEP[j]):
            v = {0: (i, 0), 1: (i, 1), 2: (i, 1), 3: (i + 1, 0)}[j] + (V_OF_STEP[j][s],)
    return j, s, old, tiles, k, v


def mixer_phase(nc, io, dram):
    with ExitStack() as ctx:
        def sb(name, shape, dt=F32):
            return ctx.enter_context(nc.sbuf_tensor("sb_" + name, shape, dt))

        def sem(name):
            return ctx.enter_context(nc.semaphore(name))

        wqT = sb("wqT", [P, DT, D])
        wpT = sb("wpT", [P, DT, D])
        wkvT = sb("wkvT", [P, DT, 2 * D])
        xpT = sb("xpT", [P, DT, R + 2 * NS])
        dpT = sb("dpT", [P, D])
        gateT = sb("gateT", [P, DT, E])
        cols = sb("cols", [P, 4, DT])
        bv_row = sb("bv_row", [P, D])
        bp_row = sb("bp_row", [P, D])
        A = sb("A", [P, DT, NS])
        ident = sb("ident", [P, P])
        headmask = sb("headmask", [P, HG])
        before = sb("before", [P, P], BF16)
        ones = sb("ones", [P, P], BF16)
        iota_e = sb("iota_e", [P, E])
        tokid = sb("tokid", [P, 1])
        tile_rows = sb("tile_rows", [P, 1])
        pause, pause_q, pause_p = (sb(n, [P, 1]) for n in ("pause", "pause_q", "pause_p"))
        neg_half = sb("neg_half", [P, 1])
        ctxT = [sb(f"ctxT{n}", [P, DT, M]) for n in range(2)]
        K_hi = [sb(f"K_hi{n}", [P, MP], F32R) for n in range(2)]
        K_lo = [sb(f"K_lo{n}", [P, MP], F32R) for n in range(2)]
        V = [sb(f"V{n}", [P, KT, D]) for n in range(2)]
        Q_hi = [sb(f"Q_hi{n}", [P, HG, N], F32R) for n in range(2)]
        Q_lo = [sb(f"Q_lo{n}", [P, HG, N], F32R) for n in range(2)]
        probs = [[sb(f"probs{n}_{s}", [P, M]) for s in range(STRIPS)] for n in range(2)]
        probsT = [sb(f"probsT{n}", [P, STRIPS * P]) for n in range(2)]
        negmax = sb("negmax", [P, STEPS * STRIPS])
        den = sb("den", [P, STEPS * STRIPS])
        rden = sb("rden", [P, STEPS * STRIPS])
        OT = sb("OT", [P, P])
        x_q = sb("x_q", [P, D])
        lnq = sb("lnq", [P, D])
        oq = sb("oq", [P, D])
        xqT = sb("xqT", [P, DT, P])
        q_f = sb("q_f", [P, DT, P])
        q_hi = sb("q_hi", [P, DT, P])
        q_lo = sb("q_lo", [P, DT, P])
        st = sb("st", [P, 64])
        o_tok = sb("o_tok", [P, D])
        x_res = sb("x_res", [P, D])
        x2 = sb("x2", [P, D])
        ln2 = sb("ln2", [P, D])
        ln2T = sb("ln2T", [P, DT, P])
        oqT = sb("oqT", [P, DT, P])
        dlT = sb("dlT", [P, P])
        BCT = sb("BCT", [2 * NS, P])
        BC = sb("BC", [P, 2 * NS, P])
        z = sb("z", [P, DT, P])
        negz = sb("negz", [P, DT, P])
        ez = sb("ez", [P, DT, P])
        ez1 = sb("ez1", [P, DT, P])
        lz = sb("lz", [P, DT, P])
        dt_ = sb("dt_", [P, DT, P])
        u = sb("u", [P, DT, P])
        abar = sb("abar", [P, NS // 2, P])
        bx = sb("bx", [P, NS, P])
        wq_rows, wp_rows = (bx[:, n:n + 4, :].rearrange("p (k a) b -> p k (a b)", k=DT) for n in (4, 8))
        y = z
        x3 = sb("x3", [P, D])
        ln3 = sb("ln3", [P, D])
        ln3T = oqT
        pr = sb("pr", [P, E])
        pr2 = sb("pr2", [P, E])
        sel = sb("sel", [P, E], BF16)
        slotv = sb("slotv", [P, E])
        base_e = sb("base_e", [P, E])
        top = sb("top", [P, TOPK])
        topi = sb("topi", [P, TOPK], U32)
        topf = sb("topf", [P, 6, TOPK])
        junk = sb("junk", [P, E])
        sc_idx = sb("sc_idx", [P, TOPK], U32)
        slots_all, scores_all = dram["slots_sb"], dram["scores_sb"]

        S = ctx.enter_context(nc.psum_tensor("S", [P, 2048], F32))
        PT = [ctx.enter_context(nc.psum_tensor(f"PT{n}", [P, 512], F32)) for n in range(2)]
        O = ctx.enter_context(nc.psum_tensor("O", [P, 512], F32))
        W = ctx.enter_context(nc.psum_tensor("W", [P, 512], F32))

        w_in = sem("w_in")
        consts = sem("consts")
        wq_set = sem("w_set")
        a_set = sem("a_set")
        w_mm = sem("w_mm")
        table_zero = sem("table_zero")
        ctx_in = [sem(f"ctx_in{n}") for n in range(2)]
        x_in = sem("x_in")
        xr_in = sem("xr_in")
        bank_full = [sem("bank_full_a"), sem("bank_full_b")]
        bank_free = [sem("bank_free_a"), sem("bank_free_b")]
        k_hi_up = sem("k_hi_up")
        var_up = sem("var_up")
        rstd_up = sem("rstd_up")
        lnq_up = sem("lnq_up")
        q_split = sem("q_split")
        q_up = sem("q_up")
        s_done = sem("s_done")
        max_done = sem("max_done")
        exp_done = sem("exp_done")
        t_done = sem("t_done")
        t_up = [sem("t_up_act"), sem("t_up_dve")]
        pv_done = sem("pv_done")
        o_up = sem("o_up")
        dve_up = sem("dve_up")
        act_up = sem("act_up")
        pool_up = sem("pool_up")
        bc_out = sem("bc_out")
        bc_in = sem("bc_in")
        x3_out = sem("x3_out")
        scattered = sem("scattered")
        tokid_up = sem("tokid_up")
        dve_w, dve_q, dve_q2, dve_o, dve_b = (sem(f"dve_{n}") for n in ("w", "q", "q2", "o", "b"))
        block = ctx.enter_context(nc.Block())

        loads = (
            (wq_rows, io["wq"].rearrange("(k p) i -> p k i", p=P)),
            (wp_rows, io["wp"].rearrange("(k p) i -> p k i", p=P)),
            (wkvT[:], io["wkvT"].rearrange("(k p) o -> p k o", p=P)),
            (xpT[:], io["xpT"].rearrange("(k p) o -> p k o", p=P)),
            (dpT[:], io["dpT"]),
            (gateT[:], io["gateT"].rearrange("(k p) o -> p k o", p=P)),
            (cols[:, 0, :], io["bq"]), (cols[:, 1, :], io["bk"]),
            (cols[:, 2, :], io["dtb"]), (cols[:, 3, :], io["Dp"]),
            (bv_row[:], io["bv"].partition_broadcast(P)),
            (bp_row[:], io["bp"].partition_broadcast(P)),
            (A[:], io["A_log"].rearrange("(h p) n -> p h n", p=P)),
        )
        BQ, BK, DTB, DP = range(4)

        @block.sync
        def _(sp):
            def x_rows(i):
                return io["x"][bass.ds(i * P, P), :]

            def ctx_of(batch):
                return io["ctxT"][bass.ds(batch, 1)].rearrange("o (k p) m -> p (o k) m", p=P)

            for dst, src in loads:
                sp.dma_start(dst, src).then_inc(w_in, 16)
            sp.dma_start(x_q[:], x_rows(0)).then_inc(x_in, 16)
            for n in range(2):
                sp.dma_start(ctxT[n][:], ctx_of(n)).then_inc(ctx_in[n], 16)

            def body(i, cur, prev, nxt):
                if cur and nxt:
                    sp.wait_ge(lnq_up, i + 1)
                    sp.dma_start(x_q[:], x_rows(i + 1)).then_inc(x_in, 16)
                    sp.wait_ge(bank_full[0], a_at(i, "K", 1, 3))
                    sp.dma_start(ctxT[0][:], ctx_of(2 * i + 2)).then_inc(ctx_in[0], 16)
                if prev:
                    after(sp, dve_up, dve_at(i - 2, "Y1"))
                    sp.dma_start(x_res[:], x_rows(i - 1)).then_inc(xr_in, 16)
                    sp.wait_ge(bank_free[1], b_at(i - 1, "xp"))
                    sp.dma_start(dram["bc"], BCT[:]).then_inc(bc_out, 16)
                    sp.wait_ge(bc_out, i * 16)
                    sp.dma_start(BC[:].rearrange("p n t -> p (n t)"), dram["bc"].rearrange("n t -> (n t)").partition_broadcast(P)).then_inc(bc_in, 16)
                if cur and nxt:
                    sp.wait_ge(bank_full[0], a_at(i, "K", 3, 3))
                    sp.dma_start(ctxT[1][:], ctx_of(2 * i + 3)).then_inc(ctx_in[1], 16)
                if prev:
                    sp.wait_ge(dve_up, dve_at(i - 1, "LN3"))
                    sp.dma_start(dram["x3"][bass.ds((i - 1) * P, P), :], x3[:]).then_inc(x3_out, 16)
                    sp.dma_start(dram["ln3"][bass.ds((i - 1) * P, P), :], ln3[:]).then_inc(x3_out, 16)

            over_pairs(sp, body)
            sp.wait_ge(x3_out, 32 * PAIRS)

        @block.gpsimd
        def _(pool):
            pool.memset(ident[:], 0.0).then_inc(consts, 1)
            pool.memset(headmask[:], 1.0).then_inc(consts, 1)
            pool.memset(ones[:], 1.0).then_inc(consts, 1)
            pool.memset(neg_half[:], -0.5).then_inc(consts, 1)
            pool.memset(bx[:, 0:2, :], 0.0).then_inc(consts, 1)
            for n in range(2):
                pool.memset(K_hi[n][:, M:MP].bitcast(F32), 0.0).then_inc(consts, 1)
                pool.memset(K_lo[n][:, M:MP].bitcast(F32), 0.0).then_inc(consts, 1)
            pool.iota(iota_e[:], [[1, E]], base=0, channel_multiplier=0,
                      allow_small_or_imprecise_dtypes=True).then_inc(consts, 1)
            pool.iota(tokid[:], [[0, 1]], base=-P, channel_multiplier=1,
                      allow_small_or_imprecise_dtypes=True).then_inc(consts, 1)
            pool.iota(base_e[:], [[CAP, E]], base=0, channel_multiplier=0,
                      allow_small_or_imprecise_dtypes=True).then_inc(consts, 1)
            pool.memset(tile_rows[:], float(P)).then_inc(consts, 1)
            pool.wait_ge(consts, 13)
            pool.affine_select(out=ident[:], in_=ident[:], compare_op=ALU.not_equal, fill=1.0, base=0,
                               pattern=[[-1, P]], channel_multiplier=1).then_inc(consts, 1)
            pool.affine_select(out=headmask[:], in_=headmask[:], compare_op=ALU.is_ge, fill=0.0, base=0,
                               pattern=[[-DH, HG]], channel_multiplier=1).then_inc(consts, 1)
            pool.affine_select(out=before[:], in_=ones[:], compare_op=ALU.is_gt, fill=0.0, base=0,
                               pattern=[[1, P]], channel_multiplier=-1).then_inc(consts, 1)
            pool.dma_start(dram["table"].rearrange("(p c) o -> p (c o)", p=P),
                           bx[:, 0:2, :].rearrange("p a b -> p (a b)")).then_inc(table_zero, 16)
            pool.wait_ge(consts, 16)
            pool.affine_select(out=headmask[:], in_=headmask[:], compare_op=ALU.is_ge, fill=0.0, base=DH - 1,
                               pattern=[[DH, HG]], channel_multiplier=-1).then_inc(consts, 1)
            pool.wait_ge(consts, 17)
            pool.wait_ge(table_zero, 16)

            def rstd_q(i):
                pool.wait_ge(var_up, i + 1)
                pool.tensor_tensor(st[:, 1:2], st[:, 0:1], neg_half[:], ALU.pow).then_inc(rstd_up, 1)

            def spread_q(i, j):
                b, g = divmod(j, 2)
                pool.wait_ge(q_split, i + 1)
                after(pool, s_done, i * SLOTS + STRIPS * (j - 1))
                for dst, src in ((Q_hi[j % 2], q_hi), (Q_lo[j % 2], q_lo)):
                    pool.tensor_tensor(
                        dst[:], src[:, g, b * N:(b + 1) * N].unsqueeze(1).to_broadcast([P, HG, N]),
                        headmask[:].unsqueeze(2).to_broadcast([P, HG, N]), ALU.mult).then_inc(q_up, 1)

            def scan_input(i, h):
                pool.wait_ge(dve_up, dve_at(i, "U" if h == 0 else "Y0"))
                pool.wait_ge(bc_in, (i + 1) * 16)
                pool.tensor_tensor(bx[:], u[:, h, :].unsqueeze(1).to_broadcast([P, NS, P]),
                                   BC[:, 0:NS, :], ALU.mult).then_inc(pool_up, 1)

            rstd_q(0)
            spread_q(0, 0)

            def body(i, cur, prev, nxt):
                if cur:
                    spread_q(i, 1)
                    spread_q(i, 2)
                if prev:
                    pool.wait_ge(dve_up, dve_at(i - 1, "V2"))
                    pool.tensor_tensor(st[:, 9:10], st[:, 8:9], neg_half[:], ALU.pow).then_inc(pool_up, 1)
                if cur:
                    spread_q(i, 3)
                if prev:
                    scan_input(i - 1, 0)
                if cur and nxt:
                    rstd_q(i + 1)
                if prev:
                    scan_input(i - 1, 1)
                if cur and nxt:
                    spread_q(i + 1, 0)
                if prev:
                    pool.wait_ge(dve_up, dve_at(i - 1, "V3"))
                    pool.tensor_tensor(st[:, 17:18], st[:, 16:17], neg_half[:], ALU.pow).then_inc(pool_up, 1)
                    after(pool, scattered, 16 * TOPK * (i - 1))
                    pool.tensor_tensor(tokid[:], tokid[:], tile_rows[:], ALU.add).then_inc(tokid_up, 1)
                    pool.wait_ge(tokid_up, 2 * i - 1)
                    pool.wait_ge(dve_up, dve_at(i - 1, "ROUTE"))
                    pool.tensor_tensor(pause_p[:], tile_rows[:], tile_rows[:], ALU.add).then_inc(tokid_up, 1)
                    for t in range(TOPK):
                        pool.indirect_dma_start(
                            dram["table"], bass.IndirectOffsetOnAxis(ap=sc_idx[:, t:t + 1], axis=0),
                            tokid[:], None, bounds_check=E * CAP - 1, oob_is_err=False).then_inc(scattered, 16)

            over_pairs(pool, body)
            pool.wait_ge(scattered, 16 * TOPK * PAIRS)

        @block.tensor
        def _(pe):
            last = [None]

            def take(part, value):
                if last[0] is not None:
                    after(pe, *last[0])
                last[0] = (bank_free[part], value)

            pe.wait_ge(consts, 17)
            for n, rows in enumerate((wq_rows, wp_rows)):
                pe.wait_ge(wq_set, 2 * n + 1)
                for k in range(DT):
                    for o in range(DT):
                        ins = pe.transpose(W[:, (k * DT + o) * P:(k * DT + o + 1) * P],
                                           rows[:, o, k * P:(k + 1) * P], ident[:])
                ins.then_inc(w_mm, 1)
            pe.wait_ge(wq_set, 4)
            pe.wait_ge(w_in, 16 * len(loads))

            def q_mm(i):
                take(0, a_at(i, "XQ"))
                pe.wait_ge(lnq_up, i + 1)
                for k in range(DT):
                    ins = pe.transpose(W[:, k * P:(k + 1) * P], lnq[:, k * P:(k + 1) * P], ident[:])
                ins.then_inc(bank_full[0], 1)
                take(0, a_at(i, "Q"))
                for g in range(2):
                    for k in range(DT):
                        ins = pe.matmul(W[:, g * P:(g + 1) * P], wqT[:, k, g * P:(g + 1) * P], xqT[:, k, :],
                                        start=(k == 0), stop=(k == DT - 1))
                ins.then_inc(bank_full[0], 1)

            def k_mm(i, j, c):
                b, g = divmod(j, 2)
                c0, cn = CHUNKS[c]
                take(0, a_at(i, "K", j, c))
                pe.wait_ge(ctx_in[b], 16 * (i + 1))
                for k in range(DT):
                    ins = pe.matmul(W[:, 0:cn], wkvT[:, k, g * P:(g + 1) * P], ctxT[b][:, k, c0:c0 + cn],
                                    start=(k == 0), stop=(k == DT - 1))
                ins.then_inc(bank_full[0], 1)

            def v_mm(i, b, unit):
                take(0, a_at(i, "V", b, unit))
                pe.wait_ge(ctx_in[b], 16 * (i + 1))
                for n, t in enumerate(V_UNITS[unit]):
                    for k in range(DT):
                        ins = pe.matmul(W[0:keys_in(t), n * D:(n + 1) * D], ctxT[b][:, k, t * P:t * P + keys_in(t)],
                                        wkvT[:, k, D:2 * D], start=(k == 0), stop=(k == DT - 1))
                ins.then_inc(bank_full[0], 1)

            def scores(i, j, s):
                if s == 0:
                    pe.wait_ge(bank_free[0], a_at(i, "K", j, 3))
                    pe.wait_ge(q_up, i * 2 * STEPS + 2 * (j + 1))
                after(pe, exp_done, i * SLOTS + STRIPS * j + s)
                for c in range(0, M, 512):
                    cn = min(512, MP - c)
                    for n, (lhs, rhs) in enumerate(((Q_hi, K_hi), (Q_hi, K_lo), (Q_lo, K_hi))):
                        ins = pe.matmul(S[:, c:c + cn], lhs[j % 2][:, 2 * s:2 * s + 2, :].rearrange("p h n -> p (h n)"),
                                        rhs[j % 2][:, c:c + cn], start=(n == 0), stop=(n == 2))
                ins.then_inc(s_done, 1)

            def turn(i, j, t):
                n = KT * j + t
                pe.wait_ge(exp_done, i * SLOTS + STRIPS * (j + 1))
                after(pe, t_up[n % 2], i * (STEPS * KT // 2) + n // 2)
                for s in range(STRIPS):
                    ins = pe.transpose(PT[n % 2][0:keys_in(t), s * P:(s + 1) * P],
                                       probs[j % 2][s][:, t * P:t * P + keys_in(t)], ident[:])
                ins.then_inc(t_done, 1)

            def times_v(i, j, t):
                n = KT * j + t
                b, g = divmod(j, 2)
                pe.wait_ge(t_up[n % 2], i * (STEPS * KT // 2) + n // 2 + 1)
                if t == 0:
                    after(pe, o_up, i * STEPS + j)
                    pe.wait_ge(bank_free[0], a_at(i, "V", b, 6))
                for s in range(STRIPS):
                    ins = pe.matmul(O[32 * s:32 * s + 32, 0:P],
                                    V[b][0:keys_in(t), t, g * P + 32 * s:g * P + 32 * s + 32],
                                    probsT[n % 2][0:keys_in(t), s * P:(s + 1) * P],
                                    start=(t == 0), stop=(t == KT - 1))
                ins.then_inc(pv_done, 1)

            def turn_o(i, j):
                part, value = (0, a_at(i, "O", j)) if j < 2 else (1, b_at(i, f"O{j}"))
                take(part, value)
                pe.wait_ge(o_up, i * STEPS + j + 1)
                pe.transpose(W[:, 0:P], OT[:], ident[:]).then_inc(bank_full[part], 1)

            def turn_two(i, name, src, ready, value):
                take(1, b_at(i, name))
                pe.wait_ge(ready, value)
                for k in range(DT):
                    ins = pe.transpose(W[:, k * P:(k + 1) * P], src(k), ident[:])
                ins.then_inc(bank_full[1], 1)

            def rest(i, slot):
                if slot == 5:
                    turn_two(i, "oqT", lambda k: oq[:, k * P:(k + 1) * P], dve_up, dve_at(i, "OQ"))
                if slot == 6:
                    take(1, b_at(i, "proj"))
                    for k in range(DT):
                        ins = pe.matmul(W[:, 0:D], oqT[:, k, :], wpT[:, k, :], start=(k == 0), stop=(k == DT - 1))
                    ins.then_inc(bank_full[1], 1)
                if slot == 7:
                    turn_two(i, "ln2T", lambda k: ln2[:, k * P:(k + 1) * P], dve_up, dve_at(i, "LN2"))
                if slot == 8:
                    take(1, b_at(i, "xp"))
                    pe.wait_ge(bank_free[1], b_at(i, "ln2T"))
                    for k in range(DT):
                        pe.matmul(W[:, 0:P], xpT[:, k, 0:R], ln2T[:, k, :], start=(k == 0), stop=(k == DT - 1))
                    for k in range(DT):
                        ins = pe.matmul(W[0:2 * NS, P:2 * P], xpT[:, k, R:R + 2 * NS], ln2T[:, k, :],
                                        start=(k == 0), stop=(k == DT - 1))
                    ins.then_inc(bank_full[1], 1)
                if slot == 9:
                    take(1, b_at(i, "dt"))
                    pe.wait_ge(bank_free[1], b_at(i, "xp"))
                    for h in range(DT):
                        ins = pe.matmul(W[:, h * P:(h + 1) * P], dpT[:, h * P:(h + 1) * P], dlT[:], start=True, stop=True)
                    ins.then_inc(bank_full[1], 1)
                if slot == 13:
                    turn_two(i, "yT", lambda k: y[:, k, :], dve_up, dve_at(i, "Y1"))
                if slot == 14:
                    turn_two(i, "ln3T", lambda k: ln3[:, k * P:(k + 1) * P], dve_up, dve_at(i, "LN3"))
                    take(1, b_at(i, "logits"))
                    for k in range(DT):
                        ins = pe.matmul(W[:, 0:E], ln3T[:, k, :], gateT[:, k, :], start=(k == 0), stop=(k == DT - 1))
                    ins.then_inc(bank_full[1], 1)
                if slot == 15:
                    take(1, b_at(i, "pos"))
                    pe.wait_ge(dve_up, dve_at(i, "SEL"))
                    pe.matmul(W[:, 0:E], before[:], sel[:], start=True, stop=True)
                    pe.matmul(W[:, E:2 * E], ones[:], sel[:], start=True, stop=True).then_inc(bank_full[1], 1)

            q_mm(0)
            for c in range(4):
                k_mm(0, 0, c)
                v_mm(0, 0, V_OF_STEP[3][c])

            def body(i, cur, prev, nxt):
                last[0] = (bank_free[0], a_at(i, "V", 0, 3)) if cur else (bank_free[1], b_at(i - 2, "pos"))
                for slot in range(SLOTS):
                    j, s, old, tiles, k, v = pieces(i, slot, cur, prev, nxt)
                    if slot == 1 and prev:
                        turn_o(i - 1, 2)
                    if slot == 4 and prev:
                        turn_o(i - 1, 3)
                    if slot in (8, 12) and cur:
                        turn_o(i, j - 2)
                    if slot == 12 and cur and nxt:
                        q_mm(i + 1)
                    if prev:
                        rest(i - 1, slot)
                    if cur:
                        scores(i, j, s)
                    for n, t in enumerate(tiles):
                        turn(*old, t)
                        if t >= 1:
                            times_v(*old, t - 1)
                        if n == 1 and k:
                            k_mm(*k)
                    if k and not tiles:
                        k_mm(*k)
                    if tiles and s == 3:
                        times_v(*old, KT - 1)
                    if v:
                        v_mm(*v)

            over_pairs(pe, body)

        @block.scalar
        def _(act):
            act.wait_ge(w_in, 16 * len(loads))
            act.activation(A[:], A[:], ACT.Exp).then_inc(a_set, 1)
            act.wait_ge(a_set, 1)
            act.mul(A[:], A[:], -1.0).then_inc(a_set, 1)
            act.wait_ge(a_set, 2)

            def k_up(i, j, c):
                g = j % 2
                c0, cn = CHUNKS[c]
                act.wait_ge(bank_full[0], a_at(i, "K", j, c))
                after(act, s_done, i * SLOTS + STRIPS * (j - 1))
                act.activation(K_hi[j % 2][:, c0:c0 + cn], W[:, 0:cn], ACT.Identity,
                               bias=cols[:, BK, g:g + 1]).then_inc(k_hi_up, 1)

            def v_up(i, b, unit):
                tiles = V_UNITS[unit]
                act.wait_ge(bank_full[0], a_at(i, "V", b, unit))
                after(act, pv_done, (i - 1) * STEPS * KT + 2 * KT * (b + 1))
                act.activation(V[b][0:keys_in(tiles[-1]), tiles[0]:tiles[-1] + 1, :].rearrange("p t d -> p (t d)"),
                               W[0:keys_in(tiles[-1]), 0:len(tiles) * D], ACT.Copy).then_inc(bank_free[0], 1)

            def turned(i, j, t):
                n = KT * j + t
                act.wait_ge(t_done, i * STEPS * KT + n + 1)
                after(act, pv_done, i * STEPS * KT + n - 1)
                act.activation(probsT[n % 2][0:keys_in(t), :], PT[0][0:keys_in(t), :], ACT.Copy).then_inc(t_up[0], 1)

            def soft(i, j, s):
                q = STRIPS * j + s
                act.wait_ge(max_done, i * SLOTS + q + 1)
                after(act, t_done, i * STEPS * KT + KT * (j - 1))
                act.activation(probs[j % 2][s][:], S[:, 0:M], ACT.Exp, bias=negmax[:, q:q + 1],
                               accum_out=den[:, q:q + 1]).then_inc(exp_done, 1)

            def o_up_(i, j):
                act.wait_ge(pv_done, i * STEPS * KT + KT * (j + 1))
                if j == 0:
                    after(act, bank_full[1], b_at(i - 1, "O3"))
                elif j == 3:
                    act.wait_ge(bank_full[1], b_at(i, "O2"))
                else:
                    act.wait_ge(bank_full[0], a_at(i, "O", j - 1))
                act.activation(OT[:], O[:, 0:P], ACT.Copy).then_inc(o_up, 1)

            def rest(i, slot):
                if slot == 9:
                    act.wait_ge(dve_up, dve_at(i, "Z"))
                    act.activation(ez[:], negz[:], ACT.Exp).then_inc(act_up, 1)
                    act.wait_ge(dve_up, dve_at(i, "EZ"))
                    act.activation(lz[:], ez1[:], ACT.Ln).then_inc(act_up, 1)
                for h, half, used in {10: [(0, 0, "U")], 11: [(0, 1, "S00"), (1, 0, "S01")],
                                      12: [(1, 1, "S10")]}.get(slot, []):
                    act.wait_ge(dve_up, dve_at(i, used))
                    for n in range(NS // 2):
                        m = half * (NS // 2) + n
                        ins = act.activation(abar[:, n, :], dt_[:, h, :], ACT.Exp, scale=A[:, h, m:m + 1])
                    ins.then_inc(act_up, 1)

            for c in range(4):
                k_up(0, 0, c)
                v_up(0, 0, V_OF_STEP[3][c])

            def body(i, cur, prev, nxt):
                for slot in range(SLOTS):
                    j, s, old, tiles, k, v = pieces(i, slot, cur, prev, nxt)
                    if slot % 4 == 0 and (prev if slot < 8 else cur):
                        o_up_(*((i - 1, 2), (i - 1, 3), (i, 0), (i, 1))[j])
                    if slot == 14 and prev:
                        act.wait_ge(dve_up, dve_at(i - 1, "LOGITS"))
                        act.activation(pr[:], W[:, 0:E], ACT.Exp, bias=st[:, 24:25], accum_out=st[:, 25:26])\
                           .then_inc(bank_free[1], 1)
                    for n, t in enumerate(tiles):
                        if (KT * old[1] + t) % 2 == 0:
                            turned(*old, t)
                        if n == 1 and k:
                            k_up(*k)
                        if n == 1 and cur:
                            soft(i, j, s)
                    if not tiles and k:
                        k_up(*k)
                    if not tiles and cur:
                        soft(i, j, s)
                    if v:
                        v_up(*v)
                    if prev:
                        rest(i - 1, slot)

            over_pairs(act, body)

        @block.vector
        def _(dve):
            def scale_of(link, rows, s0):
                link(dve.tensor_reduce(st[:, s0:s0 + 1], rows, AX.X, ALU.max, apply_absolute_value=True))
                link(dve.tensor_scalar(st[:, s0:s0 + 1], st[:, s0:s0 + 1], 1.0 / 127.0, 1e-8, ALU.mult, ALU.max))
                link(dve.reciprocal(st[:, s0 + 1:s0 + 2], st[:, s0:s0 + 1]))

            def quantise(link, out, rows, s0):
                scale_of(link, rows, s0)
                link(dve.tensor_scalar(out, rows, st[:, s0 + 1:s0 + 2], MAGIC, ALU.mult, ALU.add))
                link(dve.tensor_scalar(out, out, MAGIC, 127.0, ALU.subtract, ALU.min))
                return dve.tensor_scalar(out, out, -127.0, st[:, s0:s0 + 1], ALU.max, ALU.mult)

            def moments(link, x, s0, bn0):
                link.carried(dve.bn_stats(st[:, bn0:bn0 + 6], x))
                link(dve.bn_aggr(st[:, bn0 + 6:bn0 + 8], st[:, bn0:bn0 + 6]))
                return dve.tensor_scalar(st[:, s0:s0 + 1], st[:, bn0 + 7:bn0 + 8], EPS, None, ALU.add)

            dve.wait_ge(w_in, 16 * len(loads))
            link = Chain(dve, dve_w, 0, 22)
            for rows, wT in ((wq_rows, wqT), (wp_rows, wpT)):
                for k in range(DT):
                    ins = quantise(link, rows[:, k, :], rows[:, k, :], 28)
                    if k == 0:
                        link(ins)
                ins.then_inc(wq_set, 1)
                dve.wait_ge(w_mm, 1 if rows is wq_rows else 2)
                dve.tensor_copy(wT[:].rearrange("p k o -> p (k o)"), W[:]).then_inc(wq_set, 1)
            dve.wait_ge(wq_set, 4)

            def norm_q(i):
                link = Chain(dve, dve_q, i, 9, pause_q[:])
                dve.wait_ge(x_in, 16 * (i + 1))
                moments(link, x_q[:], 0, 32).then_inc(var_up, 1)
                dve.wait_ge(rstd_up, i + 1)
                link(dve.tensor_scalar(lnq[:], x_q[:], st[:, 38:39], st[:, 1:2], ALU.subtract, ALU.mult))
                quantise(link, lnq[:], lnq[:], 2).then_inc(lnq_up, 1)

            def split_q(i):
                link = Chain(dve, dve_q2, i, 2)
                dve.wait_ge(bank_full[0], a_at(i, "XQ"))
                dve.tensor_copy(xqT[:].rearrange("p k t -> p (k t)"), W[:, 0:D]).then_inc(bank_free[0], 1)
                dve.wait_ge(bank_full[0], a_at(i, "Q"))
                after(dve, q_up, i * 2 * STEPS)
                link(dve.tensor_scalar(q_f[:, 0, :], W[:, 0:P], cols[:, BQ, 0:1], DH ** -0.5, ALU.add, ALU.mult))
                dve.tensor_scalar(q_f[:, 1, :], W[:, P:2 * P], cols[:, BQ, 1:2], DH ** -0.5, ALU.add, ALU.mult)\
                   .then_inc(bank_free[0], 1)
                dve.wait_ge(bank_free[0], a_at(i, "Q"))
                link(dve.tensor_copy(q_hi[:].bitcast(F32R), q_f[:]))
                dve.tensor_tensor(q_lo[:], q_f[:], q_hi[:], ALU.subtract).then_inc(q_split, 1)
                link.end()

            def k_low(i, j, c):
                g = j % 2
                c0, cn = CHUNKS[c]
                dve.wait_ge(k_hi_up, (i * STEPS + j) * STRIPS + c + 1)
                dve.scalar_tensor_tensor(K_lo[j % 2][:, c0:c0 + cn], W[:, 0:cn], cols[:, BK, g:g + 1],
                                         K_hi[j % 2][:, c0:c0 + cn].bitcast(F32), ALU.add, ALU.subtract)\
                   .then_inc(bank_free[0], 1)

            def strip_max(i, j, s):
                q = STRIPS * j + s
                dve.wait_ge(s_done, i * SLOTS + q + 1)
                dve.tensor_reduce(negmax[:, q:q + 1], S[:, 0:M], AX.X, ALU.max, negate=True).then_inc(max_done, 1)

            def turned(i, j, t):
                n = KT * j + t
                dve.wait_ge(t_done, i * STEPS * KT + n + 1)
                after(dve, pv_done, i * STEPS * KT + n - 1)
                dve.tensor_copy(probsT[n % 2][0:keys_in(t), :], PT[1][0:keys_in(t), :]).then_inc(t_up[1], 1)

            def norm_o(i, j):
                b, g = divmod(j, 2)
                link = Chain(dve, dve_o, i * STEPS + j, 1)
                part, value = (0, a_at(i, "O", j)) if j < 2 else (1, b_at(i, f"O{j}"))
                rd = rden[:, STRIPS * j:STRIPS * (j + 1)]
                dve.wait_ge(exp_done, i * SLOTS + STRIPS * (j + 1))
                link(dve.reciprocal(rd, den[:, STRIPS * j:STRIPS * (j + 1)]))
                dve.wait_ge(bank_full[part], value)
                for h in range(2):
                    rows = slice(h * N, (h + 1) * N)
                    ins = dve.tensor_tensor(
                        o_tok[b * N:(b + 1) * N, g * P:(g + 1) * P].rearrange("n (s h d) -> n s h d", h=2, d=DH)[:, :, h, :],
                        W[rows, 0:P].rearrange("n (s h d) -> n s h d", h=2, d=DH)[:, :, h, :],
                        rd[rows, :].unsqueeze(2).to_broadcast([N, STRIPS, DH]), ALU.mult)
                ins.then_inc(bank_free[part], 1)
                link.end()

            def copy_out(i, name, dst, src):
                dve.wait_ge(bank_full[1], b_at(i, name))
                dve.tensor_copy(dst, src).then_inc(bank_free[1], 1)

            def empty(i, slot, link):
                if slot == 5:
                    copy_out(i, "oqT", oqT[:].rearrange("p k t -> p (k t)"), W[:, 0:D])
                if slot == 6:
                    dve.wait_ge(xr_in, 16 * (i + 1))
                    link(dve.tensor_tensor(x_res[:], x_res[:], bp_row[:], ALU.add))
                    dve.wait_ge(bank_full[1], b_at(i, "proj"))
                    dve.tensor_tensor(x2[:], W[:, 0:D], x_res[:], ALU.add).then_inc(bank_free[1], 1)
                if slot == 7:
                    copy_out(i, "ln2T", ln2T[:].rearrange("p k t -> p (k t)"), W[:, 0:D])
                if slot == 8:
                    after(dve, bc_out, 16 * i)
                    dve.wait_ge(bank_full[1], b_at(i, "xp"))
                    link(dve.tensor_copy(dlT[:], W[:, 0:P]))
                    dve.tensor_copy(BCT[:], W[0:2 * NS, P:2 * P]).then_inc(bank_free[1], 1)
                if slot == 9:
                    dve.wait_ge(bank_full[1], b_at(i, "dt"))
                    link(dve.tensor_scalar(z[:, 0, :], W[:, 0:P], cols[:, DTB, 0:1], None, ALU.add))
                    dve.tensor_scalar(z[:, 1, :], W[:, P:2 * P], cols[:, DTB, 1:2], None, ALU.add).then_inc(bank_free[1], 1)
                if slot == 13:
                    after(dve, x3_out, 32 * i)
                    dve.wait_ge(bank_full[1], b_at(i, "yT"))
                    dve.tensor_tensor(x3[:], W[:, 0:D], x2[:], ALU.add).then_inc(bank_free[1], 1)
                if slot == 14:
                    copy_out(i, "ln3T", ln3T[:].rearrange("p k t -> p (k t)"), W[:, 0:D])
                    dve.wait_ge(bank_full[1], b_at(i, "logits"))
                    dve.tensor_reduce(st[:, 24:25], W[:, 0:E], AX.X, ALU.max, negate=True).then_inc(dve_up, 1)
                if slot == 15:
                    dve.wait_ge(bank_full[1], b_at(i, "pos"))
                    link(dve.tensor_tensor(slotv[:], W[:, 0:E], base_e[:], ALU.add))
                    dve.tensor_tensor(base_e[:], W[:, E:2 * E], base_e[:], ALU.add).then_inc(bank_free[1], 1)

            def rest(i, slot, link):
                def up(ins):
                    ins.then_inc(dve_up, 1)

                if slot == 4:
                    dve.wait_ge(bank_free[1], b_at(i, "O3"))
                    link(dve.tensor_tensor(oq[:], o_tok[:], bv_row[:], ALU.add))
                    up(quantise(link, oq[:], oq[:], 4))
                if slot == 6:
                    dve.wait_ge(bank_free[1], b_at(i, "proj"))
                    up(dve.bn_stats(st[:, 40:46], x2[:]))
                    dve.wait_ge(dve_up, dve_at(i, "X2"))
                    link.carried()
                    link(dve.bn_aggr(st[:, 46:48], st[:, 40:46]))
                    up(dve.tensor_scalar(st[:, 8:9], st[:, 47:48], EPS, None, ALU.add))
                    dve.wait_ge(pool_up, pool_at(i, "R2"))
                    up(dve.tensor_scalar(ln2[:], x2[:], st[:, 46:47], st[:, 9:10], ALU.subtract, ALU.mult))
                if slot == 9:
                    dve.wait_ge(bank_free[1], b_at(i, "dt"))
                    up(dve.scalar_tensor_tensor(negz[:], z[:], -1.0, z[:], ALU.mult, ALU.min))
                    dve.wait_ge(act_up, act_at(i, "EXPZ"))
                    up(dve.tensor_scalar(ez1[:], ez[:], 1.0, None, ALU.add))
                    dve.wait_ge(dve_up, dve_at(i, "EZ"))
                    link(dve.tensor_scalar(negz[:], ez1[:], 1.0, LN_TINY, ALU.subtract, ALU.add))
                    link(dve.reciprocal(negz[:], negz[:]))
                    link(dve.tensor_tensor(negz[:], negz[:], ez[:], ALU.mult))
                    dve.wait_ge(act_up, act_at(i, "LNZ"))
                    link(dve.scalar_tensor_tensor(negz[:], lz[:], LN_TINY, negz[:], ALU.add, ALU.mult))
                    link(dve.scalar_tensor_tensor(dt_[:], z[:], 0.0, negz[:], ALU.max, ALU.add))
                    up(dve.tensor_tensor(u[:], dt_[:], ln2T[:], ALU.mult))
                for h, half in {10: [(0, 0)], 11: [(0, 1)], 12: [(1, 0), (1, 1)]}.get(slot, []):
                    dve.wait_ge(act_up, act_at(i, f"AB{h}{half}"))
                    link(dve.memset(abar[:].rearrange("p n (b t) -> p n b t", b=2)[:, :, :, 0:1], 0.0))
                    dve.wait_ge(pool_up, pool_at(i, f"BX{h}"))
                    flat = bx[:, half * (NS // 2):(half + 1) * (NS // 2), :].rearrange("p n t -> p (n t)")
                    up(dve.tensor_tensor_scan(flat, abar[:].rearrange("p n t -> p (n t)"), flat, 0.0,
                                              ALU.mult, ALU.add))
                if slot in (11, 12):
                    h = slot - 11
                    dve.wait_ge(dve_up, dve_at(i, f"S{h}1"))
                    link(dve.tensor_tensor(bx[:], bx[:], BC[:, NS:2 * NS, :], ALU.mult))
                    link(dve.tensor_reduce(y[:, h, :], bx[:].rearrange("p n t -> p t n"), AX.X, ALU.add))
                    up(dve.scalar_tensor_tensor(y[:, h, :], ln2T[:, h, :], cols[:, DP, h:h + 1], y[:, h, :],
                                                ALU.mult, ALU.add))
                if slot == 13:
                    dve.wait_ge(bank_free[1], b_at(i, "yT"))
                    up(moments(link, x3[:], 16, 48))
                    dve.wait_ge(pool_up, pool_at(i, "R3"))
                    up(dve.tensor_scalar(ln3[:], x3[:], st[:, 54:55], st[:, 17:18], ALU.subtract, ALU.mult))
                if slot == 14:
                    dve.wait_ge(bank_free[1], b_at(i, "logits"))
                    link(dve.reciprocal(st[:, 26:27], st[:, 25:26]))
                    link.carried(dve.tensor_scalar(pr[:], pr[:], st[:, 26:27], None, ALU.mult))
                    link.carried(dve.max(top[:], pr[:]))
                    link.carried(dve.max_index(topi[:], top[:], pr[:]))
                    link(dve.match_replace(pr2[:], top[:], pr[:], -1.0))
                    up(dve.tensor_scalar(sel[:], pr2[:], 0.0, None, ALU.is_lt))
                if slot == 15:
                    idx, slot_, pos, ok, low, out_ = (topf[:, n, :] for n in range(6))
                    link(dve.tensor_copy(idx, topi[:]))
                    for t in range(TOPK):
                        ins = dve.scalar_tensor_tensor(junk[:], iota_e[:], idx[:, t:t + 1], slotv[:], ALU.is_equal,
                                                       ALU.mult, accum_out=slot_[:, t:t + 1])
                        link(ins)
                    link(dve.scalar_tensor_tensor(pos, idx, -float(CAP), slot_, ALU.mult, ALU.add))
                    link(dve.tensor_scalar(ok, pos, float(CAP), None, ALU.is_lt))
                    link(dve.tensor_tensor(scores_all[:, bass.ds(i * TOPK, TOPK)], top[:], ok, ALU.mult))
                    link(dve.tensor_scalar(low, pos, float(CAP - 1), None, ALU.min))
                    link(dve.scalar_tensor_tensor(low, idx, float(CAP), low, ALU.mult, ALU.add))
                    link(dve.tensor_copy(slots_all[:, bass.ds(i * TOPK, TOPK)], low))
                    link(dve.tensor_scalar(out_, ok, -float(2 * E * CAP), float(2 * E * CAP), ALU.mult, ALU.add))
                    link(dve.tensor_tensor(out_, out_, slot_, ALU.add))
                    after(dve, scattered, 16 * TOPK * i)
                    up(dve.tensor_copy(sc_idx[:], out_))

            norm_q(0)
            split_q(0)
            for c in range(4):
                k_low(0, 0, c)

            def body(i, cur, prev, nxt):
                link = Chain(dve, dve_b, i - 1, B_LINKS, pause[:])
                for slot in range(SLOTS):
                    j, s, old, tiles, k, v = pieces(i, slot, cur, prev, nxt)
                    if slot == 1 and prev:
                        norm_o(i - 1, 2)
                    if slot == 4 and prev:
                        norm_o(i - 1, 3)
                    if slot in (8, 12) and cur:
                        norm_o(i, j - 2)
                    if slot == 12 and cur and nxt:
                        split_q(i + 1)
                    if prev:
                        empty(i - 1, slot, link)
                    if cur:
                        strip_max(i, j, s)
                    for n, t in enumerate(tiles):
                        if (KT * old[1] + t) % 2 == 1:
                            turned(*old, t)
                        if n == 1 and k:
                            k_low(*k)
                    if not tiles and k:
                        k_low(*k)
                    if prev:
                        rest(i - 1, slot, link)
                    if slot == 10 and cur and nxt:
                        norm_q(i + 1)
                if prev:
                    link.end()

            over_pairs(dve, body)


def expert_phase(nc, io, dram):
    with ExitStack() as ctx:
        def sb(name, shape, dt=F32):
            return ctx.enter_context(nc.sbuf_tensor("sb_" + name, shape, dt))

        def sem(name):
            return ctx.enter_context(nc.semaphore(name))

        ident = sb("ident2", [P, P])
        pause = sb("pause2", [P, 1])
        table = sb("table_sb", [E, CAP])
        idx_all = sb("idx_all", [P, E * CT], U32)
        idx = [sb(f"idx{n}", [P, CT], U32) for n in range(2)]
        xg = [[sb(f"xg{n}_{c}", [P, D]) for c in range(CT)] for n in range(2)]
        xT = [sb(f"xT{n}", [P, DT, CAP]) for n in range(2)]
        wgu = [sb(f"wgu{n}", [P, DT, 2 * FF]) for n in range(2)]
        wd = [sb(f"wd{n}", [FF, D]) for n in range(2)]
        sg = sb("sg", [FF, CAP])
        hid = [sb(f"hid{n}", [FF, CAP]) for n in range(2)]
        ys = [sb(f"ys{n}", [P, CT, D]) for n in range(2)]
        XT = [ctx.enter_context(nc.psum_tensor(f"XT{k}", [P, CAP], F32)) for k in range(DT)]
        G = ctx.enter_context(nc.psum_tensor("G", [P, CAP], F32))
        U = ctx.enter_context(nc.psum_tensor("U", [P, CAP], F32))
        Y = [ctx.enter_context(nc.psum_tensor(f"Y{k}", [P, 2, D], F32)) for k in range(2)]

        e_const = sem("e_const")
        tab_in = sem("tab_in")
        tab_t = sem("tab_t")
        tab_up = sem("tab_up")
        w_in = [sem(f"ew_in{n}") for n in range(2)]
        idx_up = sem("idx_up")
        x_in = [sem(f"ex_in{n}") for n in range(2)]
        xt_done = sem("xt_done")
        xt_up = [sem("xt_up_act"), sem("xt_up_dve")]
        gu_done = sem("gu_done")
        sg_up = sem("sg_up")
        hid_up = sem("hid_up")
        y_done = sem("y_done")
        y_up = [sem("y_up_act"), sem("y_up_dve")]
        y_out = [sem(f"y_out{n}") for n in range(2)]
        block = ctx.enter_context(nc.Block())

        def over_experts(eng, body):
            for e in range(2):
                body(e, e)
            with eng.Fori(1, E // 2 - 1) as two:
                for n in range(2):
                    body(2 * two + n, n)
            for e in range(E - 2, E):
                body(e, e % 2)

        def x_count(e, n):
            return (e - n) * (16 * CT // 2) + 16 * CT

        def w_count(e, n):
            return (e - n) * 16 + 32

        @block.sync
        def _(sp):
            sp.dma_start(table[:], dram["table"].rearrange("(e c) o -> e (c o)", e=E)).then_inc(tab_in, 16)

            def body(e, n):
                after(sp, gu_done, e - 1)
                sp.dma_start(wgu[n][:], io["wgu"][bass.ds(e, 1)].rearrange("o (k p) f -> p (o k) f", p=P)).then_inc(w_in[n], 16)
                after(sp, y_done, e - 1)
                sp.dma_start(wd[n][:], io["wdT"][bass.ds(e, 1)].rearrange("o f d -> (o f) d")).then_inc(w_in[n], 16)
                if isinstance(e, int) and e == 0:
                    return
                store(e - 1, 1 - n)

            def store(e, n):
                for m in range(2):
                    sp.wait_ge(y_up[m], e + 1)
                sp.dma_start(dram["y"][bass.ds(e * CAP, CAP), :].rearrange("(c p) d -> p c d", p=P), ys[n][:]).then_inc(y_out[n], 16)

            over_experts(sp, body)
            store(E - 1, (E - 1) % 2)
            for n in range(2):
                sp.wait_ge(y_out[n], 16 * (E // 2))

        @block.gpsimd
        def _(pool):
            pool.memset(ident[:], 0.0).then_inc(e_const, 1)
            pool.wait_ge(e_const, 1)
            pool.affine_select(out=ident[:], in_=ident[:], compare_op=ALU.not_equal, fill=1.0, base=0,
                               pattern=[[-1, P]], channel_multiplier=1).then_inc(e_const, 1)
            pool.wait_ge(tab_up, 1)

            def body(e, n):
                if not (isinstance(e, int) and e < 2):
                    pool.wait_ge(x_in[n], x_count(e, n) - 16 * CT)
                    pool.wait_ge(xt_done, e - 1)
                after(pool, idx_up, 2 * e)
                pool.tensor_copy(idx[n][:], idx_all[:, bass.ds(e * CT, CT)]).then_inc(idx_up, 1)
                pool.wait_ge(idx_up, 2 * e + 1)
                pool.tensor_tensor(pause[:], ident[:, 0:1], ident[:, 0:1], ALU.add).then_inc(idx_up, 1)
                for c in range(CT):
                    pool.indirect_dma_start(xg[n][c][:], None, dram["ln3"],
                                            bass.IndirectOffsetOnAxis(ap=idx[n][:, c:c + 1], axis=0)).then_inc(x_in[n], 16)

            over_experts(pool, body)

        @block.tensor
        def _(pe):
            def turn(e, n):
                pe.wait_ge(x_in[n], x_count(e, n))
                for m in range(2):
                    after(pe, xt_up[m], e)
                for k in range(DT):
                    for c in range(CT):
                        ins = pe.transpose(XT[k][:, c * P:(c + 1) * P], xg[n][c][:, k * P:(k + 1) * P], ident[:])
                ins.then_inc(xt_done, 1)

            pe.wait_ge(e_const, 2)
            pe.wait_ge(tab_in, 16)
            for c in range(CT):
                ins = pe.transpose(Y[0][:, 0, c * E:(c + 1) * E], table[:, c * P:(c + 1) * P], ident[0:E, 0:E])
            ins.then_inc(tab_t, 1)
            turn(0, 0)

            def body(e, n):
                pe.wait_ge(w_in[n], w_count(e, n))
                for m in range(2):
                    pe.wait_ge(xt_up[m], e + 1)
                after(pe, hid_up, e)
                for m, dst in enumerate((G, U)):
                    for k in range(DT):
                        ins = pe.matmul(dst[0:FF, :], wgu[n][:, k, m * FF:(m + 1) * FF], xT[n][:, k, :],
                                        start=(k == 0), stop=(k == DT - 1))
                ins.then_inc(gu_done, 1)
                if not (isinstance(e, int) and e == E - 1):
                    turn(e + 1, 1 - n)
                pe.wait_ge(hid_up, e + 1)
                for m in range(2):
                    after(pe, y_up[m], e)
                for c in range(CT):
                    ins = pe.matmul(Y[c // 2][:, c % 2, :], hid[n][:, c * P:(c + 1) * P], wd[n][:], start=True, stop=True)
                ins.then_inc(y_done, 1)

            over_experts(pe, body)

        @block.scalar
        def _(act):
            def body(e, n):
                if n == 0 and isinstance(e, int) and e == 0:
                    turned(0, 0)
                act.wait_ge(gu_done, e + 1)
                act.activation(sg[:], G[0:FF, :], ACT.Silu).then_inc(sg_up, 1)
                if not (isinstance(e, int) and e == E - 1):
                    turned(e + 1, 1 - n)
                act.wait_ge(y_done, e + 1)
                if not (isinstance(e, int) and e < 2):
                    act.wait_ge(y_out[n], (e - n) * 8)
                act.activation(ys[n][:, 0:2, :], Y[0][:], ACT.Copy).then_inc(y_up[0], 1)

            def turned(e, n):
                act.wait_ge(xt_done, e + 1)
                after(act, gu_done, e - 1)
                act.activation(xT[n][:, 0, :], XT[0][:], ACT.Copy).then_inc(xt_up[0], 1)

            over_experts(act, body)

        @block.vector
        def _(dve):
            dve.wait_ge(tab_t, 1)
            dve.tensor_copy(idx_all[:].rearrange("p (e c) -> p c e", c=CT),
                            Y[0][:, 0, 0:CT * E].rearrange("p (c e) -> p c e", c=CT)).then_inc(tab_up, 1)

            def turned(e, n):
                dve.wait_ge(xt_done, e + 1)
                after(dve, gu_done, e - 1)
                dve.tensor_copy(xT[n][:, 1, :], XT[1][:]).then_inc(xt_up[1], 1)

            def body(e, n):
                if n == 0 and isinstance(e, int) and e == 0:
                    turned(0, 0)
                dve.wait_ge(gu_done, e + 1)
                dve.wait_ge(sg_up, e + 1)
                after(dve, y_done, e - 1)
                dve.tensor_tensor(hid[n][:], U[0:FF, :], sg[:], ALU.mult).then_inc(hid_up, 1)
                if not (isinstance(e, int) and e == E - 1):
                    turned(e + 1, 1 - n)
                dve.wait_ge(y_done, e + 1)
                if not (isinstance(e, int) and e < 2):
                    dve.wait_ge(y_out[n], (e - n) * 8)
                dve.tensor_copy(ys[n][:, 2:4, :], Y[1][:]).then_inc(y_up[1], 1)

            over_experts(dve, body)


def combine_phase(nc, io, dram, out):
    with ExitStack() as ctx:
        def sb(name, shape, dt=F32):
            return ctx.enter_context(nc.sbuf_tensor("sb_" + name, shape, dt))

        def sem(name):
            return ctx.enter_context(nc.semaphore(name))

        pause = sb("pause3", [P, 1])
        zeros = sb("zeros", [P, 1])
        acc = [sb(f"acc{n}", [P, D]) for n in range(2)]
        yg = [[sb(f"yg{n}_{t}", [P, D]) for t in range(TOPK)] for n in range(2)]
        idx = [sb(f"cidx{n}", [P, TOPK], U32) for n in range(2)]
        sc = [sb(f"csc{n}", [P, TOPK]) for n in range(2)]
        x_in = [sem(f"cx_in{n}") for n in range(2)]
        idx_up = sem("cidx_up")
        zero_up = sem("zero_up")
        y_in = [sem(f"cy_in{n}") for n in range(2)]
        sc_up = sem("csc_up")
        acc_up = sem("acc_up")
        o_out = [sem(f"o_out{n}") for n in range(2)]
        block = ctx.enter_context(nc.Block())

        def over_tiles(eng, body):
            for i in range(2):
                body(i, i)
            with eng.Fori(1, PAIRS // 2) as two:
                for n in range(2):
                    body(2 * two + n, n)

        @block.sync
        def _(sp):
            def load(i, n):
                if not (isinstance(i, int) and i < 2):
                    sp.wait_ge(o_out[n], (i - n) * 8)
                sp.dma_start(acc[n][:], dram["x3"][bass.ds(i * P, P), :]).then_inc(x_in[n], 16)

            def body(i, n):
                load(i, n)
                sp.wait_ge(acc_up, TOPK * (i + 1))
                sp.dma_start(out[bass.ds(i * P, P), :], acc[n][:]).then_inc(o_out[n], 16)

            over_tiles(sp, body)
            for n in range(2):
                sp.wait_ge(o_out[n], 16 * (PAIRS // 2))

        @block.gpsimd
        def _(pool):
            pool.memset(zeros[:], 0.0).then_inc(zero_up, 1)
            pool.wait_ge(zero_up, 1)

            def body(i, n):
                if not (isinstance(i, int) and i < 2):
                    pool.wait_ge(y_in[n], (i - n) * (8 * TOPK))
                    pool.wait_ge(acc_up, TOPK * (i - 1))
                after(pool, idx_up, 2 * i)
                pool.tensor_copy(idx[n][:], dram["slots_sb"][:, bass.ds(i * TOPK, TOPK)]).then_inc(idx_up, 1)
                pool.wait_ge(idx_up, 2 * i + 1)
                pool.tensor_tensor(pause[:], zeros[:], zeros[:], ALU.add).then_inc(idx_up, 1)
                for t in range(TOPK):
                    pool.indirect_dma_start(yg[n][t][:], None, dram["y"],
                                            bass.IndirectOffsetOnAxis(ap=idx[n][:, t:t + 1], axis=0)).then_inc(y_in[n], 16)

            over_tiles(pool, body)

        @block.vector
        def _(dve):
            def body(i, n):
                dve.tensor_copy(sc[n][:], dram["scores_sb"][:, bass.ds(i * TOPK, TOPK)]).then_inc(sc_up, 1)
                dve.wait_ge(sc_up, i + 1)
                dve.wait_ge(x_in[n], (i - n) * 8 + 16)
                dve.wait_ge(y_in[n], (i - n) * (8 * TOPK) + 16 * TOPK)
                for t in range(TOPK):
                    dve.scalar_tensor_tensor(acc[n][:], yg[n][t][:], sc[n][:, t:t + 1], acc[n][:], ALU.mult, ALU.add)\
                       .then_inc(acc_up, 1)
                    dve.wait_ge(acc_up, i * TOPK + t + 1)

            over_tiles(dve, body)


def perceiver(nc, ins, out):
    with ExitStack() as ctx:
        dram = {
            "bc": nc.dram_tensor("bc_scratch", (2 * NS, P), F32).ap(),
            "x3": nc.dram_tensor("x3_scratch", (TOK, D), F32).ap(),
            "ln3": nc.dram_tensor("ln3_scratch", (TOK, D), F32).ap(),
            "table": nc.dram_tensor("table_scratch", (E * CAP, 1), F32).ap(),
            "y": nc.dram_tensor("y_scratch", (E * CAP, D), F32).ap(),
            "slots_sb": ctx.enter_context(nc.sbuf_tensor("slots_all", [P, PAIRS * TOPK], U32)),
            "scores_sb": ctx.enter_context(nc.sbuf_tensor("scores_all", [P, PAIRS * TOPK], F32)),
        }
        mixer_phase(nc, ins, dram)
        expert_phase(nc, ins, dram)
        combine_phase(nc, ins, dram, out)


def laid_out(inputs):
    a = {k: np.asarray(v) for k, v in inputs.items()}

    def cols(v):
        return v.reshape(DT, P).T

    x = a["x"]
    return {
        "x": x.reshape(TOK, D),
        "ctxT": a["ctx_2048"].transpose(0, 2, 1),
        "wq": a["L0_xattn_wq"], "bq": cols(a["L0_xattn_bq"]),
        "wkvT": a["L0_xattn_wkv"].T,
        "bk": cols(a["L0_xattn_bkv"][:D]), "bv": a["L0_xattn_bkv"][D:],
        "wp": a["L0_xattn_wp"], "bp": a["L0_xattn_bp"],
        "xpT": a["L0_attn_x_proj_w"].T, "dpT": a["L0_attn_dt_proj_w"].T,
        "dtb": cols(a["L0_attn_dt_proj_b"]), "A_log": a["L0_attn_A_log"], "Dp": cols(a["L0_attn_D_param"]),
        "gateT": a["L0_ffn_gate_w"].T,
        "wgu": np.concatenate([a["L0_ffn_w_gate"].transpose(0, 2, 1), a["L0_ffn_w_up"].transpose(0, 2, 1)], axis=2),
        "wdT": a["L0_ffn_w_down"].transpose(0, 2, 1),
    }


def kernel(**inputs):
    import concourse.bacc as bacc
    from concourse.bass_utils import run_bass_kernel_spmd

    nc = bacc.Bacc("TRN2", target_bir_lowering=False, num_devices=1)
    arrays, ins = {}, {}
    for name, a in laid_out(inputs).items():
        a = np.ascontiguousarray(a)
        arrays[name] = a
        ins[name] = nc.dram_tensor(name, a.shape, mybir.dt.from_np(a.dtype), kind="ExternalInput").ap()
    out = nc.dram_tensor("out", (TOK, D), F32, kind="ExternalOutput").ap()
    perceiver(nc, ins, out)
    r = run_bass_kernel_spmd(nc, [arrays], core_ids=[0])
    return r.results[0]["out"].reshape(B, N, D)
```

```python
from contextlib import ExitStack

import numpy as np
import concourse.bass as bass
from concourse import mybir

F32 = mybir.dt.float32
F32R = mybir.dt.float32r
BF16 = mybir.dt.bfloat16
U32 = mybir.dt.uint32
ALU = mybir.AluOpType
ACT = mybir.ActivationFunctionType
AX = mybir.AxisListType

P = 128
B, N, D = 32, 64, 256
M = 1601
H, DH = 16, 16
DT = D // P
TOK = B * N
PAIRS = TOK // P
HG = 8
STRIPS = 4
MP = 1602
KT = (M + P - 1) // P
CHUNKS = [(c, min(512, M - c)) for c in range(0, M, 512)]
NS, R = 16, 128
E, TOPK, FF = 64, 8, 96
CAP = 2 * TOK * TOPK // E
CT = CAP // P
MAGIC = 12582912.0
EPS = 1e-5
LN_TINY = 1e-30

STEPS = 4
SLOTS = STEPS * STRIPS
PV_SPLIT = [0, 4, 7, 10, 13]
V_UNITS = [[t for t in (2 * u, 2 * u + 1) if t < KT] for u in range((KT + 1) // 2)]
V_OF_STEP = {0: [4, 5, 6], 1: [0, 1, 2, 3], 2: [4, 5, 6], 3: [0, 1, 2, 3]}



TURNED_BY = [(t - first) % 2 for first, end in zip(PV_SPLIT, PV_SPLIT[1:]) for t in range(first, end)]


def a_order():
    order = []
    for slot in range(SLOTS):
        j, s = divmod(slot, STRIPS)
        if slot == 12:
            order.append(("O", 1))
        if slot == 13:
            order.append(("XQ",))
        k = [("K", (j + 1) % STEPS, s)]
        v = [("V", 1 if j in (1, 2) else 0, V_OF_STEP[j][s])] if s < len(V_OF_STEP[j]) else []
        order += k if s == 3 else v
        if slot == 8:
            order.append(("O", 0))
        if slot == 13:
            order.append(("Q",))
        order += v if s == 3 else k
    return order


A_ORDER = a_order()
assert A_ORDER.index(("V", 0, 6)) < A_ORDER.index(("K", 1, 3)) and A_ORDER.index(("V", 1, 6)) < A_ORDER.index(("K", 3, 3))
AHEAD = A_ORDER[A_ORDER.index(("V", 0, 0)):]
B_ORDER = ["O2", "O3", "oqT", "proj", "ln2T", "xp", "dt", "yT", "ln3T", "logits", "pos"]
DVE_ORDER = ["OQ", "X2", "V2", "LN2", "Z", "EZ", "U", "S00", "S01", "Y0", "S10", "S11", "Y1", "V3", "LN3", "LOGITS", "SEL", "ROUTE"]
ACT_ORDER = ["EXPZ", "LNZ", "AB00", "AB01", "AB10", "AB11"]
POOL_ORDER = ["R2", "BX0", "BX1", "R3"]


B_LINKS = 55


def a_at(i, *name):
    return len(AHEAD) + (i - (name in AHEAD)) * len(A_ORDER) + A_ORDER.index(name) + 1


def in_order(order):
    def at(i, name):
        return i * len(order) + order.index(name) + 1
    return at


b_at, dve_at, act_at, pool_at = (in_order(o) for o in (B_ORDER, DVE_ORDER, ACT_ORDER, POOL_ORDER))


def up_at(i, j, t):
    e = TURNED_BY[t]
    per = TURNED_BY.count(e)
    return e, (i * STEPS + j) * per + TURNED_BY[:t + 1].count(e)


def two_before(i, j, t):
    return (i, j, t - 2) if t >= 2 else (i, j - 1, KT - 2 + t) if j else (i - 1, STEPS - 1, KT - 2 + t)


def keys_in(t):
    return min(P, M - t * P)


def after(eng, sem, value):
    if isinstance(value, int) and value <= 0:
        return
    eng.wait_ge(sem, value)


class Chain:

    def __init__(self, eng, sem, turn, per, pause=None):
        self.eng, self.sem, self.base, self.per, self.n, self.pause = eng, sem, turn * per, per, 0, pause

    def __call__(self, ins):
        self.n += 1
        ins.then_inc(self.sem, 1)
        self.eng.wait_ge(self.sem, self.base + self.n)

    def carried(self, ins=None):
        if ins is not None:
            self(ins)
        self.n += 1
        self.eng.memset(self.pause, 0.0).then_inc(self.sem, 1)

    def end(self):
        assert self.n == self.per, self.n


def over_pairs(eng, body):
    body(0, True, False, True)
    body(1, True, True, True)
    with eng.Fori(2, PAIRS - 1) as i:
        body(i, True, True, True)
    body(PAIRS - 1, True, True, False)
    body(PAIRS, False, True, False)


def pieces(i, slot, cur, prev, nxt):
    j, s = divmod(slot, STRIPS)
    old = (i - 1, 3) if j == 0 else (i, j - 1)
    tiles = list(range(PV_SPLIT[s], PV_SPLIT[s + 1])) if (prev if j == 0 else cur) else []
    k = v = None
    if cur and (j < 3 or nxt):
        k = (i, j + 1, s) if j < 3 else (i + 1, 0, s)
        if s < len(V_OF_STEP[j]):
            v = {0: (i, 0), 1: (i, 1), 2: (i, 1), 3: (i + 1, 0)}[j] + (V_OF_STEP[j][s],)
    return j, s, old, tiles, k, v


def left_over(i, slot, cur, prev, nxt):
    if slot == 0:
        return None, ((i, 0, V_OF_STEP[3][3]) if cur else None)
    j, s, old, tiles, k, v = pieces(i, slot - 1, cur, prev, nxt)
    return (None, v) if s == 3 else (k, None)


def mixer_phase(nc, io, dram):
    with ExitStack() as ctx:
        def sb(name, shape, dt=F32):
            return ctx.enter_context(nc.sbuf_tensor("sb_" + name, shape, dt))

        def sem(name):
            return ctx.enter_context(nc.semaphore(name))

        wqT = sb("wqT", [P, DT, D])
        wpT = sb("wpT", [P, DT, D])
        wkvT = sb("wkvT", [P, DT, 2 * D])
        xpT = sb("xpT", [P, DT, R + 2 * NS])
        dpT = sb("dpT", [P, D])
        gateT = sb("gateT", [P, DT, E])
        cols = sb("cols", [P, 4, DT])
        bv_row = sb("bv_row", [P, D])
        bp_row = sb("bp_row", [P, D])
        A = sb("A", [P, DT, NS])
        ident = sb("ident", [P, P])
        headmask = sb("headmask", [P, HG])
        before = sb("before", [P, P], BF16)
        ones = sb("ones", [P, P], BF16)
        iota_e = sb("iota_e", [P, E])
        tokid = sb("tokid", [P, 1])
        tile_rows = sb("tile_rows", [P, 1])
        pause, pause_q, pause_p = (sb(n, [P, 1]) for n in ("pause", "pause_q", "pause_p"))
        neg_half = sb("neg_half", [P, 1])
        ctxT = [sb(f"ctxT{n}", [P, DT, M]) for n in range(2)]
        K_hi = [sb(f"K_hi{n}", [P, MP], F32R) for n in range(2)]
        K_lo = [sb(f"K_lo{n}", [P, MP], F32R) for n in range(2)]
        V = [sb(f"V{n}", [P, KT, D]) for n in range(2)]
        Q_hi = [sb(f"Q_hi{n}", [P, HG, N], F32R) for n in range(2)]
        Q_lo = [sb(f"Q_lo{n}", [P, HG, N], F32R) for n in range(2)]
        probs = [[sb(f"probs{n}_{s}", [P, M]) for s in range(STRIPS)] for n in range(2)]
        probsT = [sb(f"probsT{n}", [P, STRIPS * P]) for n in range(2)]
        negmax = sb("negmax", [P, STEPS * STRIPS])
        den = sb("den", [P, STEPS * STRIPS])
        rden = sb("rden", [P, STEPS * STRIPS])
        OT = sb("OT", [P, P])
        x_q = sb("x_q", [P, D])
        lnq = sb("lnq", [P, D])
        oq = sb("oq", [P, D])
        xqT = sb("xqT", [P, DT, P])
        q_f = sb("q_f", [P, DT, P])
        q_hi = sb("q_hi", [P, DT, P])
        q_lo = sb("q_lo", [P, DT, P])
        st = sb("st", [P, 64])
        o_tok = sb("o_tok", [P, D])
        x_res = sb("x_res", [P, D])
        x2 = sb("x2", [P, D])
        ln2 = sb("ln2", [P, D])
        ln2T = sb("ln2T", [P, DT, P])
        oqT = sb("oqT", [P, DT, P])
        dlT = sb("dlT", [P, P])
        BCT = sb("BCT", [2 * NS, P])
        BC = sb("BC", [P, 2 * NS, P])
        z = sb("z", [P, DT, P])
        soft_ = sb("soft", [P, 4, DT, P])
        negz, ez, ez1, lz = (soft_[:, n] for n in range(4))
        dt_ = sb("dt_", [P, DT, P])
        u = sb("u", [P, DT, P])
        abar = [sb("abar", [P, NS // 2, P])[:], soft_[:].rearrange("p a h t -> p (a h) t")]
        bx = sb("bx", [P, NS, P])
        wq_rows, wp_rows = (bx[:, n:n + 4, :].rearrange("p (k a) b -> p k (a b)", k=DT) for n in (4, 8))
        y = z
        x3 = sb("x3", [P, D])
        ln3 = sb("ln3", [P, D])
        ln3T = oqT
        pr = sb("pr", [P, E])
        pr2 = sb("pr2", [P, E])
        sel = sb("sel", [P, E], BF16)
        slotv = sb("slotv", [P, E])
        base_e = sb("base_e", [P, E])
        top = sb("top", [P, TOPK])
        topi = sb("topi", [P, TOPK], U32)
        topf = sb("topf", [P, 6, TOPK])
        junk = sb("junk", [P, E])
        sc_idx = sb("sc_idx", [P, TOPK], U32)
        slots_all, scores_all = dram["slots_sb"], dram["scores_sb"]

        S = ctx.enter_context(nc.psum_tensor("S", [P, 2048], F32))
        PT = [ctx.enter_context(nc.psum_tensor(f"PT{n}", [P, 512], F32)) for n in range(2)]
        O = ctx.enter_context(nc.psum_tensor("O", [P, 512], F32))
        W = ctx.enter_context(nc.psum_tensor("W", [P, 512], F32))

        w_in = sem("w_in")
        consts = sem("consts")
        wq_set = sem("w_set")
        a_set = sem("a_set")
        w_mm = sem("w_mm")
        table_zero = sem("table_zero")
        ctx_in = [sem(f"ctx_in{n}") for n in range(2)]
        x_in = sem("x_in")
        xr_in = sem("xr_in")
        bank_full = [sem("bank_full_a"), sem("bank_full_b")]
        bank_free = [sem("bank_free_a"), sem("bank_free_b")]
        k_hi_up = sem("k_hi_up")
        var_up = sem("var_up")
        rstd_up = sem("rstd_up")
        lnq_up = sem("lnq_up")
        q_split = sem("q_split")
        q_up = sem("q_up")
        s_done = sem("s_done")
        max_done = sem("max_done")
        exp_done = sem("exp_done")
        t_done = sem("t_done")
        t_up = [sem("t_up_act"), sem("t_up_dve")]
        pv_done = sem("pv_done")
        o_up = sem("o_up")
        dve_up = sem("dve_up")
        act_up = sem("act_up")
        pool_up = sem("pool_up")
        bc_out = sem("bc_out")
        bc_in = sem("bc_in")
        x3_out = sem("x3_out")
        scattered = sem("scattered")
        tokid_up = sem("tokid_up")
        dve_w, dve_q, dve_q2, dve_o, dve_b = (sem(f"dve_{n}") for n in ("w", "q", "q2", "o", "b"))
        block = ctx.enter_context(nc.Block())

        loads = (
            (wq_rows, io["wq"].rearrange("(k p) i -> p k i", p=P)),
            (wp_rows, io["wp"].rearrange("(k p) i -> p k i", p=P)),
            (wkvT[:], io["wkvT"].rearrange("(k p) o -> p k o", p=P)),
            (xpT[:], io["xpT"].rearrange("(k p) o -> p k o", p=P)),
            (dpT[:], io["dpT"]),
            (gateT[:], io["gateT"].rearrange("(k p) o -> p k o", p=P)),
            (cols[:, 0, :], io["bq"]), (cols[:, 1, :], io["bk"]),
            (cols[:, 2, :], io["dtb"]), (cols[:, 3, :], io["Dp"]),
            (bv_row[:], io["bv"].partition_broadcast(P)),
            (bp_row[:], io["bp"].partition_broadcast(P)),
            (A[:], io["A_log"].rearrange("(h p) n -> p h n", p=P)),
        )
        BQ, BK, DTB, DP = range(4)

        @block.sync
        def _(sp):
            def x_rows(i):
                return io["x"][bass.ds(i * P, P), :]

            def ctx_of(batch):
                return io["ctxT"][bass.ds(batch, 1)].rearrange("o (k p) m -> p (o k) m", p=P)

            for dst, src in loads:
                sp.dma_start(dst, src).then_inc(w_in, 16)
            sp.dma_start(x_q[:], x_rows(0)).then_inc(x_in, 16)
            for n in range(2):
                sp.dma_start(ctxT[n][:], ctx_of(n)).then_inc(ctx_in[n], 16)

            def body(i, cur, prev, nxt):
                if cur and nxt:
                    sp.wait_ge(lnq_up, i + 1)
                    sp.dma_start(x_q[:], x_rows(i + 1)).then_inc(x_in, 16)
                    sp.wait_ge(bank_full[0], a_at(i, "K", 1, 3))
                    sp.dma_start(ctxT[0][:], ctx_of(2 * i + 2)).then_inc(ctx_in[0], 16)
                if prev:
                    after(sp, dve_up, dve_at(i - 2, "Y1"))
                    sp.dma_start(x_res[:], x_rows(i - 1)).then_inc(xr_in, 16)
                    sp.wait_ge(bank_free[1], b_at(i - 1, "xp"))
                    sp.dma_start(dram["bc"], BCT[:]).then_inc(bc_out, 16)
                    sp.wait_ge(bc_out, i * 16)
                    sp.dma_start(BC[:].rearrange("p n t -> p (n t)"), dram["bc"].rearrange("n t -> (n t)").partition_broadcast(P)).then_inc(bc_in, 16)
                if cur and nxt:
                    sp.wait_ge(bank_full[0], a_at(i, "K", 3, 3))
                    sp.dma_start(ctxT[1][:], ctx_of(2 * i + 3)).then_inc(ctx_in[1], 16)
                if prev:
                    sp.wait_ge(dve_up, dve_at(i - 1, "LN3"))
                    sp.dma_start(dram["x3"][bass.ds((i - 1) * P, P), :], x3[:]).then_inc(x3_out, 16)
                    sp.dma_start(dram["ln3"][bass.ds((i - 1) * P, P), :], ln3[:]).then_inc(x3_out, 16)

            over_pairs(sp, body)
            sp.wait_ge(x3_out, 32 * PAIRS)

        @block.gpsimd
        def _(pool):
            pool.memset(ident[:], 0.0).then_inc(consts, 1)
            pool.memset(headmask[:], 1.0).then_inc(consts, 1)
            pool.memset(ones[:], 1.0).then_inc(consts, 1)
            pool.memset(neg_half[:], -0.5).then_inc(consts, 1)
            pool.memset(bx[:, 0:2, :], 0.0).then_inc(consts, 1)
            for n in range(2):
                pool.memset(K_hi[n][:, M:MP].bitcast(F32), 0.0).then_inc(consts, 1)
                pool.memset(K_lo[n][:, M:MP].bitcast(F32), 0.0).then_inc(consts, 1)
            pool.iota(iota_e[:], [[1, E]], base=0, channel_multiplier=0,
                      allow_small_or_imprecise_dtypes=True).then_inc(consts, 1)
            pool.iota(tokid[:], [[0, 1]], base=-P, channel_multiplier=1,
                      allow_small_or_imprecise_dtypes=True).then_inc(consts, 1)
            pool.iota(base_e[:], [[CAP, E]], base=0, channel_multiplier=0,
                      allow_small_or_imprecise_dtypes=True).then_inc(consts, 1)
            pool.memset(tile_rows[:], float(P)).then_inc(consts, 1)
            pool.wait_ge(consts, 13)
            pool.affine_select(out=ident[:], in_=ident[:], compare_op=ALU.not_equal, fill=1.0, base=0,
                               pattern=[[-1, P]], channel_multiplier=1).then_inc(consts, 1)
            pool.affine_select(out=headmask[:], in_=headmask[:], compare_op=ALU.is_ge, fill=0.0, base=0,
                               pattern=[[-DH, HG]], channel_multiplier=1).then_inc(consts, 1)
            pool.affine_select(out=before[:], in_=ones[:], compare_op=ALU.is_gt, fill=0.0, base=0,
                               pattern=[[1, P]], channel_multiplier=-1).then_inc(consts, 1)
            pool.dma_start(dram["table"].rearrange("(p c) o -> p (c o)", p=P),
                           bx[:, 0:2, :].rearrange("p a b -> p (a b)")).then_inc(table_zero, 16)
            pool.wait_ge(consts, 16)
            pool.affine_select(out=headmask[:], in_=headmask[:], compare_op=ALU.is_ge, fill=0.0, base=DH - 1,
                               pattern=[[DH, HG]], channel_multiplier=-1).then_inc(consts, 1)
            pool.wait_ge(consts, 17)
            pool.wait_ge(table_zero, 16)

            def rstd_q(i):
                pool.wait_ge(var_up, i + 1)
                pool.tensor_tensor(st[:, 1:2], st[:, 0:1], neg_half[:], ALU.pow).then_inc(rstd_up, 1)

            def spread_q(i, j):
                b, g = divmod(j, 2)
                pool.wait_ge(q_split, i + 1)
                after(pool, s_done, i * SLOTS + STRIPS * (j - 1))
                for dst, src in ((Q_hi[j % 2], q_hi), (Q_lo[j % 2], q_lo)):
                    pool.tensor_tensor(
                        dst[:], src[:, g, b * N:(b + 1) * N].unsqueeze(1).to_broadcast([P, HG, N]),
                        headmask[:].unsqueeze(2).to_broadcast([P, HG, N]), ALU.mult).then_inc(q_up, 1)

            def scan_input(i, h):
                pool.wait_ge(dve_up, dve_at(i, "U" if h == 0 else "Y0"))
                pool.wait_ge(bc_in, (i + 1) * 16)
                pool.tensor_tensor(bx[:], u[:, h, :].unsqueeze(1).to_broadcast([P, NS, P]),
                                   BC[:, 0:NS, :], ALU.mult).then_inc(pool_up, 1)

            rstd_q(0)
            spread_q(0, 0)

            def body(i, cur, prev, nxt):
                if cur:
                    spread_q(i, 1)
                    spread_q(i, 2)
                if prev:
                    pool.wait_ge(dve_up, dve_at(i - 1, "V2"))
                    pool.tensor_tensor(st[:, 9:10], st[:, 8:9], neg_half[:], ALU.pow).then_inc(pool_up, 1)
                if cur:
                    spread_q(i, 3)
                if prev:
                    scan_input(i - 1, 0)
                    scan_input(i - 1, 1)
                if cur and nxt:
                    rstd_q(i + 1)
                    spread_q(i + 1, 0)
                if prev:
                    pool.wait_ge(dve_up, dve_at(i - 1, "V3"))
                    pool.tensor_tensor(st[:, 17:18], st[:, 16:17], neg_half[:], ALU.pow).then_inc(pool_up, 1)
                    after(pool, scattered, 16 * TOPK * (i - 1))
                    pool.tensor_tensor(tokid[:], tokid[:], tile_rows[:], ALU.add).then_inc(tokid_up, 1)
                    pool.wait_ge(tokid_up, 2 * i - 1)
                    pool.wait_ge(dve_up, dve_at(i - 1, "ROUTE"))
                    pool.tensor_tensor(pause_p[:], tile_rows[:], tile_rows[:], ALU.add).then_inc(tokid_up, 1)
                    for t in range(TOPK):
                        pool.indirect_dma_start(
                            dram["table"], bass.IndirectOffsetOnAxis(ap=sc_idx[:, t:t + 1], axis=0),
                            tokid[:], None, bounds_check=E * CAP - 1, oob_is_err=False).then_inc(scattered, 16)

            over_pairs(pool, body)
            pool.wait_ge(scattered, 16 * TOPK * PAIRS)

        @block.tensor
        def _(pe):
            last = [None]

            def take(part, value):
                if last[0] is not None:
                    after(pe, *last[0])
                last[0] = (bank_free[part], value)

            pe.wait_ge(consts, 17)
            for n, rows in enumerate((wq_rows, wp_rows)):
                pe.wait_ge(wq_set, 2 * n + 1)
                for k in range(DT):
                    for o in range(DT):
                        ins = pe.transpose(W[:, (k * DT + o) * P:(k * DT + o + 1) * P],
                                           rows[:, o, k * P:(k + 1) * P], ident[:])
                ins.then_inc(w_mm, 1)
            pe.wait_ge(wq_set, 4)
            pe.wait_ge(w_in, 16 * len(loads))

            def turn_x(i):
                take(0, a_at(i, "XQ"))
                pe.wait_ge(lnq_up, i + 1)
                for k in range(DT):
                    ins = pe.transpose(W[:, k * P:(k + 1) * P], lnq[:, k * P:(k + 1) * P], ident[:])
                ins.then_inc(bank_full[0], 1)

            def q_mm(i):
                take(0, a_at(i, "Q"))
                pe.wait_ge(bank_free[0], a_at(i, "XQ"))
                for g in range(2):
                    for k in range(DT):
                        ins = pe.matmul(W[:, g * P:(g + 1) * P], wqT[:, k, g * P:(g + 1) * P], xqT[:, k, :],
                                        start=(k == 0), stop=(k == DT - 1))
                ins.then_inc(bank_full[0], 1)

            def k_mm(i, j, c):
                b, g = divmod(j, 2)
                c0, cn = CHUNKS[c]
                take(0, a_at(i, "K", j, c))
                pe.wait_ge(ctx_in[b], 16 * (i + 1))
                for k in range(DT):
                    ins = pe.matmul(W[:, 0:cn], wkvT[:, k, g * P:(g + 1) * P], ctxT[b][:, k, c0:c0 + cn],
                                    start=(k == 0), stop=(k == DT - 1))
                ins.then_inc(bank_full[0], 1)

            def v_mm(i, b, unit):
                take(0, a_at(i, "V", b, unit))
                pe.wait_ge(ctx_in[b], 16 * (i + 1))
                for n, t in enumerate(V_UNITS[unit]):
                    for k in range(DT):
                        ins = pe.matmul(W[0:keys_in(t), n * D:(n + 1) * D], ctxT[b][:, k, t * P:t * P + keys_in(t)],
                                        wkvT[:, k, D:2 * D], start=(k == 0), stop=(k == DT - 1))
                ins.then_inc(bank_full[0], 1)

            def scores(i, j, s):
                if s == 0:
                    pe.wait_ge(bank_free[0], a_at(i, "K", j, 3))
                    pe.wait_ge(q_up, i * 2 * STEPS + 2 * (j + 1))
                after(pe, exp_done, i * SLOTS + STRIPS * j + s)
                for c in range(0, M, 512):
                    cn = min(512, MP - c)
                    for n, (lhs, rhs) in enumerate(((Q_hi, K_hi), (Q_hi, K_lo), (Q_lo, K_hi))):
                        ins = pe.matmul(S[:, c:c + cn], lhs[j % 2][:, 2 * s:2 * s + 2, :].rearrange("p h n -> p (h n)"),
                                        rhs[j % 2][:, c:c + cn], start=(n == 0), stop=(n == 2))
                ins.then_inc(s_done, 1)

            def turn(i, j, t):
                n = KT * j + t
                pe.wait_ge(exp_done, i * SLOTS + STRIPS * (j + 1))
                e, count = up_at(*two_before(i, j, t))
                after(pe, t_up[e], count)
                for s in range(STRIPS):
                    ins = pe.transpose(PT[n % 2][0:keys_in(t), s * P:(s + 1) * P],
                                       probs[j % 2][s][:, t * P:t * P + keys_in(t)], ident[:])
                ins.then_inc(t_done, 1)

            def times_v(i, j, t):
                n = KT * j + t
                b, g = divmod(j, 2)
                e, count = up_at(i, j, t)
                pe.wait_ge(t_up[e], count)
                if t == 0:
                    after(pe, o_up, i * STEPS + j)
                    pe.wait_ge(bank_free[0], a_at(i, "V", b, 6))
                for s in range(STRIPS):
                    ins = pe.matmul(O[32 * s:32 * s + 32, 0:P],
                                    V[b][0:keys_in(t), t, g * P + 32 * s:g * P + 32 * s + 32],
                                    probsT[n % 2][0:keys_in(t), s * P:(s + 1) * P],
                                    start=(t == 0), stop=(t == KT - 1))
                ins.then_inc(pv_done, 1)

            def turn_o(i, j):
                part, value = (0, a_at(i, "O", j)) if j < 2 else (1, b_at(i, f"O{j}"))
                take(part, value)
                pe.wait_ge(o_up, i * STEPS + j + 1)
                pe.transpose(W[:, 0:P], OT[:], ident[:]).then_inc(bank_full[part], 1)

            def turn_two(i, name, src, ready, value):
                take(1, b_at(i, name))
                pe.wait_ge(ready, value)
                for k in range(DT):
                    ins = pe.transpose(W[:, k * P:(k + 1) * P], src(k), ident[:])
                ins.then_inc(bank_full[1], 1)

            def rest(i, slot, middle):
                at = (slot, middle)
                if at == (5, False):
                    turn_two(i, "oqT", lambda k: oq[:, k * P:(k + 1) * P], dve_up, dve_at(i, "OQ"))
                if at == (5, True):
                    take(1, b_at(i, "proj"))
                    pe.wait_ge(bank_free[1], b_at(i, "oqT"))
                    for k in range(DT):
                        ins = pe.matmul(W[:, 0:D], oqT[:, k, :], wpT[:, k, :], start=(k == 0), stop=(k == DT - 1))
                    ins.then_inc(bank_full[1], 1)
                if at == (6, False):
                    turn_two(i, "ln2T", lambda k: ln2[:, k * P:(k + 1) * P], dve_up, dve_at(i, "LN2"))
                if at == (6, True):
                    take(1, b_at(i, "xp"))
                    pe.wait_ge(bank_free[1], b_at(i, "ln2T"))
                    for k in range(DT):
                        pe.matmul(W[:, 0:P], xpT[:, k, 0:R], ln2T[:, k, :], start=(k == 0), stop=(k == DT - 1))
                    for k in range(DT):
                        ins = pe.matmul(W[0:2 * NS, P:2 * P], xpT[:, k, R:R + 2 * NS], ln2T[:, k, :],
                                        start=(k == 0), stop=(k == DT - 1))
                    ins.then_inc(bank_full[1], 1)
                if at == (7, False):
                    take(1, b_at(i, "dt"))
                    pe.wait_ge(bank_free[1], b_at(i, "xp"))
                    for h in range(DT):
                        ins = pe.matmul(W[:, h * P:(h + 1) * P], dpT[:, h * P:(h + 1) * P], dlT[:], start=True, stop=True)
                    ins.then_inc(bank_full[1], 1)
                if at == (13, False):
                    turn_two(i, "yT", lambda k: y[:, k, :], dve_up, dve_at(i, "Y1"))
                if at == (14, False):
                    turn_two(i, "ln3T", lambda k: ln3[:, k * P:(k + 1) * P], dve_up, dve_at(i, "LN3"))
                if at == (14, True):
                    take(1, b_at(i, "logits"))
                    pe.wait_ge(bank_free[1], b_at(i, "ln3T"))
                    for k in range(DT):
                        ins = pe.matmul(W[:, 0:E], ln3T[:, k, :], gateT[:, k, :], start=(k == 0), stop=(k == DT - 1))
                    ins.then_inc(bank_full[1], 1)
                if at == (15, False):
                    take(1, b_at(i, "pos"))
                    pe.wait_ge(dve_up, dve_at(i, "SEL"))
                    pe.matmul(W[:, 0:E], before[:], sel[:], start=True, stop=True)
                    pe.matmul(W[:, E:2 * E], ones[:], sel[:], start=True, stop=True).then_inc(bank_full[1], 1)

            for c in range(STRIPS):
                if c == 1:
                    turn_x(0)
                first, second = (v_mm, (0, 0, V_OF_STEP[3][c])), (k_mm, (0, 0, c))
                if c == 3:
                    first, second = second, first
                first[0](*first[1])
                if c == 1:
                    q_mm(0)
                second[0](*second[1])

            def body(i, cur, prev, nxt):
                last[0] = (bank_free[0], a_at(i, "V", 0, 3)) if cur else (bank_free[1], b_at(i - 2, "pos"))
                for slot in range(SLOTS):
                    j, s, old, tiles, k, v = pieces(i, slot, cur, prev, nxt)
                    if slot == 1 and prev:
                        turn_o(i - 1, 2)
                    if slot == 12 and cur:
                        turn_o(i, 1)
                    if slot == 13 and cur and nxt:
                        turn_x(i + 1)
                    if prev:
                        rest(i - 1, slot, False)
                    if cur:
                        scores(i, j, s)
                    for t in tiles[:2]:
                        turn(*old, t)
                    if k and s == 3:
                        k_mm(*k)
                    if v and s < 3:
                        v_mm(*v)
                    if slot == 8 and cur:
                        turn_o(i, 0)
                    if slot == 4 and prev:
                        turn_o(i - 1, 3)
                    if slot == 13 and cur and nxt:
                        q_mm(i + 1)
                    if prev:
                        rest(i - 1, slot, True)
                    for n, t in enumerate(tiles[:2]):
                        times_v(*old, t)
                        if tiles[n + 2:n + 3]:
                            turn(*old, tiles[n + 2])
                    if k and s < 3:
                        k_mm(*k)
                    if v and s == 3:
                        v_mm(*v)
                    for t in tiles[2:]:
                        times_v(*old, t)

            over_pairs(pe, body)

        @block.scalar
        def _(act):
            act.wait_ge(w_in, 16 * len(loads))
            act.activation(A[:], A[:], ACT.Exp).then_inc(a_set, 1)
            act.wait_ge(a_set, 1)
            act.mul(A[:], A[:], -1.0).then_inc(a_set, 1)
            act.wait_ge(a_set, 2)

            def k_up(i, j, c):
                g = j % 2
                c0, cn = CHUNKS[c]
                act.wait_ge(bank_full[0], a_at(i, "K", j, c))
                after(act, s_done, i * SLOTS + STRIPS * (j - 1))
                act.activation(K_hi[j % 2][:, c0:c0 + cn], W[:, 0:cn], ACT.Identity,
                               bias=cols[:, BK, g:g + 1]).then_inc(k_hi_up, 1)

            def turned(i, j, t):
                n = KT * j + t
                act.wait_ge(t_done, i * STEPS * KT + n + 1)
                after(act, pv_done, i * STEPS * KT + n - 1)
                act.activation(probsT[n % 2][0:keys_in(t), :], PT[n % 2][0:keys_in(t), :], ACT.Copy).then_inc(t_up[0], 1)

            def soft(i, j, s):
                q = STRIPS * j + s
                act.wait_ge(max_done, i * SLOTS + q + 1)
                after(act, t_done, i * STEPS * KT + KT * (j - 1))
                act.activation(probs[j % 2][s][:], S[:, 0:M], ACT.Exp, bias=negmax[:, q:q + 1],
                               accum_out=den[:, q:q + 1]).then_inc(exp_done, 1)

            def o_up_(i, j):
                act.wait_ge(pv_done, i * STEPS * KT + KT * (j + 1))
                if j == 0:
                    after(act, bank_full[1], b_at(i - 1, "O3"))
                elif j == 3:
                    act.wait_ge(bank_full[1], b_at(i, "O2"))
                else:
                    act.wait_ge(bank_full[0], a_at(i, "O", j - 1))
                act.activation(OT[:], O[:, 0:P], ACT.Copy).then_inc(o_up, 1)

            def rest(i, slot):
                if slot == 7:
                    act.wait_ge(dve_up, dve_at(i, "Z"))
                    act.activation(ez, negz, ACT.Exp).then_inc(act_up, 1)
                    act.wait_ge(dve_up, dve_at(i, "EZ"))
                    act.activation(lz, ez1, ACT.Ln).then_inc(act_up, 1)
                for h, half, used in {8: [(0, 0, "U"), (0, 1, "U")], 9: [(1, 0, "S00")],
                                      10: [(1, 1, "S01")]}.get(slot, []):
                    act.wait_ge(dve_up, dve_at(i, used))
                    for n in range(NS // 2):
                        m = half * (NS // 2) + n
                        ins = act.activation(abar[half][:, n, :], dt_[:, h, :], ACT.Exp, scale=A[:, h, m:m + 1])
                    ins.then_inc(act_up, 1)

            for c in range(4):
                k_up(0, 0, c)

            def body(i, cur, prev, nxt):
                for slot in range(SLOTS):
                    j, s, old, tiles, k, v = pieces(i, slot, cur, prev, nxt)
                    last_k, _ = left_over(i, slot, cur, prev, nxt)
                    if last_k:
                        k_up(*last_k)
                    if slot % 4 == 0 and (prev if slot < 8 else cur):
                        o_up_(*((i - 1, 2), (i - 1, 3), (i, 0), (i, 1))[j])
                    for t in tiles[:1]:
                        turned(*old, t)
                    if k and s == 3:
                        k_up(*k)
                    if cur:
                        soft(i, j, s)
                    for t in tiles[2:3]:
                        turned(*old, t)
                    if slot == 14 and prev:
                        act.wait_ge(dve_up, dve_at(i - 1, "LOGITS"))
                        act.activation(pr[:], W[:, 0:E], ACT.Exp, bias=st[:, 24:25], accum_out=st[:, 25:26])\
                           .then_inc(bank_free[1], 1)
                    if prev:
                        rest(i - 1, slot)

            over_pairs(act, body)

        @block.vector
        def _(dve):
            def scale_of(link, rows, s0):
                link(dve.tensor_reduce(st[:, s0:s0 + 1], rows, AX.X, ALU.max, apply_absolute_value=True))
                link(dve.tensor_scalar(st[:, s0:s0 + 1], st[:, s0:s0 + 1], 1.0 / 127.0, 1e-8, ALU.mult, ALU.max))
                link(dve.reciprocal(st[:, s0 + 1:s0 + 2], st[:, s0:s0 + 1]))

            def quantise(link, out, rows, s0):
                scale_of(link, rows, s0)
                link(dve.tensor_scalar(out, rows, st[:, s0 + 1:s0 + 2], MAGIC, ALU.mult, ALU.add))
                link(dve.tensor_scalar(out, out, MAGIC, 127.0, ALU.subtract, ALU.min))
                return dve.tensor_scalar(out, out, -127.0, st[:, s0:s0 + 1], ALU.max, ALU.mult)

            def moments(link, x, s0, bn0):
                link.carried(dve.bn_stats(st[:, bn0:bn0 + 6], x))
                link(dve.bn_aggr(st[:, bn0 + 6:bn0 + 8], st[:, bn0:bn0 + 6]))
                return dve.tensor_scalar(st[:, s0:s0 + 1], st[:, bn0 + 7:bn0 + 8], EPS, None, ALU.add)

            dve.wait_ge(w_in, 16 * len(loads))
            link = Chain(dve, dve_w, 0, 22)
            for rows, wT in ((wq_rows, wqT), (wp_rows, wpT)):
                for k in range(DT):
                    ins = quantise(link, rows[:, k, :], rows[:, k, :], 28)
                    if k == 0:
                        link(ins)
                ins.then_inc(wq_set, 1)
                dve.wait_ge(w_mm, 1 if rows is wq_rows else 2)
                dve.tensor_copy(wT[:].rearrange("p k o -> p (k o)"), W[:]).then_inc(wq_set, 1)
            dve.wait_ge(wq_set, 4)

            def norm_q(i):
                link = Chain(dve, dve_q, i, 9, pause_q[:])
                dve.wait_ge(x_in, 16 * (i + 1))
                moments(link, x_q[:], 0, 32).then_inc(var_up, 1)
                dve.wait_ge(rstd_up, i + 1)
                link(dve.tensor_scalar(lnq[:], x_q[:], st[:, 38:39], st[:, 1:2], ALU.subtract, ALU.mult))
                quantise(link, lnq[:], lnq[:], 2).then_inc(lnq_up, 1)

            def x_up(i):
                dve.wait_ge(bank_full[0], a_at(i, "XQ"))
                dve.tensor_copy(xqT[:].rearrange("p k t -> p (k t)"), W[:, 0:D]).then_inc(bank_free[0], 1)

            def split_q(i):
                link = Chain(dve, dve_q2, i, 2)
                dve.wait_ge(bank_full[0], a_at(i, "Q"))
                after(dve, q_up, i * 2 * STEPS)
                link(dve.tensor_scalar(q_f[:, 0, :], W[:, 0:P], cols[:, BQ, 0:1], DH ** -0.5, ALU.add, ALU.mult))
                dve.tensor_scalar(q_f[:, 1, :], W[:, P:2 * P], cols[:, BQ, 1:2], DH ** -0.5, ALU.add, ALU.mult)\
                   .then_inc(bank_free[0], 1)
                dve.wait_ge(bank_free[0], a_at(i, "Q"))
                link(dve.tensor_copy(q_hi[:].bitcast(F32R), q_f[:]))
                dve.tensor_tensor(q_lo[:], q_f[:], q_hi[:], ALU.subtract).then_inc(q_split, 1)
                link.end()

            def k_low(i, j, c):
                g = j % 2
                c0, cn = CHUNKS[c]
                dve.wait_ge(k_hi_up, (i * STEPS + j) * STRIPS + c + 1)
                dve.scalar_tensor_tensor(K_lo[j % 2][:, c0:c0 + cn], W[:, 0:cn], cols[:, BK, g:g + 1],
                                         K_hi[j % 2][:, c0:c0 + cn].bitcast(F32), ALU.add, ALU.subtract)\
                   .then_inc(bank_free[0], 1)

            def v_up(i, b, unit):
                tiles = V_UNITS[unit]
                dve.wait_ge(bank_full[0], a_at(i, "V", b, unit))
                after(dve, pv_done, (i - 1) * STEPS * KT + 2 * KT * (b + 1))
                dve.tensor_copy(V[b][0:keys_in(tiles[-1]), tiles[0]:tiles[-1] + 1, :].rearrange("p t d -> p (t d)"),
                                W[0:keys_in(tiles[-1]), 0:len(tiles) * D]).then_inc(bank_free[0], 1)

            def strip_max(i, j, s):
                q = STRIPS * j + s
                dve.wait_ge(s_done, i * SLOTS + q + 1)
                dve.tensor_reduce(negmax[:, q:q + 1], S[:, 0:M], AX.X, ALU.max, negate=True).then_inc(max_done, 1)

            def turned(i, j, t):
                n = KT * j + t
                dve.wait_ge(t_done, i * STEPS * KT + n + 1)
                after(dve, pv_done, i * STEPS * KT + n - 1)
                dve.tensor_copy(probsT[n % 2][0:keys_in(t), :], PT[n % 2][0:keys_in(t), :]).then_inc(t_up[1], 1)

            def norm_o(i, j):
                b, g = divmod(j, 2)
                link = Chain(dve, dve_o, i * STEPS + j, 1)
                part, value = (0, a_at(i, "O", j)) if j < 2 else (1, b_at(i, f"O{j}"))
                rd = rden[:, STRIPS * j:STRIPS * (j + 1)]
                dve.wait_ge(exp_done, i * SLOTS + STRIPS * (j + 1))
                link(dve.reciprocal(rd, den[:, STRIPS * j:STRIPS * (j + 1)]))
                dve.wait_ge(bank_full[part], value)
                for h in range(2):
                    rows = slice(h * N, (h + 1) * N)
                    ins = dve.tensor_tensor(
                        o_tok[b * N:(b + 1) * N, g * P:(g + 1) * P].rearrange("n (s h d) -> n s h d", h=2, d=DH)[:, :, h, :],
                        W[rows, 0:P].rearrange("n (s h d) -> n s h d", h=2, d=DH)[:, :, h, :],
                        rd[rows, :].unsqueeze(2).to_broadcast([N, STRIPS, DH]), ALU.mult)
                ins.then_inc(bank_free[part], 1)
                link.end()

            def copy_out(i, name, dst, src):
                dve.wait_ge(bank_full[1], b_at(i, name))
                dve.tensor_copy(dst, src).then_inc(bank_free[1], 1)

            def empty(i, slot, middle, link):
                at = (slot, middle)
                if at == (5, False):
                    copy_out(i, "oqT", oqT[:].rearrange("p k t -> p (k t)"), W[:, 0:D])
                if at == (5, True):
                    dve.wait_ge(xr_in, 16 * (i + 1))
                    link(dve.tensor_tensor(x_res[:], x_res[:], bp_row[:], ALU.add))
                    dve.wait_ge(bank_full[1], b_at(i, "proj"))
                    dve.tensor_tensor(x2[:], W[:, 0:D], x_res[:], ALU.add).then_inc(bank_free[1], 1)
                if at == (6, False):
                    copy_out(i, "ln2T", ln2T[:].rearrange("p k t -> p (k t)"), W[:, 0:D])
                if at == (6, True):
                    after(dve, bc_out, 16 * i)
                    dve.wait_ge(bank_full[1], b_at(i, "xp"))
                    link(dve.tensor_copy(dlT[:], W[:, 0:P]))
                    dve.tensor_copy(BCT[:], W[0:2 * NS, P:2 * P]).then_inc(bank_free[1], 1)
                if at == (7, False):
                    dve.wait_ge(bank_full[1], b_at(i, "dt"))
                    link(dve.tensor_scalar(z[:, 0, :], W[:, 0:P], cols[:, DTB, 0:1], None, ALU.add))
                    dve.tensor_scalar(z[:, 1, :], W[:, P:2 * P], cols[:, DTB, 1:2], None, ALU.add).then_inc(bank_free[1], 1)
                if at == (13, False):
                    after(dve, x3_out, 32 * i)
                    dve.wait_ge(bank_full[1], b_at(i, "yT"))
                    dve.tensor_tensor(x3[:], W[:, 0:D], x2[:], ALU.add).then_inc(bank_free[1], 1)
                if at == (14, False):
                    copy_out(i, "ln3T", ln3T[:].rearrange("p k t -> p (k t)"), W[:, 0:D])
                if at == (14, True):
                    dve.wait_ge(bank_full[1], b_at(i, "logits"))
                    dve.tensor_reduce(st[:, 24:25], W[:, 0:E], AX.X, ALU.max, negate=True).then_inc(dve_up, 1)
                if at == (15, False):
                    dve.wait_ge(bank_full[1], b_at(i, "pos"))
                    link(dve.tensor_tensor(slotv[:], W[:, 0:E], base_e[:], ALU.add))
                    dve.tensor_tensor(base_e[:], W[:, E:2 * E], base_e[:], ALU.add).then_inc(bank_free[1], 1)

            def rest(i, slot, link):
                def up(ins):
                    ins.then_inc(dve_up, 1)

                if slot == 4:
                    dve.wait_ge(bank_free[1], b_at(i, "O3"))
                    link(dve.tensor_tensor(oq[:], o_tok[:], bv_row[:], ALU.add))
                    up(quantise(link, oq[:], oq[:], 4))
                if slot == 5:
                    dve.wait_ge(bank_free[1], b_at(i, "proj"))
                    up(dve.bn_stats(st[:, 40:46], x2[:]))
                    dve.wait_ge(dve_up, dve_at(i, "X2"))
                    link.carried()
                    link(dve.bn_aggr(st[:, 46:48], st[:, 40:46]))
                    up(dve.tensor_scalar(st[:, 8:9], st[:, 47:48], EPS, None, ALU.add))
                    dve.wait_ge(pool_up, pool_at(i, "R2"))
                    up(dve.tensor_scalar(ln2[:], x2[:], st[:, 46:47], st[:, 9:10], ALU.subtract, ALU.mult))
                if slot == 7:
                    dve.wait_ge(bank_free[1], b_at(i, "dt"))
                    up(dve.scalar_tensor_tensor(negz, z[:], -1.0, z[:], ALU.mult, ALU.min))
                    dve.wait_ge(act_up, act_at(i, "EXPZ"))
                    up(dve.tensor_scalar(ez1, ez, 1.0, None, ALU.add))
                    dve.wait_ge(dve_up, dve_at(i, "EZ"))
                    link(dve.tensor_scalar(negz, ez1, 1.0, LN_TINY, ALU.subtract, ALU.add))
                    link(dve.reciprocal(negz, negz))
                    link(dve.tensor_tensor(negz, negz, ez, ALU.mult))
                    dve.wait_ge(act_up, act_at(i, "LNZ"))
                    link(dve.scalar_tensor_tensor(negz, lz, LN_TINY, negz, ALU.add, ALU.mult))
                    link(dve.scalar_tensor_tensor(dt_[:], z[:], 0.0, negz, ALU.max, ALU.add))
                    up(dve.tensor_tensor(u[:], dt_[:], ln2T[:], ALU.mult))
                for h, half in {8: [(0, 0)], 9: [(0, 1)], 11: [(1, 0)], 12: [(1, 1)]}.get(slot, []):
                    dve.wait_ge(act_up, act_at(i, f"AB{h}{half}"))
                    link(dve.memset(abar[half].rearrange("p n (b t) -> p n b t", b=2)[:, :, :, 0:1], 0.0))
                    dve.wait_ge(pool_up, pool_at(i, f"BX{h}"))
                    mine = bx[:, half * (NS // 2):(half + 1) * (NS // 2), :]
                    flat = mine.rearrange("p n t -> p (n t)")
                    up(dve.tensor_tensor_scan(flat, abar[half].rearrange("p n t -> p (n t)"), flat, 0.0,
                                              ALU.mult, ALU.add))
                    dve.wait_ge(dve_up, dve_at(i, f"S{h}{half}"))
                    link(dve.tensor_tensor(mine, mine, BC[:, NS + half * (NS // 2):NS + (half + 1) * (NS // 2), :],
                                           ALU.mult))
                if slot in (9, 12):
                    h = (9, 12).index(slot)
                    link(dve.tensor_reduce(y[:, h, :], bx[:].rearrange("p n t -> p t n"), AX.X, ALU.add))
                    up(dve.scalar_tensor_tensor(y[:, h, :], ln2T[:, h, :], cols[:, DP, h:h + 1], y[:, h, :],
                                                ALU.mult, ALU.add))
                if slot == 13:
                    dve.wait_ge(bank_free[1], b_at(i, "yT"))
                    up(moments(link, x3[:], 16, 48))
                    dve.wait_ge(pool_up, pool_at(i, "R3"))
                    up(dve.tensor_scalar(ln3[:], x3[:], st[:, 54:55], st[:, 17:18], ALU.subtract, ALU.mult))
                if slot == 14:
                    dve.wait_ge(bank_free[1], b_at(i, "logits"))
                    link(dve.reciprocal(st[:, 26:27], st[:, 25:26]))
                    link.carried(dve.tensor_scalar(pr[:], pr[:], st[:, 26:27], None, ALU.mult))
                    link.carried(dve.max(top[:], pr[:]))
                    link.carried(dve.max_index(topi[:], top[:], pr[:]))
                    link(dve.match_replace(pr2[:], top[:], pr[:], -1.0))
                    up(dve.tensor_scalar(sel[:], pr2[:], 0.0, None, ALU.is_lt))
                if slot == 15:
                    idx, slot_, pos, ok, low, out_ = (topf[:, n, :] for n in range(6))
                    link(dve.tensor_copy(idx, topi[:]))
                    for t in range(TOPK):
                        ins = dve.scalar_tensor_tensor(junk[:], iota_e[:], idx[:, t:t + 1], slotv[:], ALU.is_equal,
                                                       ALU.mult, accum_out=slot_[:, t:t + 1])
                        link(ins)
                    link(dve.scalar_tensor_tensor(pos, idx, -float(CAP), slot_, ALU.mult, ALU.add))
                    link(dve.tensor_scalar(ok, pos, float(CAP), None, ALU.is_lt))
                    link(dve.tensor_tensor(scores_all[:, bass.ds(i * TOPK, TOPK)], top[:], ok, ALU.mult))
                    link(dve.tensor_scalar(low, pos, float(CAP - 1), None, ALU.min))
                    link(dve.scalar_tensor_tensor(low, idx, float(CAP), low, ALU.mult, ALU.add))
                    link(dve.tensor_copy(slots_all[:, bass.ds(i * TOPK, TOPK)], low))
                    link(dve.tensor_scalar(out_, ok, -float(2 * E * CAP), float(2 * E * CAP), ALU.mult, ALU.add))
                    link(dve.tensor_tensor(out_, out_, slot_, ALU.add))
                    after(dve, scattered, 16 * TOPK * i)
                    up(dve.tensor_copy(sc_idx[:], out_))

            norm_q(0)
            for c in range(STRIPS):
                if c == 1:
                    x_up(0)
                if c < 3:
                    v_up(0, 0, V_OF_STEP[3][c])
                if c == 1:
                    split_q(0)
                k_low(0, 0, c)

            def body(i, cur, prev, nxt):
                link = Chain(dve, dve_b, i - 1, B_LINKS, pause[:])
                for slot in range(SLOTS):
                    j, s, old, tiles, k, v = pieces(i, slot, cur, prev, nxt)
                    last_k, last_v = left_over(i, slot, cur, prev, nxt)
                    if last_k:
                        k_low(*last_k)
                    if last_v:
                        v_up(*last_v)
                    if slot == 1 and prev:
                        norm_o(i - 1, 2)
                    if slot == 12 and cur:
                        norm_o(i, 1)
                    if slot == 13 and cur and nxt:
                        x_up(i + 1)
                    if prev:
                        empty(i - 1, slot, False, link)
                    if cur:
                        strip_max(i, j, s)
                    for t in tiles[1:2]:
                        turned(*old, t)
                    if k and s == 3:
                        k_low(*k)
                    if v and s < 3:
                        v_up(*v)
                    if slot == 8 and cur:
                        norm_o(i, 0)
                    if slot == 4 and prev:
                        norm_o(i - 1, 3)
                    if slot == 13 and cur and nxt:
                        split_q(i + 1)
                    if prev:
                        empty(i - 1, slot, True, link)
                    for t in tiles[3:4]:
                        turned(*old, t)
                    if prev:
                        rest(i - 1, slot, link)
                    if slot == 10 and cur and nxt:
                        norm_q(i + 1)
                if prev:
                    link.end()

            over_pairs(dve, body)


def expert_phase(nc, io, dram):
    with ExitStack() as ctx:
        def sb(name, shape, dt=F32):
            return ctx.enter_context(nc.sbuf_tensor("sb_" + name, shape, dt))

        def sem(name):
            return ctx.enter_context(nc.semaphore(name))

        ident = sb("ident2", [P, P])
        pause = sb("pause2", [P, 1])
        table = sb("table_sb", [E, CAP])
        idx_all = sb("idx_all", [P, E * CT], U32)
        idx = [sb(f"idx{n}", [P, CT], U32) for n in range(2)]
        xg = [[sb(f"xg{n}_{c}", [P, D]) for c in range(CT)] for n in range(2)]
        xT = [sb(f"xT{n}", [P, DT, CAP]) for n in range(2)]
        wgu = [sb(f"wgu{n}", [P, DT, 2 * FF]) for n in range(2)]
        wd = [sb(f"wd{n}", [FF, D]) for n in range(2)]
        sg = sb("sg", [FF, CAP])
        hid = [sb(f"hid{n}", [FF, CAP]) for n in range(2)]
        ys = [sb(f"ys{n}", [P, CT, D]) for n in range(2)]
        XT = [ctx.enter_context(nc.psum_tensor(f"XT{k}", [P, CAP], F32)) for k in range(DT)]
        G = ctx.enter_context(nc.psum_tensor("G", [P, CAP], F32))
        U = ctx.enter_context(nc.psum_tensor("U", [P, CAP], F32))
        Y = [ctx.enter_context(nc.psum_tensor(f"Y{k}", [P, 2, D], F32)) for k in range(2)]

        e_const = sem("e_const")
        tab_in = sem("tab_in")
        tab_t = sem("tab_t")
        tab_up = sem("tab_up")
        w_in = [sem(f"ew_in{n}") for n in range(2)]
        idx_up = sem("idx_up")
        x_in = [sem(f"ex_in{n}") for n in range(2)]
        xt_done = sem("xt_done")
        xt_up = [sem("xt_up_act"), sem("xt_up_dve")]
        gu_done = sem("gu_done")
        sg_up = sem("sg_up")
        hid_up = sem("hid_up")
        y_done = sem("y_done")
        y_up = [sem("y_up_act"), sem("y_up_dve")]
        y_out = [sem(f"y_out{n}") for n in range(2)]
        block = ctx.enter_context(nc.Block())

        def over_experts(eng, body):
            for e in range(2):
                body(e, e)
            with eng.Fori(1, E // 2 - 1) as two:
                for n in range(2):
                    body(2 * two + n, n)
            for e in range(E - 2, E):
                body(e, e % 2)

        def x_count(e, n):
            return (e - n) * (16 * CT // 2) + 16 * CT

        def w_count(e, n):
            return (e - n) * 16 + 32

        @block.sync
        def _(sp):
            sp.dma_start(table[:], dram["table"].rearrange("(e c) o -> e (c o)", e=E)).then_inc(tab_in, 16)

            def body(e, n):
                after(sp, gu_done, e - 1)
                sp.dma_start(wgu[n][:], io["wgu"][bass.ds(e, 1)].rearrange("o (k p) f -> p (o k) f", p=P)).then_inc(w_in[n], 16)
                after(sp, y_done, e - 1)
                sp.dma_start(wd[n][:], io["wdT"][bass.ds(e, 1)].rearrange("o f d -> (o f) d")).then_inc(w_in[n], 16)
                if isinstance(e, int) and e == 0:
                    return
                store(e - 1, 1 - n)

            def store(e, n):
                for m in range(2):
                    sp.wait_ge(y_up[m], e + 1)
                sp.dma_start(dram["y"][bass.ds(e * CAP, CAP), :].rearrange("(c p) d -> p c d", p=P), ys[n][:]).then_inc(y_out[n], 16)

            over_experts(sp, body)
            store(E - 1, (E - 1) % 2)
            for n in range(2):
                sp.wait_ge(y_out[n], 16 * (E // 2))

        @block.gpsimd
        def _(pool):
            pool.memset(ident[:], 0.0).then_inc(e_const, 1)
            pool.wait_ge(e_const, 1)
            pool.affine_select(out=ident[:], in_=ident[:], compare_op=ALU.not_equal, fill=1.0, base=0,
                               pattern=[[-1, P]], channel_multiplier=1).then_inc(e_const, 1)
            pool.wait_ge(tab_up, 1)

            def body(e, n):
                if not (isinstance(e, int) and e < 2):
                    pool.wait_ge(x_in[n], x_count(e, n) - 16 * CT)
                    pool.wait_ge(xt_done, e - 1)
                after(pool, idx_up, 2 * e)
                pool.tensor_copy(idx[n][:], idx_all[:, bass.ds(e * CT, CT)]).then_inc(idx_up, 1)
                pool.wait_ge(idx_up, 2 * e + 1)
                pool.tensor_tensor(pause[:], ident[:, 0:1], ident[:, 0:1], ALU.add).then_inc(idx_up, 1)
                for c in range(CT):
                    pool.indirect_dma_start(xg[n][c][:], None, dram["ln3"],
                                            bass.IndirectOffsetOnAxis(ap=idx[n][:, c:c + 1], axis=0)).then_inc(x_in[n], 16)

            over_experts(pool, body)

        @block.tensor
        def _(pe):
            def turn(e, n):
                pe.wait_ge(x_in[n], x_count(e, n))
                for m in range(2):
                    after(pe, xt_up[m], e)
                for k in range(DT):
                    for c in range(CT):
                        ins = pe.transpose(XT[k][:, c * P:(c + 1) * P], xg[n][c][:, k * P:(k + 1) * P], ident[:])
                ins.then_inc(xt_done, 1)

            pe.wait_ge(e_const, 2)
            pe.wait_ge(tab_in, 16)
            for c in range(CT):
                ins = pe.transpose(Y[0][:, 0, c * E:(c + 1) * E], table[:, c * P:(c + 1) * P], ident[0:E, 0:E])
            ins.then_inc(tab_t, 1)
            turn(0, 0)

            def body(e, n):
                pe.wait_ge(w_in[n], w_count(e, n))
                for m in range(2):
                    pe.wait_ge(xt_up[m], e + 1)
                after(pe, hid_up, e)
                for m, dst in enumerate((G, U)):
                    for k in range(DT):
                        ins = pe.matmul(dst[0:FF, :], wgu[n][:, k, m * FF:(m + 1) * FF], xT[n][:, k, :],
                                        start=(k == 0), stop=(k == DT - 1))
                ins.then_inc(gu_done, 1)
                if not (isinstance(e, int) and e == E - 1):
                    turn(e + 1, 1 - n)
                pe.wait_ge(hid_up, e + 1)
                for m in range(2):
                    after(pe, y_up[m], e)
                for c in range(CT):
                    ins = pe.matmul(Y[c // 2][:, c % 2, :], hid[n][:, c * P:(c + 1) * P], wd[n][:], start=True, stop=True)
                ins.then_inc(y_done, 1)

            over_experts(pe, body)

        @block.scalar
        def _(act):
            def body(e, n):
                if n == 0 and isinstance(e, int) and e == 0:
                    turned(0, 0)
                act.wait_ge(gu_done, e + 1)
                act.activation(sg[:], G[0:FF, :], ACT.Silu).then_inc(sg_up, 1)
                if not (isinstance(e, int) and e == E - 1):
                    turned(e + 1, 1 - n)
                act.wait_ge(y_done, e + 1)
                if not (isinstance(e, int) and e < 2):
                    act.wait_ge(y_out[n], (e - n) * 8)
                act.activation(ys[n][:, 0:2, :], Y[0][:], ACT.Copy).then_inc(y_up[0], 1)

            def turned(e, n):
                act.wait_ge(xt_done, e + 1)
                after(act, gu_done, e - 1)
                act.activation(xT[n][:, 0, :], XT[0][:], ACT.Copy).then_inc(xt_up[0], 1)

            over_experts(act, body)

        @block.vector
        def _(dve):
            dve.wait_ge(tab_t, 1)
            dve.tensor_copy(idx_all[:].rearrange("p (e c) -> p c e", c=CT),
                            Y[0][:, 0, 0:CT * E].rearrange("p (c e) -> p c e", c=CT)).then_inc(tab_up, 1)

            def turned(e, n):
                dve.wait_ge(xt_done, e + 1)
                after(dve, gu_done, e - 1)
                dve.tensor_copy(xT[n][:, 1, :], XT[1][:]).then_inc(xt_up[1], 1)

            def body(e, n):
                if n == 0 and isinstance(e, int) and e == 0:
                    turned(0, 0)
                dve.wait_ge(gu_done, e + 1)
                dve.wait_ge(sg_up, e + 1)
                after(dve, y_done, e - 1)
                dve.tensor_tensor(hid[n][:], U[0:FF, :], sg[:], ALU.mult).then_inc(hid_up, 1)
                if not (isinstance(e, int) and e == E - 1):
                    turned(e + 1, 1 - n)
                dve.wait_ge(y_done, e + 1)
                if not (isinstance(e, int) and e < 2):
                    dve.wait_ge(y_out[n], (e - n) * 8)
                dve.tensor_copy(ys[n][:, 2:4, :], Y[1][:]).then_inc(y_up[1], 1)

            over_experts(dve, body)


def combine_phase(nc, io, dram, out):
    with ExitStack() as ctx:
        def sb(name, shape, dt=F32):
            return ctx.enter_context(nc.sbuf_tensor("sb_" + name, shape, dt))

        def sem(name):
            return ctx.enter_context(nc.semaphore(name))

        pause = sb("pause3", [P, 1])
        zeros = sb("zeros", [P, 1])
        acc = [sb(f"acc{n}", [P, D]) for n in range(2)]
        yg = [[sb(f"yg{n}_{t}", [P, D]) for t in range(TOPK)] for n in range(2)]
        idx = [sb(f"cidx{n}", [P, TOPK], U32) for n in range(2)]
        sc = [sb(f"csc{n}", [P, TOPK]) for n in range(2)]
        x_in = [sem(f"cx_in{n}") for n in range(2)]
        idx_up = sem("cidx_up")
        zero_up = sem("zero_up")
        y_in = [sem(f"cy_in{n}") for n in range(2)]
        sc_up = sem("csc_up")
        acc_up = sem("acc_up")
        o_out = [sem(f"o_out{n}") for n in range(2)]
        block = ctx.enter_context(nc.Block())

        def over_tiles(eng, body):
            for i in range(2):
                body(i, i)
            with eng.Fori(1, PAIRS // 2) as two:
                for n in range(2):
                    body(2 * two + n, n)

        @block.sync
        def _(sp):
            def load(i, n):
                if not (isinstance(i, int) and i < 2):
                    sp.wait_ge(o_out[n], (i - n) * 8)
                sp.dma_start(acc[n][:], dram["x3"][bass.ds(i * P, P), :]).then_inc(x_in[n], 16)

            def body(i, n):
                load(i, n)
                sp.wait_ge(acc_up, TOPK * (i + 1))
                sp.dma_start(out[bass.ds(i * P, P), :], acc[n][:]).then_inc(o_out[n], 16)

            over_tiles(sp, body)
            for n in range(2):
                sp.wait_ge(o_out[n], 16 * (PAIRS // 2))

        @block.gpsimd
        def _(pool):
            pool.memset(zeros[:], 0.0).then_inc(zero_up, 1)
            pool.wait_ge(zero_up, 1)

            def body(i, n):
                if not (isinstance(i, int) and i < 2):
                    pool.wait_ge(y_in[n], (i - n) * (8 * TOPK))
                    pool.wait_ge(acc_up, TOPK * (i - 1))
                after(pool, idx_up, 2 * i)
                pool.tensor_copy(idx[n][:], dram["slots_sb"][:, bass.ds(i * TOPK, TOPK)]).then_inc(idx_up, 1)
                pool.wait_ge(idx_up, 2 * i + 1)
                pool.tensor_tensor(pause[:], zeros[:], zeros[:], ALU.add).then_inc(idx_up, 1)
                for t in range(TOPK):
                    pool.indirect_dma_start(yg[n][t][:], None, dram["y"],
                                            bass.IndirectOffsetOnAxis(ap=idx[n][:, t:t + 1], axis=0)).then_inc(y_in[n], 16)

            over_tiles(pool, body)

        @block.vector
        def _(dve):
            def body(i, n):
                dve.tensor_copy(sc[n][:], dram["scores_sb"][:, bass.ds(i * TOPK, TOPK)]).then_inc(sc_up, 1)
                dve.wait_ge(sc_up, i + 1)
                dve.wait_ge(x_in[n], (i - n) * 8 + 16)
                dve.wait_ge(y_in[n], (i - n) * (8 * TOPK) + 16 * TOPK)
                for t in range(TOPK):
                    dve.scalar_tensor_tensor(acc[n][:], yg[n][t][:], sc[n][:, t:t + 1], acc[n][:], ALU.mult, ALU.add)\
                       .then_inc(acc_up, 1)
                    dve.wait_ge(acc_up, i * TOPK + t + 1)

            over_tiles(dve, body)


def perceiver(nc, ins, out):
    with ExitStack() as ctx:
        dram = {
            "bc": nc.dram_tensor("bc_scratch", (2 * NS, P), F32).ap(),
            "x3": nc.dram_tensor("x3_scratch", (TOK, D), F32).ap(),
            "ln3": nc.dram_tensor("ln3_scratch", (TOK, D), F32).ap(),
            "table": nc.dram_tensor("table_scratch", (E * CAP, 1), F32).ap(),
            "y": nc.dram_tensor("y_scratch", (E * CAP, D), F32).ap(),
            "slots_sb": ctx.enter_context(nc.sbuf_tensor("slots_all", [P, PAIRS * TOPK], U32)),
            "scores_sb": ctx.enter_context(nc.sbuf_tensor("scores_all", [P, PAIRS * TOPK], F32)),
        }
        mixer_phase(nc, ins, dram)
        expert_phase(nc, ins, dram)
        combine_phase(nc, ins, dram, out)


def laid_out(inputs):
    a = {k: np.asarray(v) for k, v in inputs.items()}

    def cols(v):
        return v.reshape(DT, P).T

    x = a["x"]
    return {
        "x": x.reshape(TOK, D),
        "ctxT": a["ctx_2048"].transpose(0, 2, 1),
        "wq": a["L0_xattn_wq"], "bq": cols(a["L0_xattn_bq"]),
        "wkvT": a["L0_xattn_wkv"].T,
        "bk": cols(a["L0_xattn_bkv"][:D]), "bv": a["L0_xattn_bkv"][D:],
        "wp": a["L0_xattn_wp"], "bp": a["L0_xattn_bp"],
        "xpT": a["L0_attn_x_proj_w"].T, "dpT": a["L0_attn_dt_proj_w"].T,
        "dtb": cols(a["L0_attn_dt_proj_b"]), "A_log": a["L0_attn_A_log"], "Dp": cols(a["L0_attn_D_param"]),
        "gateT": a["L0_ffn_gate_w"].T,
        "wgu": np.concatenate([a["L0_ffn_w_gate"].transpose(0, 2, 1), a["L0_ffn_w_up"].transpose(0, 2, 1)], axis=2),
        "wdT": a["L0_ffn_w_down"].transpose(0, 2, 1),
    }


def kernel(**inputs):
    import concourse.bacc as bacc
    from concourse.bass_utils import run_bass_kernel_spmd

    nc = bacc.Bacc("TRN2", target_bir_lowering=False, num_devices=1)
    arrays, ins = {}, {}
    for name, a in laid_out(inputs).items():
        a = np.ascontiguousarray(a)
        arrays[name] = a
        ins[name] = nc.dram_tensor(name, a.shape, mybir.dt.from_np(a.dtype), kind="ExternalInput").ap()
    out = nc.dram_tensor("out", (TOK, D), F32, kind="ExternalOutput").ap()
    perceiver(nc, ins, out)
    r = run_bass_kernel_spmd(nc, [arrays], core_ids=[0])
    return r.results[0]["out"].reshape(B, N, D)
```

```python
from contextlib import ExitStack

import numpy as np
import concourse.bass as bass
from concourse import mybir

F32 = mybir.dt.float32
F32R = mybir.dt.float32r
BF16 = mybir.dt.bfloat16
U32 = mybir.dt.uint32
ALU = mybir.AluOpType
ACT = mybir.ActivationFunctionType
AX = mybir.AxisListType

P = 128
B, N, D = 32, 64, 256
M = 1601
H, DH = 16, 16
DT = D // P
TOK = B * N
PAIRS = TOK // P
HG = H // DT
STRIPS = 4
MP = 1602
KT = (M + P - 1) // P
CHUNKS = [(c, min(512, M - c)) for c in range(0, M, 512)]
CHUNKS_FIRST, CHUNKS_LAST = (0, 1), (2, 3)
NS, R = 16, 128
E, TOPK, FF = 64, 8, 96
CAP = 2 * TOK * TOPK // E
CT = CAP // P
MAGIC = 12582912.0
EPS = 1e-5

STEPS = 4
SLOTS = STEPS * STRIPS
PV_SPLIT = [0, 3, 6, 9, 13]
V_UNITS = [[t for t in (2 * u, 2 * u + 1) if t < KT] for u in range((KT + 1) // 2)]
V_OF_STEP = {0: [4, 5, 6], 1: [0, 1, 2, 3], 2: [4, 5, 6], 3: [0, 1, 2, 3]}



TURNED_BY = [(t - first) % 2 for first, end in zip(PV_SPLIT, PV_SPLIT[1:]) for t in range(first, end)]


def a_order():
    order = []
    for slot in range(SLOTS):
        j, s = divmod(slot, STRIPS)
        if slot == 12:
            order.append(("Q",))
        k = [("K", (j + 1) % STEPS, s)]
        v = [("V", 1 if j in (1, 2) else 0, V_OF_STEP[j][s])] if s < len(V_OF_STEP[j]) else []
        order += k if s == 3 else v
        order += {8: [("O", 0)], 11: [("XQ",)], 12: [("O", 1)]}.get(slot, [])
        order += v if s == 3 else k
    return order


A_ORDER = a_order()
assert A_ORDER.index(("V", 0, 6)) < A_ORDER.index(("K", 1, 3)) and A_ORDER.index(("V", 1, 6)) < A_ORDER.index(("K", 3, 3))
AHEAD = [use for use in A_ORDER[A_ORDER.index(("XQ",)):] if use[0] != "O"]
B_ORDER = ["O2", "O3", "oqT", "proj", "ln2T", "xp", "dt", "yT", "ln3T", "logits", "pos"]
DVE_ORDER = ["OQ", "X2", "V2", "LN2", "Z", "EZ", "U", "S00", "S01", "Y0", "S10", "S11", "Y1", "V3", "LN3", "LOGITS", "SEL", "ROUTE"]
ACT_ORDER = ["EXPZ", "LNZ", "AB00", "AB01", "AB10", "AB11"]
POOL_ORDER = ["R2", "BX00", "BX01", "BX10", "BX11", "R3"]


CTX_SLOTS = [1, 3, 5, 6]
DECAYS = {8: [(0, 0, 0, 8), (0, 1, 0, 4)], 9: [(0, 1, 4, 8), (1, 0, 0, 4)], 10: [(1, 0, 4, 8), (1, 1, 0, 4)],
          11: [(1, 1, 4, 8)]}
B_LINKS = 48


def a_at(i, *name):
    if isinstance(i, int) and i == 0 and name in AHEAD:
        return AHEAD.index(name) + 1
    at = len(AHEAD) + (i - (name in AHEAD)) * len(A_ORDER) + A_ORDER.index(name) + 1
    if isinstance(i, int) and i == PAIRS - 1:
        at -= sum(use in AHEAD for use in A_ORDER[:A_ORDER.index(name)]) * (name not in AHEAD)
    return at


def in_order(order):
    def at(i, name):
        return i * len(order) + order.index(name) + 1
    return at


b_at, dve_at, act_at, pool_at = (in_order(o) for o in (B_ORDER, DVE_ORDER, ACT_ORDER, POOL_ORDER))


def up_at(i, j, t):
    e = TURNED_BY[t]
    per = TURNED_BY.count(e)
    return e, (i * STEPS + j) * per + TURNED_BY[:t + 1].count(e)


def two_before(i, j, t):
    return (i, j, t - 2) if t >= 2 else (i, j - 1, KT - 2 + t) if j else (i - 1, STEPS - 1, KT - 2 + t)


def keys_in(t):
    return min(P, M - t * P)


def after(eng, sem, value):
    if isinstance(value, int) and value <= 0:
        return
    eng.wait_ge(sem, value)


class Chain:

    def __init__(self, eng, sem, turn, per, pause=None):
        self.eng, self.sem, self.base, self.per, self.n, self.pause = eng, sem, turn * per, per, 0, pause

    def __call__(self, ins):
        self.n += 1
        ins.then_inc(self.sem, 1)
        self.eng.wait_ge(self.sem, self.base + self.n)

    def carried(self, ins=None):
        if ins is not None:
            self(ins)
        self.n += 1
        self.eng.memset(self.pause, 0.0).then_inc(self.sem, 1)

    def end(self):
        assert self.n == self.per, self.n


def over_pairs(eng, body):
    body(0, True, False, True)
    body(1, True, True, True)
    with eng.Fori(2, PAIRS - 1) as i:
        body(i, True, True, True)
    body(PAIRS - 1, True, True, False)
    body(PAIRS, False, True, False)


def pieces(i, slot, cur, prev, nxt):
    j, s = divmod(slot, STRIPS)
    old = (i - 1, 3) if j == 0 else (i, j - 1)
    tiles = list(range(PV_SPLIT[s], PV_SPLIT[s + 1])) if (prev if j == 0 else cur) else []
    k = v = None
    if cur and (j < 3 or nxt):
        k = (i, j + 1, s) if j < 3 else (i + 1, 0, s)
        if s < len(V_OF_STEP[j]):
            v = {0: (i, 0), 1: (i, 1), 2: (i, 1), 3: (i + 1, 0)}[j] + (V_OF_STEP[j][s],)
    return j, s, old, tiles, k, v


def left_over(i, slot, cur, prev, nxt):
    if slot == 0:
        return None, ((i, 0, V_OF_STEP[3][3]) if cur else None)
    j, s, old, tiles, k, v = pieces(i, slot - 1, cur, prev, nxt)
    return (None, v) if s == 3 else (k, None)


def mixer_phase(nc, io, dram):
    with ExitStack() as ctx:
        def sb(name, shape, dt=F32):
            return ctx.enter_context(nc.sbuf_tensor("sb_" + name, shape, dt))

        def sem(name):
            return ctx.enter_context(nc.semaphore(name))

        wqT = sb("wqT", [P, DT, D])
        wpT = sb("wpT", [P, DT, D])
        wkv_in = sb("wkv_in", [P, DT, 2 * D])
        wkv_hi, wkv_lo = (sb(f"wkv_{m}", [P, DT, 2 * D], F32R) for m in ("hi", "lo"))
        ctx_new = wkv_in
        ctx_hi, ctx_lo = (sb(f"ctx_{m}", [P, DT, MP], F32R) for m in ("hi", "lo"))
        xpT = sb("xpT", [P, DT, R + 2 * NS])
        dpT = sb("dpT", [P, D])
        gateT = sb("gateT", [P, DT, E])
        cols = sb("cols", [P, 4, DT])
        bv_row = sb("bv_row", [P, D])
        bp_row = sb("bp_row", [P, D])
        A = sb("A", [P, DT, NS])
        ident = sb("ident", [P, P])
        by_head = sb("by_head", [P, HG])
        headmask = sb("headmask", [P, 2])
        before = sb("before", [P, P], BF16)
        ones = sb("ones", [P, P], BF16)
        iota_e = sb("iota_e", [P, E])
        tokid = sb("tokid", [P, 1])
        tile_rows = sb("tile_rows", [P, 1])
        pause, pause_q, pause_p = (sb(n, [P, 1]) for n in ("pause", "pause_q", "pause_p"))
        neg_half = sb("neg_half", [P, 1])
        K_hi = [sb(f"K_hi{n}", [P, MP], F32R) for n in range(2)]
        K_lo = [sb(f"K_lo{n}", [P, MP], F32R) for n in range(2)]
        V = [sb(f"V{n}", [P, KT, D]) for n in range(2)]
        Q_hi = [sb(f"Q_hi{n}", [P, 2, N], F32R) for n in range(2)]
        Q_lo = [sb(f"Q_lo{n}", [P, 2, N], F32R) for n in range(2)]
        probs = [[sb(f"probs{n}_{s}", [P, M]) for s in range(STRIPS)] for n in range(2)]
        probsT = [sb(f"probsT{n}", [P, STRIPS * P]) for n in range(2)]
        negmax = sb("negmax", [P, STEPS * STRIPS])
        den = sb("den", [P, STEPS * STRIPS])
        rden = sb("rden", [P, STEPS * STRIPS])
        OT = sb("OT", [P, P])
        x_q = sb("x_q", [P, D])
        lnq = x_q
        xqT = sb("xqT", [P, DT, P])
        q_f = sb("q_f", [P, DT, P])
        q_hi = sb("q_hi", [P, DT, P])
        q_lo = q_f
        st = sb("st", [P, 64])
        o_tok = sb("o_tok", [P, D])
        oq = o_tok
        x_res = sb("x_res", [P, D])
        x2 = sb("x2", [P, D])
        ln2 = sb("ln2", [P, D])
        ln2T = sb("ln2T", [P, DT, P])
        oqT = sb("oqT", [P, DT, P])
        dlT = sb("dlT", [P, P])
        BCT = sb("BCT", [2 * NS, P])
        BC = sb("BC", [P, 2 * NS, P])
        z = sb("z", [P, DT, P])
        soft_ = sb("soft", [P, 4, DT, P])
        negz, ez, ez1, lz = (soft_[:, n] for n in range(4))
        dt_ = sb("dt_", [P, DT, P])
        u = sb("u", [P, DT, P])
        abar = [sb("abar", [P, NS // 2, P])[:], soft_[:].rearrange("p a h t -> p (a h) t")]
        bx = sb("bx", [P, NS, P])
        wq_rows, wp_rows = (bx[:, n:n + 4, :].rearrange("p (k a) b -> p k (a b)", k=DT) for n in (4, 8))
        y = z
        x3 = x2
        ln3 = sb("ln3", [P, D])
        ln3T = oqT
        pr = sb("pr", [P, E])
        pr2 = sb("pr2", [P, E])
        sel = sb("sel", [P, E], BF16)
        slotv = sb("slotv", [P, E])
        base_e = sb("base_e", [P, E])
        top = sb("top", [P, TOPK])
        topi = sb("topi", [P, TOPK], U32)
        topf = sb("topf", [P, 6, TOPK])
        junk = bx[:].rearrange("p (t a) b -> p t (a b)", t=TOPK)[:, :, 0:E]
        sc_idx = sb("sc_idx", [P, TOPK], U32)
        slots_all, scores_all = dram["slots_sb"], dram["scores_sb"]

        S = ctx.enter_context(nc.psum_tensor("S", [P, 2048], F32))
        PT = [ctx.enter_context(nc.psum_tensor(f"PT{n}", [P, 512], F32)) for n in range(2)]
        O = ctx.enter_context(nc.psum_tensor("O", [P, 512], F32))
        W = ctx.enter_context(nc.psum_tensor("W", [P, 512], F32))

        w_in = sem("w_in")
        consts = sem("consts")
        wq_set = sem("w_set")
        a_set = sem("a_set")
        w_mm = sem("w_mm")
        table_zero = sem("table_zero")
        ctx_in = [sem(f"ctx_in{c}") for c in range(len(CHUNKS))]
        ctx_hi_up = sem("ctx_hi_up")
        ctx_up = sem("ctx_up")
        wkv_hi_up = sem("wkv_hi_up")
        wkv_up = sem("wkv_up")
        x_in = sem("x_in")
        xr_in = sem("xr_in")
        bank_full = [sem("bank_full_a"), sem("bank_full_b")]
        bank_free = [sem("bank_free_a"), sem("bank_free_b")]
        k_hi_up = sem("k_hi_up")
        var_up = sem("var_up")
        rstd_up = sem("rstd_up")
        lnq_up = sem("lnq_up")
        q_split = sem("q_split")
        q_up = sem("q_up")
        s_done = sem("s_done")
        max_done = sem("max_done")
        exp_done = sem("exp_done")
        t_done = sem("t_done")
        t_up = [sem("t_up_act"), sem("t_up_dve")]
        pv_done = sem("pv_done")
        o_up = sem("o_up")
        dve_up = sem("dve_up")
        act_up = sem("act_up")
        pool_up = sem("pool_up")
        bc_out = sem("bc_out")
        bc_in = sem("bc_in")
        x3_out = sem("x3_out")
        scattered = sem("scattered")
        tokid_up = sem("tokid_up")
        dve_w, dve_q, dve_q2, dve_o, dve_b, dve_y = (sem(f"dve_{n}") for n in ("w", "q", "q2", "o", "b", "y"))
        block = ctx.enter_context(nc.Block())

        loads = (
            (wq_rows, io["wq"].rearrange("(k p) i -> p k i", p=P)),
            (wp_rows, io["wp"].rearrange("(k p) i -> p k i", p=P)),
            (wkv_in[:], io["wkvT"].rearrange("(k p) o -> p k o", p=P)),
            (xpT[:], io["xpT"].rearrange("(k p) o -> p k o", p=P)),
            (dpT[:], io["dpT"]),
            (gateT[:], io["gateT"].rearrange("(k p) o -> p k o", p=P)),
            (cols[:, 0, :], io["bq"]), (cols[:, 1, :], io["bk"]),
            (cols[:, 2, :], io["dtb"]), (cols[:, 3, :], io["Dp"]),
            (bv_row[:], io["bv"].partition_broadcast(P)),
            (bp_row[:], io["bp"].partition_broadcast(P)),
            (A[:], io["A_log"].rearrange("(h p) n -> p h n", p=P)),
        )
        BQ, BK, DTB, DP = range(4)

        @block.sync
        def _(sp):
            def x_rows(i):
                return io["x"][bass.ds(i * P, P), :]

            def load_ctx(batch, c):
                c0, cn = CHUNKS[c]
                after(sp, ctx_up, batch * len(CHUNKS) + c)
                src = io["ctxT"][bass.ds(batch, 1)].rearrange("o (k p) m -> p (o k) m", p=P)
                sp.dma_start(ctx_new[:, :, 0:cn], src[:, :, c0:c0 + cn]).then_inc(ctx_in[c], 16)

            for dst, src in loads:
                sp.dma_start(dst, src).then_inc(w_in, 16)
            sp.dma_start(x_q[:], x_rows(0)).then_inc(x_in, 16)
            sp.wait_ge(wkv_up, 1)
            for c in range(len(CHUNKS)):
                load_ctx(0, c)

            def body(i, cur, prev, nxt):
                if cur and nxt:
                    sp.wait_ge(bank_full[0], a_at(i, "XQ"))
                    sp.dma_start(x_q[:], x_rows(i + 1)).then_inc(x_in, 16)
                if prev:
                    after(sp, dve_up, dve_at(i - 2, "Y1"))
                    sp.dma_start(x_res[:], x_rows(i - 1)).then_inc(xr_in, 16)
                if cur:
                    for c in range(len(CHUNKS)):
                        load_ctx(2 * i + 1, c)
                if prev:
                    sp.wait_ge(bank_free[1], b_at(i - 1, "xp"))
                    sp.dma_start(dram["bc"], BCT[:]).then_inc(bc_out, 16)
                    sp.wait_ge(bc_out, i * 16)
                    sp.dma_start(BC[:].rearrange("p n t -> p (n t)"), dram["bc"].rearrange("n t -> (n t)").partition_broadcast(P)).then_inc(bc_in, 16)
                if cur and nxt:
                    for c in range(len(CHUNKS)):
                        load_ctx(2 * i + 2, c)
                if prev:
                    sp.wait_ge(dve_up, dve_at(i - 1, "LN3"))
                    sp.dma_start(dram["x3"][bass.ds((i - 1) * P, P), :], x3[:]).then_inc(x3_out, 16)
                    sp.dma_start(dram["ln3"][bass.ds((i - 1) * P, P), :], ln3[:]).then_inc(x3_out, 16)

            over_pairs(sp, body)
            sp.wait_ge(x3_out, 32 * PAIRS)

        @block.gpsimd
        def _(pool):
            pool.memset(ident[:], 0.0).then_inc(consts, 1)
            pool.memset(by_head[:], 1.0).then_inc(consts, 1)
            pool.memset(ones[:], 1.0).then_inc(consts, 1)
            pool.memset(neg_half[:], -0.5).then_inc(consts, 1)
            pool.memset(bx[:, 0:2, :], 0.0).then_inc(consts, 1)
            for part in (ctx_hi, ctx_lo):
                pool.memset(part[:, :, M:MP].bitcast(F32), 0.0).then_inc(consts, 1)
            for n in range(2):
                pool.memset(K_hi[n][:, M:MP].bitcast(F32), 0.0).then_inc(consts, 1)
                pool.memset(K_lo[n][:, M:MP].bitcast(F32), 0.0).then_inc(consts, 1)
            pool.iota(iota_e[:], [[1, E]], base=0, channel_multiplier=0,
                      allow_small_or_imprecise_dtypes=True).then_inc(consts, 1)
            pool.iota(tokid[:], [[0, 1]], base=-P, channel_multiplier=1,
                      allow_small_or_imprecise_dtypes=True).then_inc(consts, 1)
            pool.iota(base_e[:], [[CAP, E]], base=0, channel_multiplier=0,
                      allow_small_or_imprecise_dtypes=True).then_inc(consts, 1)
            pool.memset(tile_rows[:], float(P)).then_inc(consts, 1)
            pool.wait_ge(consts, 15)
            pool.affine_select(out=ident[:], in_=ident[:], compare_op=ALU.not_equal, fill=1.0, base=0,
                               pattern=[[-1, P]], channel_multiplier=1).then_inc(consts, 1)
            pool.affine_select(out=by_head[:], in_=by_head[:], compare_op=ALU.is_ge, fill=0.0, base=0,
                               pattern=[[-DH, HG]], channel_multiplier=1).then_inc(consts, 1)
            pool.affine_select(out=before[:], in_=ones[:], compare_op=ALU.is_gt, fill=0.0, base=0,
                               pattern=[[1, P]], channel_multiplier=-1).then_inc(consts, 1)
            pool.dma_start(dram["table"].rearrange("(p c) o -> p (c o)", p=P),
                           bx[:, 0:2, :].rearrange("p a b -> p (a b)")).then_inc(table_zero, 16)
            pool.wait_ge(consts, 18)
            pool.affine_select(out=by_head[:], in_=by_head[:], compare_op=ALU.is_ge, fill=0.0, base=DH - 1,
                               pattern=[[DH, HG]], channel_multiplier=-1).then_inc(consts, 1)
            pool.wait_ge(consts, 19)
            pool.tensor_tensor(by_head[:, 0:4], by_head[:, 0:4], by_head[:, 4:8], ALU.add).then_inc(consts, 1)
            pool.wait_ge(consts, 20)
            pool.tensor_tensor(headmask[:], by_head[:, 0:2], by_head[:, 2:4], ALU.add).then_inc(consts, 1)
            pool.wait_ge(consts, 21)
            pool.wait_ge(table_zero, 16)

            def rstd_q(i):
                pool.wait_ge(var_up, i + 1)
                pool.tensor_tensor(st[:, 1:2], st[:, 0:1], neg_half[:], ALU.pow).then_inc(rstd_up, 1)

            def spread_q(i, j):
                b, g = divmod(j, 2)
                pool.wait_ge(q_split, i + 1)
                after(pool, s_done, i * SLOTS + STRIPS * (j - 1))
                for dst, src in ((Q_hi[j % 2], q_hi), (Q_lo[j % 2], q_lo)):
                    pool.tensor_tensor(
                        dst[:], src[:, g, b * N:(b + 1) * N].unsqueeze(1).to_broadcast([P, 2, N]),
                        headmask[:].unsqueeze(2).to_broadcast([P, 2, N]), ALU.mult).then_inc(q_up, 1)

            def scan_input(i, h):
                for half in range(2):
                    if h == 0:
                        pool.wait_ge(dve_up, dve_at(i, "U"))
                        pool.wait_ge(bc_in, (i + 1) * 16)
                    elif half == 0:
                        pool.wait_ge(dve_y, i * DT + 1)
                    else:
                        pool.wait_ge(dve_up, dve_at(i, "Y0"))
                    pool.tensor_tensor(bx[:, half * (NS // 2):(half + 1) * (NS // 2), :],
                                       u[:, h, :].unsqueeze(1).to_broadcast([P, NS // 2, P]),
                                       BC[:, half * (NS // 2):(half + 1) * (NS // 2), :], ALU.mult).then_inc(pool_up, 1)

            def ctx_rest(batch, c):
                c0, cn = CHUNKS[c]
                pool.wait_ge(ctx_hi_up, batch * len(CHUNKS) + c + 1)
                pool.tensor_tensor(ctx_lo[:, :, c0:c0 + cn], ctx_new[:, :, 0:cn], ctx_hi[:, :, c0:c0 + cn].bitcast(F32), ALU.subtract)\
                    .then_inc(ctx_up, 1)

            rstd_q(0)
            pool.wait_ge(wkv_hi_up, 1)
            pool.tensor_tensor(wkv_lo[:], wkv_in[:], wkv_hi[:].bitcast(F32), ALU.subtract)\
                .then_inc(wkv_up, 1)
            for c in range(len(CHUNKS)):
                ctx_rest(0, c)
            spread_q(0, 0)

            def body(i, cur, prev, nxt):
                if cur:
                    spread_q(i, 1)
                if cur:
                    ctx_rest(2 * i + 1, 0)
                if cur and nxt:
                    rstd_q(i + 1)
                if cur:
                    ctx_rest(2 * i + 1, 1)
                    spread_q(i, 2)
                if prev:
                    pool.wait_ge(dve_up, dve_at(i - 1, "V2"))
                    pool.tensor_tensor(st[:, 9:10], st[:, 8:9], neg_half[:], ALU.pow).then_inc(pool_up, 1)
                if cur:
                    ctx_rest(2 * i + 1, 2)
                    ctx_rest(2 * i + 1, 3)
                    spread_q(i, 3)
                if prev:
                    scan_input(i - 1, 0)
                if cur and nxt:
                    ctx_rest(2 * i + 2, 0)
                if prev:
                    scan_input(i - 1, 1)
                if cur and nxt:
                    ctx_rest(2 * i + 2, 1)
                    spread_q(i + 1, 0)
                if prev:
                    pool.wait_ge(dve_up, dve_at(i - 1, "V3"))
                    pool.tensor_tensor(st[:, 17:18], st[:, 16:17], neg_half[:], ALU.pow).then_inc(pool_up, 1)
                if cur and nxt:
                    ctx_rest(2 * i + 2, 2)
                    ctx_rest(2 * i + 2, 3)
                if prev:
                    after(pool, scattered, 16 * TOPK * (i - 1))
                    pool.tensor_tensor(tokid[:], tokid[:], tile_rows[:], ALU.add).then_inc(tokid_up, 1)
                    pool.wait_ge(tokid_up, 2 * i - 1)
                    pool.wait_ge(dve_up, dve_at(i - 1, "ROUTE"))
                    pool.tensor_tensor(pause_p[:], tile_rows[:], tile_rows[:], ALU.add).then_inc(tokid_up, 1)
                    for t in range(TOPK):
                        pool.indirect_dma_start(
                            dram["table"], bass.IndirectOffsetOnAxis(ap=sc_idx[:, t:t + 1], axis=0),
                            tokid[:], None, bounds_check=E * CAP - 1, oob_is_err=False).then_inc(scattered, 16)

            over_pairs(pool, body)
            pool.wait_ge(scattered, 16 * TOPK * PAIRS)

        @block.tensor
        def _(pe):
            last = [None]

            def take(part, value):
                if last[0] is not None:
                    after(pe, *last[0])
                last[0] = (bank_free[part], value)

            pe.wait_ge(consts, 19)
            for n, rows in enumerate((wq_rows, wp_rows)):
                pe.wait_ge(wq_set, 2 * n + 1)
                for k in range(DT):
                    for o in range(DT):
                        ins = pe.transpose(W[:, (k * DT + o) * P:(k * DT + o + 1) * P],
                                           rows[:, o, k * P:(k + 1) * P], ident[:])
                ins.then_inc(w_mm, 1)
            pe.wait_ge(wq_set, 4)
            pe.wait_ge(wkv_up, 1)
            pe.wait_ge(w_in, 16 * len(loads))

            def turn_x(i):
                take(0, a_at(i, "XQ"))
                pe.wait_ge(lnq_up, i + 1)
                for k in range(DT):
                    ins = pe.transpose(W[:, k * P:(k + 1) * P], lnq[:, k * P:(k + 1) * P], ident[:])
                ins.then_inc(bank_full[0], 1)

            def q_mm(i):
                take(0, a_at(i, "Q"))
                pe.wait_ge(bank_free[0], a_at(i, "XQ"))
                for g in range(2):
                    for k in range(DT):
                        ins = pe.matmul(W[:, g * P:(g + 1) * P], wqT[:, k, g * P:(g + 1) * P], xqT[:, k, :],
                                        start=(k == 0), stop=(k == DT - 1))
                ins.then_inc(bank_full[0], 1)

            def k_mm(i, j, c):
                b, g = divmod(j, 2)
                c0, cn = CHUNKS[c]
                take(0, a_at(i, "K", j, c))
                pe.wait_ge(ctx_up, (2 * i + b) * len(CHUNKS) + c + 1)
                cn += cn % 2
                products = [(w, x, k) for w, x in ((wkv_hi, ctx_hi), (wkv_lo, ctx_hi), (wkv_hi, ctx_lo)) for k in range(DT)]
                for p, (w, x, k) in enumerate(products):
                    ins = pe.matmul(W[:, 0:cn], w[:, k, g * P:(g + 1) * P], x[:, k, c0:c0 + cn],
                                    start=(p == 0), stop=(p == len(products) - 1))
                ins.then_inc(bank_full[0], 1)

            def v_mm(i, b, unit):
                take(0, a_at(i, "V", b, unit))
                chunk = V_UNITS[unit][-1] * P // 512
                pe.wait_ge(ctx_up, (2 * i + b) * len(CHUNKS) + chunk + 1)
                products = [(x, w, k) for k in range(DT) for x, w in ((ctx_hi, wkv_hi), (ctx_hi, wkv_lo), (ctx_lo, wkv_hi))]
                for n, t in enumerate(V_UNITS[unit]):
                    keys = keys_in(t) + keys_in(t) % 2
                    for p, (x, w, k) in enumerate(products):
                        ins = pe.matmul(W[0:keys, n * D:(n + 1) * D], x[:, k, t * P:t * P + keys],
                                        w[:, k, D:2 * D], start=(p == 0), stop=(p == len(products) - 1))
                ins.then_inc(bank_full[0], 1)

            def scores(i, j, s, chunks):
                if chunks[0] == 0:
                    if s == 0:
                        pe.wait_ge(bank_free[0], a_at(i, "K", j, 3))
                        pe.wait_ge(q_up, i * 2 * STEPS + 2 * (j + 1))
                    after(pe, exp_done, i * SLOTS + STRIPS * j + s)
                for c in chunks:
                    c0, cn = CHUNKS[c][0], min(512, MP - CHUNKS[c][0])
                    for n, (lhs, rhs) in enumerate(((Q_hi, K_hi), (Q_hi, K_lo), (Q_lo, K_hi))):
                        rows = slice(2 * DH * s, 2 * DH * (s + 1))
                        ins = pe.matmul(S[:, c0:c0 + cn], lhs[j % 2][rows, :, :].rearrange("p h n -> p (h n)"),
                                        rhs[j % 2][rows, c0:c0 + cn], start=(n == 0), stop=(n == 2))
                if chunks[-1] == len(CHUNKS) - 1:
                    ins.then_inc(s_done, 1)

            def turn(i, j, t):
                n = KT * j + t
                pe.wait_ge(exp_done, i * SLOTS + STRIPS * (j + 1))
                e, count = up_at(*two_before(i, j, t))
                after(pe, t_up[e], count)
                for s in range(STRIPS):
                    ins = pe.transpose(PT[n % 2][0:keys_in(t), s * P:(s + 1) * P],
                                       probs[j % 2][s][:, t * P:t * P + keys_in(t)], ident[:])
                ins.then_inc(t_done, 1)

            def times_v(i, j, t):
                n = KT * j + t
                b, g = divmod(j, 2)
                e, count = up_at(i, j, t)
                pe.wait_ge(t_up[e], count)
                if t == 0:
                    after(pe, o_up, i * STEPS + j)
                    pe.wait_ge(bank_free[0], a_at(i, "V", b, 6))
                for s in range(STRIPS):
                    ins = pe.matmul(O[32 * s:32 * s + 32, 0:P],
                                    V[b][0:keys_in(t), t, g * P + 32 * s:g * P + 32 * s + 32],
                                    probsT[n % 2][0:keys_in(t), s * P:(s + 1) * P],
                                    start=(t == 0), stop=(t == KT - 1))
                ins.then_inc(pv_done, 1)

            def turn_o(i, j):
                part, value = (0, a_at(i, "O", j)) if j < 2 else (1, b_at(i, f"O{j}"))
                take(part, value)
                pe.wait_ge(o_up, i * STEPS + j + 1)
                pe.transpose(W[:, 0:P], OT[:], ident[:]).then_inc(bank_full[part], 1)

            def turn_two(i, name, src, ready, value):
                take(1, b_at(i, name))
                pe.wait_ge(ready, value)
                for k in range(DT):
                    ins = pe.transpose(W[:, k * P:(k + 1) * P], src(k), ident[:])
                ins.then_inc(bank_full[1], 1)

            def rest(i, slot, middle):
                at = (slot, middle)
                if at == (5, False):
                    turn_two(i, "oqT", lambda k: oq[:, k * P:(k + 1) * P], dve_up, dve_at(i, "OQ"))
                if at == (5, True):
                    take(1, b_at(i, "proj"))
                    pe.wait_ge(bank_free[1], b_at(i, "oqT"))
                    for k in range(DT):
                        ins = pe.matmul(W[:, 0:D], oqT[:, k, :], wpT[:, k, :], start=(k == 0), stop=(k == DT - 1))
                    ins.then_inc(bank_full[1], 1)
                if at == (6, False):
                    turn_two(i, "ln2T", lambda k: ln2[:, k * P:(k + 1) * P], dve_up, dve_at(i, "LN2"))
                if at == (6, True):
                    take(1, b_at(i, "xp"))
                    pe.wait_ge(bank_free[1], b_at(i, "ln2T"))
                    for k in range(DT):
                        pe.matmul(W[:, 0:P], xpT[:, k, 0:R], ln2T[:, k, :], start=(k == 0), stop=(k == DT - 1))
                    for k in range(DT):
                        ins = pe.matmul(W[0:2 * NS, P:2 * P], xpT[:, k, R:R + 2 * NS], ln2T[:, k, :],
                                        start=(k == 0), stop=(k == DT - 1))
                    ins.then_inc(bank_full[1], 1)
                if at == (7, False):
                    take(1, b_at(i, "dt"))
                    pe.wait_ge(bank_free[1], b_at(i, "xp"))
                    for h in range(DT):
                        ins = pe.matmul(W[:, h * P:(h + 1) * P], dpT[:, h * P:(h + 1) * P], dlT[:], start=True, stop=True)
                    ins.then_inc(bank_full[1], 1)
                if at == (13, True):
                    turn_two(i, "yT", lambda k: y[:, k, :], dve_up, dve_at(i, "Y1"))
                if at == (14, False):
                    turn_two(i, "ln3T", lambda k: ln3[:, k * P:(k + 1) * P], dve_up, dve_at(i, "LN3"))
                if at == (14, True):
                    take(1, b_at(i, "logits"))
                    pe.wait_ge(bank_free[1], b_at(i, "ln3T"))
                    for k in range(DT):
                        ins = pe.matmul(W[:, 0:E], ln3T[:, k, :], gateT[:, k, :], start=(k == 0), stop=(k == DT - 1))
                    ins.then_inc(bank_full[1], 1)
                if at == (15, False):
                    take(1, b_at(i, "pos"))
                    pe.wait_ge(dve_up, dve_at(i, "SEL"))
                    pe.matmul(W[:, 0:E], before[:], sel[:], start=True, stop=True)
                    pe.matmul(W[:, E:2 * E], ones[:], sel[:], start=True, stop=True).then_inc(bank_full[1], 1)

            turn_x(0)
            q_mm(0)
            for c in range(STRIPS):
                first, second = (v_mm, (0, 0, V_OF_STEP[3][c])), (k_mm, (0, 0, c))
                if c == 3:
                    first, second = second, first
                first[0](*first[1])
                second[0](*second[1])

            def middle(i, slot, cur, prev, nxt):
                if slot == 8 and cur:
                    turn_o(i, 0)
                if slot == 4 and prev:
                    turn_o(i - 1, 3)
                if slot == 11 and cur and nxt:
                    turn_x(i + 1)
                if slot == 12 and cur:
                    turn_o(i, 1)
                if prev:
                    rest(i - 1, slot, True)

            def body(i, cur, prev, nxt):
                last[0] = (bank_free[0], a_at(i, "V", 0, 3)) if cur else (bank_free[1], b_at(i - 2, "pos"))
                for slot in range(SLOTS):
                    j, s, old, tiles, k, v = pieces(i, slot, cur, prev, nxt)
                    if cur:
                        scores(i, j, s, CHUNKS_FIRST)
                    if slot == 1 and prev:
                        turn_o(i - 1, 2)
                    if slot == 12 and cur and nxt:
                        q_mm(i + 1)
                    if prev:
                        rest(i - 1, slot, False)
                    if cur:
                        scores(i, j, s, CHUNKS_LAST)
                    for t in tiles[:2]:
                        turn(*old, t)
                    if k and s == 3:
                        k_mm(*k)
                    if v and s < 3:
                        v_mm(*v)
                    for n, t in enumerate(tiles[:2]):
                        times_v(*old, t)
                        if tiles[n + 2:n + 3]:
                            turn(*old, tiles[n + 2])
                        if n == 0:
                            middle(i, slot, cur, prev, nxt)
                    if not tiles:
                        middle(i, slot, cur, prev, nxt)
                    if k and s < 3:
                        k_mm(*k)
                    if v and s == 3:
                        v_mm(*v)
                    for t in tiles[2:]:
                        times_v(*old, t)

            over_pairs(pe, body)

        @block.scalar
        def _(act):
            act.preload_act_table_set("natural_log_exp_and_others")
            act.wait_ge(w_in, 16 * len(loads))
            act.activation(A[:], A[:], ACT.Exp).then_inc(a_set, 1)
            act.wait_ge(a_set, 1)
            act.mul(A[:], A[:], -1.0).then_inc(a_set, 1)
            act.wait_ge(a_set, 2)

            def k_up(i, j, c):
                g = j % 2
                c0, cn = CHUNKS[c]
                act.wait_ge(bank_full[0], a_at(i, "K", j, c))
                after(act, s_done, i * SLOTS + STRIPS * (j - 1))
                act.activation(K_hi[j % 2][:, c0:c0 + cn], W[:, 0:cn], ACT.Identity,
                               bias=cols[:, BK, g:g + 1]).then_inc(k_hi_up, 1)

            def turned(i, j, t):
                n = KT * j + t
                act.wait_ge(t_done, i * STEPS * KT + n + 1)
                after(act, pv_done, i * STEPS * KT + n - 1)
                act.activation(probsT[n % 2][0:keys_in(t), :], PT[n % 2][0:keys_in(t), :], ACT.Copy).then_inc(t_up[0], 1)

            def soft(i, j, s):
                q = STRIPS * j + s
                act.wait_ge(max_done, i * SLOTS + q + 1)
                after(act, t_done, i * STEPS * KT + KT * (j - 1))
                act.activation(probs[j % 2][s][:], S[:, 0:M], ACT.Exp, bias=negmax[:, q:q + 1],
                               accum_out=den[:, q:q + 1]).then_inc(exp_done, 1)

            def o_up_(i, j):
                act.wait_ge(pv_done, i * STEPS * KT + KT * (j + 1))
                if j == 0:
                    after(act, bank_full[1], b_at(i - 1, "O3"))
                elif j == 3:
                    act.wait_ge(bank_full[1], b_at(i, "O2"))
                else:
                    act.wait_ge(bank_full[0], a_at(i, "O", j - 1))
                act.activation(OT[:], O[:, 0:P], ACT.Copy).then_inc(o_up, 1)

            def rest(i, slot):
                if slot == 7:
                    act.wait_ge(dve_up, dve_at(i, "EZ"))
                    act.activation(lz, ez1, ACT.Ln).then_inc(act_up, 1)
                for part in DECAYS.get(slot, []):
                    decay(i, *part)

            def decay(i, h, half, first, end):
                if first == 0:
                    act.wait_ge(dve_up, dve_at(i, "U" if h == 0 else f"S0{half}"))
                for n in range(first, end):
                    m = half * (NS // 2) + n
                    ins = act.activation(abar[half][:, n, :], dt_[:, h, :], ACT.Exp, scale=A[:, h, m:m + 1])
                if end == NS // 2:
                    ins.then_inc(act_up, 1)

            def ctx_round(batch, c, pair=None, step=None):
                c0, cn = CHUNKS[c]
                act.wait_ge(ctx_in[c], 16 * (batch + 1))
                if pair is not None:
                    act.wait_ge(bank_full[0], a_at(pair, "K", step, c))
                act.activation(ctx_hi[:, :, c0:c0 + cn], ctx_new[:, :, 0:cn], ACT.Copy)\
                   .then_inc(ctx_hi_up, 1)

            act.activation(wkv_hi[:], wkv_in[:], ACT.Copy).then_inc(wkv_hi_up, 1)
            for c in range(len(CHUNKS)):
                ctx_round(0, c)
            for c in range(4):
                k_up(0, 0, c)

            def body(i, cur, prev, nxt):
                for slot in range(SLOTS):
                    j, s, old, tiles, k, v = pieces(i, slot, cur, prev, nxt)
                    last_k, _ = left_over(i, slot, cur, prev, nxt)
                    if last_k:
                        k_up(*last_k)
                    if slot % 4 == 0 and (prev if slot < 8 else cur):
                        o_up_(*((i - 1, 2), (i - 1, 3), (i, 0), (i, 1))[j])
                    for t in tiles[:1]:
                        turned(*old, t)
                    if k and s == 3:
                        k_up(*k)
                    if cur:
                        soft(i, j, s)
                    if slot == 7 and prev:
                        act.wait_ge(dve_up, dve_at(i - 1, "Z"))
                        act.activation(ez, negz, ACT.Exp).then_inc(act_up, 1)
                    for t in tiles[2:3]:
                        turned(*old, t)
                    if slot == 14 and prev:
                        act.wait_ge(dve_up, dve_at(i - 1, "LOGITS"))
                        act.activation(pr[:], W[:, 0:E], ACT.Exp, bias=st[:, 24:25], accum_out=st[:, 25:26])\
                           .then_inc(bank_free[1], 1)
                    if prev:
                        rest(i - 1, slot)
                    if cur and slot in CTX_SLOTS:
                        ctx_round(2 * i + 1, CTX_SLOTS.index(slot), i, 1)
                    if cur and nxt and slot - 8 in CTX_SLOTS:
                        ctx_round(2 * i + 2, CTX_SLOTS.index(slot - 8), i, 3)

            over_pairs(act, body)

        @block.vector
        def _(dve):
            def scale_of(link, rows, s0):
                link(dve.tensor_reduce(st[:, s0:s0 + 1], rows, AX.X, ALU.max, apply_absolute_value=True))
                link(dve.tensor_scalar(st[:, s0:s0 + 1], st[:, s0:s0 + 1], 1.0 / 127.0, 1e-8, ALU.mult, ALU.max))
                link(dve.reciprocal(st[:, s0 + 1:s0 + 2], st[:, s0:s0 + 1]))

            def quantise(link, out, rows, s0):
                scale_of(link, rows, s0)
                link(dve.tensor_scalar(out, rows, st[:, s0 + 1:s0 + 2], MAGIC, ALU.mult, ALU.add))
                link(dve.tensor_scalar(out, out, MAGIC, 127.0, ALU.subtract, ALU.min))
                return dve.tensor_scalar(out, out, -127.0, st[:, s0:s0 + 1], ALU.max, ALU.mult)

            def moments(link, x, s0, bn0):
                link.carried(dve.bn_stats(st[:, bn0:bn0 + 6], x))
                link(dve.bn_aggr(st[:, bn0 + 6:bn0 + 8], st[:, bn0:bn0 + 6]))
                return dve.tensor_scalar(st[:, s0:s0 + 1], st[:, bn0 + 7:bn0 + 8], EPS, None, ALU.add)

            dve.wait_ge(w_in, 16 * len(loads))
            link = Chain(dve, dve_w, 0, 22)
            for rows, wT in ((wq_rows, wqT), (wp_rows, wpT)):
                for k in range(DT):
                    ins = quantise(link, rows[:, k, :], rows[:, k, :], 28)
                    if k == 0:
                        link(ins)
                ins.then_inc(wq_set, 1)
                dve.wait_ge(w_mm, 1 if rows is wq_rows else 2)
                dve.tensor_copy(wT[:].rearrange("p k o -> p (k o)"), W[:]).then_inc(wq_set, 1)
            dve.wait_ge(wq_set, 4)

            def norm_q(i):
                link = Chain(dve, dve_q, i, 9, pause_q[:])
                dve.wait_ge(x_in, 16 * (i + 1))
                moments(link, x_q[:], 0, 32).then_inc(var_up, 1)
                dve.wait_ge(rstd_up, i + 1)
                link(dve.tensor_scalar(lnq[:], x_q[:], st[:, 38:39], st[:, 1:2], ALU.subtract, ALU.mult))
                quantise(link, lnq[:], lnq[:], 2).then_inc(lnq_up, 1)

            def x_up(i):
                dve.wait_ge(bank_full[0], a_at(i, "XQ"))
                dve.tensor_copy(xqT[:].rearrange("p k t -> p (k t)"), W[:, 0:D]).then_inc(bank_free[0], 1)

            def q_out(i):
                dve.wait_ge(bank_full[0], a_at(i, "Q"))
                after(dve, q_up, i * 2 * STEPS)
                dve.tensor_scalar(q_f[:, 0, :], W[:, 0:P], cols[:, BQ, 0:1], DH ** -0.5, ALU.add, ALU.mult)\
                   .then_inc(dve_q2, 1)
                dve.tensor_scalar(q_f[:, 1, :], W[:, P:2 * P], cols[:, BQ, 1:2], DH ** -0.5, ALU.add, ALU.mult)\
                   .then_inc(bank_free[0], 1)

            def split_q(i):
                dve.wait_ge(dve_q2, 2 * i + 1)
                dve.wait_ge(bank_free[0], a_at(i, "Q"))
                dve.tensor_copy(q_hi[:].bitcast(F32R), q_f[:]).then_inc(dve_q2, 1)
                dve.wait_ge(dve_q2, 2 * i + 2)
                dve.tensor_tensor(q_lo[:], q_f[:], q_hi[:], ALU.subtract).then_inc(q_split, 1)

            def k_low(i, j, c):
                g = j % 2
                c0, cn = CHUNKS[c]
                dve.wait_ge(k_hi_up, (i * STEPS + j) * STRIPS + c + 1)
                dve.scalar_tensor_tensor(K_lo[j % 2][:, c0:c0 + cn], W[:, 0:cn], cols[:, BK, g:g + 1],
                                         K_hi[j % 2][:, c0:c0 + cn].bitcast(F32), ALU.add, ALU.subtract)\
                   .then_inc(bank_free[0], 1)

            def v_up(i, b, unit):
                tiles = V_UNITS[unit]
                dve.wait_ge(bank_full[0], a_at(i, "V", b, unit))
                after(dve, pv_done, (i - 1) * STEPS * KT + 2 * KT * (b + 1))
                dve.tensor_copy(V[b][0:keys_in(tiles[-1]), tiles[0]:tiles[-1] + 1, :].rearrange("p t d -> p (t d)"),
                                W[0:keys_in(tiles[-1]), 0:len(tiles) * D]).then_inc(bank_free[0], 1)

            def strip_max(i, j, s):
                q = STRIPS * j + s
                dve.wait_ge(s_done, i * SLOTS + q + 1)
                dve.tensor_reduce(negmax[:, q:q + 1], S[:, 0:M], AX.X, ALU.max, negate=True).then_inc(max_done, 1)

            def turned(i, j, t):
                n = KT * j + t
                dve.wait_ge(t_done, i * STEPS * KT + n + 1)
                after(dve, pv_done, i * STEPS * KT + n - 1)
                dve.tensor_copy(probsT[n % 2][0:keys_in(t), :], PT[n % 2][0:keys_in(t), :]).then_inc(t_up[1], 1)

            def norm_o(i, j):
                b, g = divmod(j, 2)
                link = Chain(dve, dve_o, i * STEPS + j, 1)
                part, value = (0, a_at(i, "O", j)) if j < 2 else (1, b_at(i, f"O{j}"))
                rd = rden[:, STRIPS * j:STRIPS * (j + 1)]
                dve.wait_ge(exp_done, i * SLOTS + STRIPS * (j + 1))
                link(dve.reciprocal(rd, den[:, STRIPS * j:STRIPS * (j + 1)]))
                dve.wait_ge(bank_full[part], value)
                for h in range(2):
                    rows = slice(h * N, (h + 1) * N)
                    ins = dve.tensor_tensor(
                        o_tok[b * N:(b + 1) * N, g * P:(g + 1) * P].rearrange("n (s h d) -> n s h d", h=2, d=DH)[:, :, h, :],
                        W[rows, 0:P].rearrange("n (s h d) -> n s h d", h=2, d=DH)[:, :, h, :],
                        rd[rows, :].unsqueeze(2).to_broadcast([N, STRIPS, DH]), ALU.mult)
                ins.then_inc(bank_free[part], 1)
                link.end()

            def copy_out(i, name, dst, src):
                dve.wait_ge(bank_full[1], b_at(i, name))
                dve.tensor_copy(dst, src).then_inc(bank_free[1], 1)

            def empty(i, slot, middle, link):
                at = (slot, middle)
                if at == (5, False):
                    copy_out(i, "oqT", oqT[:].rearrange("p k t -> p (k t)"), W[:, 0:D])
                if at == (5, True):
                    dve.wait_ge(xr_in, 16 * (i + 1))
                    link(dve.tensor_tensor(x_res[:], x_res[:], bp_row[:], ALU.add))
                    after(dve, x3_out, 32 * i)
                    dve.wait_ge(bank_full[1], b_at(i, "proj"))
                    dve.tensor_tensor(x2[:], W[:, 0:D], x_res[:], ALU.add).then_inc(bank_free[1], 1)
                if at == (6, False):
                    copy_out(i, "ln2T", ln2T[:].rearrange("p k t -> p (k t)"), W[:, 0:D])
                if at == (6, True):
                    after(dve, bc_out, 16 * i)
                    dve.wait_ge(bank_full[1], b_at(i, "xp"))
                    link(dve.tensor_copy(dlT[:], W[:, 0:P]))
                    dve.tensor_copy(BCT[:], W[0:2 * NS, P:2 * P]).then_inc(bank_free[1], 1)
                if at == (7, False):
                    dve.wait_ge(bank_full[1], b_at(i, "dt"))
                    link(dve.tensor_scalar(z[:, 0, :], W[:, 0:P], cols[:, DTB, 0:1], None, ALU.add))
                    dve.tensor_scalar(z[:, 1, :], W[:, P:2 * P], cols[:, DTB, 1:2], None, ALU.add).then_inc(bank_free[1], 1)
                if at == (13, True):
                    dve.wait_ge(bank_full[1], b_at(i, "yT"))
                    dve.tensor_tensor(x3[:], W[:, 0:D], x2[:], ALU.add).then_inc(bank_free[1], 1)
                if at == (14, False):
                    copy_out(i, "ln3T", ln3T[:].rearrange("p k t -> p (k t)"), W[:, 0:D])
                if at == (14, True):
                    dve.wait_ge(bank_full[1], b_at(i, "logits"))
                    dve.tensor_reduce(st[:, 24:25], W[:, 0:E], AX.X, ALU.max, negate=True).then_inc(dve_up, 1)
                if at == (15, False):
                    dve.wait_ge(bank_full[1], b_at(i, "pos"))
                    link(dve.tensor_tensor(slotv[:], W[:, 0:E], base_e[:], ALU.add))
                    dve.tensor_tensor(base_e[:], W[:, E:2 * E], base_e[:], ALU.add).then_inc(bank_free[1], 1)

            def states(half):
                return slice(half * (NS // 2), (half + 1) * (NS // 2))

            def scan(i, h, half, link):
                dve.wait_ge(act_up, act_at(i, f"AB{h}{half}"))
                link(dve.memset(abar[half].rearrange("p n (b t) -> p n b t", b=2)[:, :, :, 0:1], 0.0))
                dve.wait_ge(pool_up, pool_at(i, f"BX{h}{half}"))
                flat = bx[:, states(half), :].rearrange("p n t -> p (n t)")
                dve.tensor_tensor_scan(flat, abar[half].rearrange("p n t -> p (n t)"), flat, 0.0,
                                       ALU.mult, ALU.add).then_inc(dve_up, 1)

            def times_c(i, h, half, link):
                dve.wait_ge(dve_up, dve_at(i, f"S{h}{half}"))
                mine = bx[:, states(half), :]
                link(dve.tensor_tensor(mine, mine, BC[:, NS:2 * NS, :][:, states(half), :], ALU.mult))

            def sum_states(i, h, half, link):
                part = (y, oqT)[half][:, h, :]
                mine = bx[:, states(half), :]
                link(dve.tensor_reduce(part, mine.rearrange("p n t -> p t n"), AX.X, ALU.add))
                if half == 0:
                    dve.scalar_tensor_tensor(part, ln2T[:, h, :], cols[:, DP, h:h + 1], part, ALU.mult, ALU.add)\
                       .then_inc(dve_y, 1)
                else:
                    dve.wait_ge(dve_y, i * DT + h + 1)
                    dve.tensor_tensor(y[:, h, :], y[:, h, :], part, ALU.add).then_inc(dve_up, 1)

            def rest(i, slot, link):
                def up(ins):
                    ins.then_inc(dve_up, 1)

                if slot == 4:
                    dve.wait_ge(bank_free[1], b_at(i, "O3"))
                    link(dve.tensor_tensor(oq[:], o_tok[:], bv_row[:], ALU.add))
                    up(quantise(link, oq[:], oq[:], 4))
                if slot == 5:
                    dve.wait_ge(bank_free[1], b_at(i, "proj"))
                    up(dve.bn_stats(st[:, 40:46], x2[:]))
                    dve.wait_ge(dve_up, dve_at(i, "X2"))
                    link.carried()
                    link(dve.bn_aggr(st[:, 46:48], st[:, 40:46]))
                    up(dve.tensor_scalar(st[:, 8:9], st[:, 47:48], EPS, None, ALU.add))
                    dve.wait_ge(pool_up, pool_at(i, "R2"))
                    up(dve.tensor_scalar(ln2[:], x2[:], st[:, 46:47], st[:, 9:10], ALU.subtract, ALU.mult))
                if slot == 7:
                    dve.wait_ge(act_up, act_at(i, "EXPZ"))
                    up(dve.tensor_scalar(ez1, ez, 1.0, None, ALU.add))
                    dve.wait_ge(dve_up, dve_at(i, "EZ"))
                    link(dve.scalar_tensor_tensor(negz, ez1, 1.0, ez, ALU.subtract, ALU.subtract))
                    dve.wait_ge(act_up, act_at(i, "LNZ"))
                    link(dve.tensor_tensor(negz, lz, negz, ALU.subtract))
                    link(dve.scalar_tensor_tensor(dt_[:], z[:], 0.0, negz, ALU.max, ALU.add))
                    up(dve.tensor_tensor(u[:], dt_[:], ln2T[:], ALU.mult))
                for step, h, half in {8: [(scan, 0, 0), (times_c, 0, 0)],
                                      9: [(sum_states, 0, 0), (scan, 0, 1)],
                                      10: [(times_c, 0, 1), (sum_states, 0, 1), (scan, 1, 0)],
                                      11: [(times_c, 1, 0), (sum_states, 1, 0), (scan, 1, 1)],
                                      12: [(times_c, 1, 1), (sum_states, 1, 1)]}.get(slot, []):
                    step(i, h, half, link)
                if slot == 13:
                    dve.wait_ge(bank_free[1], b_at(i, "yT"))
                    up(moments(link, x3[:], 16, 48))
                    dve.wait_ge(pool_up, pool_at(i, "R3"))
                    up(dve.tensor_scalar(ln3[:], x3[:], st[:, 54:55], st[:, 17:18], ALU.subtract, ALU.mult))
                if slot == 14:
                    dve.wait_ge(bank_free[1], b_at(i, "logits"))
                    link(dve.reciprocal(st[:, 26:27], st[:, 25:26]))
                    link.carried(dve.tensor_scalar(pr[:], pr[:], st[:, 26:27], None, ALU.mult))
                    link.carried(dve.max(top[:], pr[:]))
                    link.carried(dve.max_index(topi[:], top[:], pr[:]))
                    link(dve.match_replace(pr2[:], top[:], pr[:], -1.0))
                    up(dve.tensor_scalar(sel[:], pr2[:], 0.0, None, ALU.is_lt))
                if slot == 15:
                    idx, slot_, pos, ok, low, out_ = (topf[:, n, :] for n in range(6))
                    link(dve.tensor_copy(idx, topi[:]))
                    for t in range(TOPK):
                        ins = dve.scalar_tensor_tensor(junk[:, t], iota_e[:], idx[:, t:t + 1], slotv[:], ALU.is_equal,
                                                       ALU.mult, accum_out=slot_[:, t:t + 1])
                    link(ins)
                    link(dve.scalar_tensor_tensor(pos, idx, -float(CAP), slot_, ALU.mult, ALU.add))
                    link(dve.tensor_scalar(ok, pos, float(CAP), None, ALU.is_lt))
                    link(dve.tensor_tensor(scores_all[:, bass.ds(i * TOPK, TOPK)], top[:], ok, ALU.mult))
                    link(dve.tensor_scalar(low, pos, float(CAP - 1), None, ALU.min))
                    link(dve.scalar_tensor_tensor(low, idx, float(CAP), low, ALU.mult, ALU.add))
                    link(dve.tensor_copy(slots_all[:, bass.ds(i * TOPK, TOPK)], low))
                    link(dve.tensor_scalar(out_, ok, -float(2 * E * CAP), float(2 * E * CAP), ALU.mult, ALU.add))
                    link(dve.tensor_tensor(out_, out_, slot_, ALU.add))
                    after(dve, scattered, 16 * TOPK * i)
                    up(dve.tensor_copy(sc_idx[:], out_))

            norm_q(0)
            x_up(0)
            q_out(0)
            split_q(0)
            for c in range(STRIPS):
                if c < 3:
                    v_up(0, 0, V_OF_STEP[3][c])
                k_low(0, 0, c)

            def body(i, cur, prev, nxt):
                link = Chain(dve, dve_b, i - 1, B_LINKS, pause[:])
                for slot in range(SLOTS):
                    j, s, old, tiles, k, v = pieces(i, slot, cur, prev, nxt)
                    last_k, last_v = left_over(i, slot, cur, prev, nxt)
                    if last_k:
                        k_low(*last_k)
                    if last_v:
                        v_up(*last_v)
                    if slot == 1 and prev:
                        norm_o(i - 1, 2)
                    if slot == 12 and cur and nxt:
                        q_out(i + 1)
                    if prev:
                        empty(i - 1, slot, False, link)
                    if cur:
                        strip_max(i, j, s)
                    for t in tiles[1:2]:
                        turned(*old, t)
                    if slot == 7 and prev:
                        dve.wait_ge(bank_free[1], b_at(i - 1, "dt"))
                        dve.scalar_tensor_tensor(negz, z[:], -1.0, z[:], ALU.mult, ALU.min).then_inc(dve_up, 1)
                    if k and s == 3:
                        k_low(*k)
                    if v and s < 3:
                        v_up(*v)
                    if slot == 8 and cur:
                        norm_o(i, 0)
                    if slot == 4 and prev:
                        norm_o(i - 1, 3)
                    if slot == 11 and cur and nxt:
                        x_up(i + 1)
                    if slot == 12 and cur:
                        norm_o(i, 1)
                    if slot == 12 and cur and nxt:
                        split_q(i + 1)
                    if prev:
                        empty(i - 1, slot, True, link)
                    for t in tiles[3:4]:
                        turned(*old, t)
                    if prev:
                        rest(i - 1, slot, link)
                    if slot == 2 and cur and nxt:
                        norm_q(i + 1)
                if prev:
                    link.end()

            over_pairs(dve, body)


def expert_phase(nc, io, dram):
    with ExitStack() as ctx:
        def sb(name, shape, dt=F32):
            return ctx.enter_context(nc.sbuf_tensor("sb_" + name, shape, dt))

        def sem(name):
            return ctx.enter_context(nc.semaphore(name))

        ident = sb("ident2", [P, P])
        pause = sb("pause2", [P, 1])
        table = sb("table_sb", [E, CAP])
        idx_all = sb("idx_all", [P, E * CT], U32)
        idx = [sb(f"idx{n}", [P, CT], U32) for n in range(2)]
        xg = [[sb(f"xg{n}_{c}", [P, D]) for c in range(CT)] for n in range(2)]
        wgu = [sb(f"wgu{n}", [P, DT, 2 * FF]) for n in range(2)]
        wd = [sb(f"wd{n}", [FF, D]) for n in range(2)]
        w_hi, w_lo = ([sb(f"w_{m}{n}", [P, DT, 2 * FF], F32R) for n in range(2)] for m in ("hi", "lo"))
        x_hi, x_lo = ([sb(f"x_{m}{n}", [P, DT, CAP], F32R) for n in range(2)] for m in ("hi", "lo"))
        sg = sb("sg", [FF, CAP])
        hid = [sb(f"hid{n}", [FF, CAP]) for n in range(2)]
        ys = [sb(f"ys{n}", [P, CT, D]) for n in range(2)]
        XT = [ctx.enter_context(nc.psum_tensor(f"XT{k}", [P, CAP], F32)) for k in range(DT)]
        G = ctx.enter_context(nc.psum_tensor("G", [P, CAP], F32))
        U = ctx.enter_context(nc.psum_tensor("U", [P, CAP], F32))
        Y = [ctx.enter_context(nc.psum_tensor(f"Y{k}", [P, 2, D], F32)) for k in range(2)]

        e_const = sem("e_const")
        tab_in = sem("tab_in")
        tab_t = sem("tab_t")
        tab_up = sem("tab_up")
        wgu_in = [sem(f"wgu_in{n}") for n in range(2)]
        wd_in = [sem(f"wd_in{n}") for n in range(2)]
        w_hi_up = sem("w_hi_up")
        w_lo_up = sem("w_lo_up")
        idx_up = sem("idx_up")
        x_in = [sem(f"ex_in{n}") for n in range(2)]
        xt_done = sem("xt_done")
        x_hi_up = sem("x_hi_up")
        x_lo_up = sem("x_lo_up")
        g_done = sem("g_done")
        gu_done = sem("gu_done")
        sg_up = sem("sg_up")
        hid_up = sem("hid_up")
        y_done = sem("y_done")
        y_up = [sem("y_up_act"), sem("y_up_dve")]
        y_out = [sem(f"y_out{n}") for n in range(2)]
        block = ctx.enter_context(nc.Block())

        def over_experts(eng, body):
            for e in range(2):
                body(e, e)
            with eng.Fori(1, E // 2 - 1) as two:
                for n in range(2):
                    body(2 * two + n, n)
            for e in range(E - 2, E):
                body(e, e % 2)

        def first(e):
            return isinstance(e, int) and e == 0

        def last(e):
            return isinstance(e, int) and e == E - 1

        def early(e):
            return isinstance(e, int) and e < 2

        def in_count(e, n, each=16):
            return (e - n) * (each // 2) + each

        @block.sync
        def _(sp):
            sp.dma_start(table[:], dram["table"].rearrange("(e c) o -> e (c o)", e=E)).then_inc(tab_in, 16)

            def load_gu(e, n):
                after(sp, w_lo_up, e - 1)
                sp.dma_start(wgu[n][:], io["wgu"][bass.ds(e, 1)].rearrange("o (k p) f -> p (o k) f", p=P)).then_inc(wgu_in[n], 16)

            def store(e, n):
                for m in range(2):
                    sp.wait_ge(y_up[m], e + 1)
                sp.dma_start(dram["y"][bass.ds(e * CAP, CAP), :].rearrange("(c p) d -> p c d", p=P), ys[n][:]).then_inc(y_out[n], 16)

            def body(e, n):
                if not last(e):
                    load_gu(e + 1, 1 - n)
                after(sp, y_done, e - 1)
                sp.dma_start(wd[n][:], io["wdT"][bass.ds(e, 1)].rearrange("o f d -> (o f) d")).then_inc(wd_in[n], 16)
                if not early(e):
                    store(e - 2, n)

            load_gu(0, 0)
            over_experts(sp, body)
            for e in range(E - 2, E):
                store(e, e % 2)
            for n in range(2):
                sp.wait_ge(y_out[n], 16 * (E // 2))

        @block.gpsimd
        def _(pool):
            pool.memset(ident[:], 0.0).then_inc(e_const, 1)
            pool.wait_ge(e_const, 1)
            pool.affine_select(out=ident[:], in_=ident[:], compare_op=ALU.not_equal, fill=1.0, base=0,
                               pattern=[[-1, P]], channel_multiplier=1).then_inc(e_const, 1)
            pool.wait_ge(e_const, 2)
            pool.wait_ge(tab_up, 1)

            def body(e, n):
                if not early(e):
                    pool.wait_ge(x_in[n], in_count(e, n, 16 * CT) - 16 * CT)
                    pool.wait_ge(xt_done, DT * (e - 1))
                after(pool, idx_up, 2 * e)
                pool.tensor_copy(idx[n][:], idx_all[:, bass.ds(e * CT, CT)]).then_inc(idx_up, 1)
                pool.wait_ge(idx_up, 2 * e + 1)
                pool.tensor_tensor(pause[:], ident[:, 0:1], ident[:, 0:1], ALU.add).then_inc(idx_up, 1)
                for c in range(CT):
                    pool.indirect_dma_start(xg[n][c][:], None, dram["ln3"],
                                            bass.IndirectOffsetOnAxis(ap=idx[n][:, c:c + 1], axis=0)).then_inc(x_in[n], 16)

            over_experts(pool, body)

        @block.tensor
        def _(pe):
            def turn(e, n):
                pe.wait_ge(x_in[n], in_count(e, n, 16 * CT))
                after(pe, x_lo_up, DT * e)
                for k in range(DT):
                    for c in range(CT):
                        ins = pe.transpose(XT[k][:, c * P:(c + 1) * P], xg[n][c][:, k * P:(k + 1) * P], ident[:])
                    ins.then_inc(xt_done, 1)

            def gate_up(e, n):
                pe.wait_ge(w_lo_up, e + 1)
                pe.wait_ge(x_lo_up, DT * (e + 1))
                after(pe, hid_up, e)
                for m, (dst, done) in enumerate(((G, g_done), (U, gu_done))):
                    products = [(w, x, k) for w, x in ((w_hi, x_hi), (w_lo, x_hi), (w_hi, x_lo)) for k in range(DT)]
                    for p, (w, x, k) in enumerate(products):
                        ins = pe.matmul(dst[0:FF, :], w[n][:, k, m * FF:(m + 1) * FF], x[n][:, k, :],
                                        start=(p == 0), stop=(p == len(products) - 1))
                    ins.then_inc(done, 1)

            def down(e, n):
                pe.wait_ge(hid_up, e + 1)
                pe.wait_ge(wd_in[n], in_count(e, n))
                for m in range(2):
                    after(pe, y_up[m], e)
                for c in range(CT):
                    ins = pe.matmul(Y[c // 2][:, c % 2, :], hid[n][:, c * P:(c + 1) * P], wd[n][:], start=True, stop=True)
                ins.then_inc(y_done, 1)

            pe.wait_ge(e_const, 2)
            pe.wait_ge(tab_in, 16)
            for c in range(CT):
                ins = pe.transpose(Y[0][:, 0, c * E:(c + 1) * E], table[:, c * P:(c + 1) * P], ident[0:E, 0:E])
            ins.then_inc(tab_t, 1)
            pe.wait_ge(tab_up, 1)
            turn(0, 0)

            def body(e, n):
                gate_up(e, n)
                if not last(e):
                    turn(e + 1, 1 - n)
                if not first(e):
                    down(e - 1, 1 - n)

            over_experts(pe, body)
            down(E - 1, (E - 1) % 2)

        @block.scalar
        def _(act):
            def split(e, n):
                act.wait_ge(wgu_in[n], in_count(e, n))
                after(act, gu_done, e - 1)
                act.activation(w_hi[n][:], wgu[n][:], ACT.Copy).then_inc(w_hi_up, 1)
                for k in range(DT):
                    act.wait_ge(xt_done, DT * e + k + 1)
                    act.activation(x_hi[n][:, k, :], XT[k][:], ACT.Copy).then_inc(x_hi_up, 1)

            def out(e, n):
                act.wait_ge(y_done, e + 1)
                if not early(e):
                    act.wait_ge(y_out[n], (e - n) * 8)
                act.activation(ys[n][:, 0:2, :], Y[0][:], ACT.Copy).then_inc(y_up[0], 1)

            def body(e, n):
                act.wait_ge(g_done, e + 1)
                after(act, hid_up, e)
                act.activation(sg[:], G[0:FF, :], ACT.Silu).then_inc(sg_up, 1)
                if not last(e):
                    split(e + 1, 1 - n)
                if not first(e):
                    out(e - 1, 1 - n)

            split(0, 0)
            over_experts(act, body)
            out(E - 1, (E - 1) % 2)

        @block.vector
        def _(dve):
            dve.wait_ge(tab_t, 1)
            dve.tensor_copy(idx_all[:].rearrange("p (e c) -> p c e", c=CT),
                            Y[0][:, 0, 0:CT * E].rearrange("p (c e) -> p c e", c=CT)).then_inc(tab_up, 1)

            def split(e, n):
                dve.wait_ge(w_hi_up, e + 1)
                dve.tensor_tensor(w_lo[n][:], wgu[n][:], w_hi[n][:].bitcast(F32), ALU.subtract).then_inc(w_lo_up, 1)
                for k in range(DT):
                    dve.wait_ge(x_hi_up, DT * e + k + 1)
                    dve.tensor_tensor(x_lo[n][:, k, :], XT[k][:], x_hi[n][:, k, :].bitcast(F32), ALU.subtract)\
                       .then_inc(x_lo_up, 1)

            def out(e, n):
                dve.wait_ge(y_done, e + 1)
                if not early(e):
                    dve.wait_ge(y_out[n], (e - n) * 8)
                dve.tensor_copy(ys[n][:, 2:4, :], Y[1][:]).then_inc(y_up[1], 1)

            def body(e, n):
                dve.wait_ge(gu_done, e + 1)
                dve.wait_ge(sg_up, e + 1)
                after(dve, y_done, e - 1)
                dve.tensor_tensor(hid[n][:], U[0:FF, :], sg[:], ALU.mult).then_inc(hid_up, 1)
                if not last(e):
                    split(e + 1, 1 - n)
                if not first(e):
                    out(e - 1, 1 - n)

            split(0, 0)
            over_experts(dve, body)
            out(E - 1, (E - 1) % 2)


def combine_phase(nc, io, dram, out):
    with ExitStack() as ctx:
        def sb(name, shape, dt=F32):
            return ctx.enter_context(nc.sbuf_tensor("sb_" + name, shape, dt))

        def sem(name):
            return ctx.enter_context(nc.semaphore(name))

        pause = sb("pause3", [P, 1])
        zeros = sb("zeros", [P, 1])
        acc = [sb(f"acc{n}", [P, D]) for n in range(2)]
        yg = [[sb(f"yg{n}_{t}", [P, D]) for t in range(TOPK)] for n in range(2)]
        idx = [sb(f"cidx{n}", [P, TOPK], U32) for n in range(2)]
        sc = [sb(f"csc{n}", [P, TOPK]) for n in range(2)]
        x_in = [sem(f"cx_in{n}") for n in range(2)]
        idx_up = sem("cidx_up")
        zero_up = sem("zero_up")
        y_in = [sem(f"cy_in{n}") for n in range(2)]
        sc_up = sem("csc_up")
        acc_up = sem("acc_up")
        o_out = [sem(f"o_out{n}") for n in range(2)]
        block = ctx.enter_context(nc.Block())

        def over_tiles(eng, body):
            for i in range(2):
                body(i, i)
            with eng.Fori(1, PAIRS // 2) as two:
                for n in range(2):
                    body(2 * two + n, n)

        @block.sync
        def _(sp):
            def load(i, n):
                if not (isinstance(i, int) and i < 2):
                    sp.wait_ge(o_out[n], (i - n) * 8)
                sp.dma_start(acc[n][:], dram["x3"][bass.ds(i * P, P), :]).then_inc(x_in[n], 16)

            def body(i, n):
                load(i, n)
                sp.wait_ge(acc_up, TOPK * (i + 1))
                sp.dma_start(out[bass.ds(i * P, P), :], acc[n][:]).then_inc(o_out[n], 16)

            over_tiles(sp, body)
            for n in range(2):
                sp.wait_ge(o_out[n], 16 * (PAIRS // 2))

        @block.gpsimd
        def _(pool):
            pool.memset(zeros[:], 0.0).then_inc(zero_up, 1)
            pool.wait_ge(zero_up, 1)

            def body(i, n):
                if not (isinstance(i, int) and i < 2):
                    pool.wait_ge(y_in[n], (i - n) * (8 * TOPK))
                    pool.wait_ge(acc_up, TOPK * (i - 1))
                after(pool, idx_up, 2 * i)
                pool.tensor_copy(idx[n][:], dram["slots_sb"][:, bass.ds(i * TOPK, TOPK)]).then_inc(idx_up, 1)
                pool.wait_ge(idx_up, 2 * i + 1)
                pool.tensor_tensor(pause[:], zeros[:], zeros[:], ALU.add).then_inc(idx_up, 1)
                for t in range(TOPK):
                    pool.indirect_dma_start(yg[n][t][:], None, dram["y"],
                                            bass.IndirectOffsetOnAxis(ap=idx[n][:, t:t + 1], axis=0)).then_inc(y_in[n], 16)

            over_tiles(pool, body)

        @block.vector
        def _(dve):
            def body(i, n):
                dve.tensor_copy(sc[n][:], dram["scores_sb"][:, bass.ds(i * TOPK, TOPK)]).then_inc(sc_up, 1)
                dve.wait_ge(sc_up, i + 1)
                dve.wait_ge(x_in[n], (i - n) * 8 + 16)
                dve.wait_ge(y_in[n], (i - n) * (8 * TOPK) + 16 * TOPK)
                for t in range(TOPK):
                    dve.scalar_tensor_tensor(acc[n][:], yg[n][t][:], sc[n][:, t:t + 1], acc[n][:], ALU.mult, ALU.add)\
                       .then_inc(acc_up, 1)
                    dve.wait_ge(acc_up, i * TOPK + t + 1)

            over_tiles(dve, body)


def perceiver(nc, ins, out):
    with ExitStack() as ctx:
        dram = {
            "bc": nc.dram_tensor("bc_scratch", (2 * NS, P), F32).ap(),
            "x3": nc.dram_tensor("x3_scratch", (TOK, D), F32).ap(),
            "ln3": nc.dram_tensor("ln3_scratch", (TOK, D), F32).ap(),
            "table": nc.dram_tensor("table_scratch", (E * CAP, 1), F32).ap(),
            "y": nc.dram_tensor("y_scratch", (E * CAP, D), F32).ap(),
            "slots_sb": ctx.enter_context(nc.sbuf_tensor("slots_all", [P, PAIRS * TOPK], U32)),
            "scores_sb": ctx.enter_context(nc.sbuf_tensor("scores_all", [P, PAIRS * TOPK], F32)),
        }
        mixer_phase(nc, ins, dram)
        expert_phase(nc, ins, dram)
        combine_phase(nc, ins, dram, out)


def laid_out(inputs):
    a = {k: np.asarray(v) for k, v in inputs.items()}

    def cols(v):
        return v.reshape(DT, P).T

    x = a["x"]
    return {
        "x": x.reshape(TOK, D),
        "ctxT": a["ctx_2048"].transpose(0, 2, 1),
        "wq": a["L0_xattn_wq"], "bq": cols(a["L0_xattn_bq"]),
        "wkvT": a["L0_xattn_wkv"].T,
        "bk": cols(a["L0_xattn_bkv"][:D]), "bv": a["L0_xattn_bkv"][D:],
        "wp": a["L0_xattn_wp"], "bp": a["L0_xattn_bp"],
        "xpT": a["L0_attn_x_proj_w"].T, "dpT": a["L0_attn_dt_proj_w"].T,
        "dtb": cols(a["L0_attn_dt_proj_b"]), "A_log": a["L0_attn_A_log"], "Dp": cols(a["L0_attn_D_param"]),
        "gateT": a["L0_ffn_gate_w"].T,
        "wgu": np.concatenate([a["L0_ffn_w_gate"].transpose(0, 2, 1), a["L0_ffn_w_up"].transpose(0, 2, 1)], axis=2),
        "wdT": a["L0_ffn_w_down"].transpose(0, 2, 1),
    }


def kernel(**inputs):
    import concourse.bacc as bacc
    from concourse.bass_utils import run_bass_kernel_spmd

    nc = bacc.Bacc("TRN2", target_bir_lowering=False, num_devices=1)
    arrays, ins = {}, {}
    for name, a in laid_out(inputs).items():
        a = np.ascontiguousarray(a)
        arrays[name] = a
        ins[name] = nc.dram_tensor(name, a.shape, mybir.dt.from_np(a.dtype), kind="ExternalInput").ap()
    out = nc.dram_tensor("out", (TOK, D), F32, kind="ExternalOutput").ap()
    perceiver(nc, ins, out)
    r = run_bass_kernel_spmd(nc, [arrays], core_ids=[0])
    return r.results[0]["out"].reshape(B, N, D)
```
